# Optimizing a Trainium2 kernel written in Bass

```python
import numpy as np
import jax
import jax.numpy as jnp

def _softmax(x, axis=-1):
    return jax.nn.softmax(x, axis=axis)

def _gelu(x):
    return jax.nn.gelu(x, approximate=True)

def _silu(x):
    return jax.nn.silu(x)

def _sigmoid(x):
    return jax.nn.sigmoid(x)

def _layernorm(x, axis=-1, eps=1e-05):
    m = jnp.mean(x, axis=axis, keepdims=True)
    v = jnp.var(x, axis=axis, keepdims=True)
    return (x - m) / jnp.sqrt(v + eps)

def _scatter_add(tgt, idx, src, axis=0):
    return tgt.at[idx].add(src)

def _segment_sum(src, seg, n):
    return jax.ops.segment_sum(src, seg, n)
kernel_name = 'mk_audio_tower_d4_tok_audfeat256_r4_a224a6'

def setup_inputs(seed: int=0):
    np.random.seed(seed)
    _w = jnp.asarray

    def _rec_inputs():
        import jax
        import jax.numpy as jnp
        _rk = jax.random.key(seed)
        x = 7.22013e-05 + 1.00017 * jax.random.normal(jax.random.fold_in(_rk, 1), (4, 750, 64), jnp.float32)
        return x
    x = _rec_inputs()

    def _L0_tok_setup():
        import jax, jax.numpy as jnp
        import numpy as np
        K = 8

        def exp_dilation(n, base=2):
            return [base ** i for i in range(n)]

        def _tap_offsets(k):
            dil = np.asarray(exp_dilation(k - 1), dtype=np.int64)
            return np.concatenate([np.zeros(1, np.int64), np.cumsum(dil)])
        B, L, D, O = (8, 1024, 64, 64)
        key = jax.random.key(seed)
        k1, k2, k3 = jax.random.split(key, 3)
        x = jax.random.normal(k1, (B, L, D), jnp.float32)
        weight = jax.random.normal(k2, (K * D, O), jnp.float32) * 0.02
        bias = jax.random.normal(k3, (1, O), jnp.float32) * 0.02
        return {'x': x, 'weight': weight, 'bias': bias}
    _L0_tok_all = _L0_tok_setup()
    _L0_tok_in = {k: v for k, v in _L0_tok_all.items() if k in ('weight', 'bias')}
    del _L0_tok_all

    def _L0_attn_setup():
        import jax, jax.numpy as jnp
        import numpy as np
        DIM = 64
        D_INNER = 128
        D_STATE = 16
        DT_RANK = 16
        BATCH = 4
        SEQ_LEN = 1024
        key = jax.random.key(seed)
        ks = jax.random.split(key, 6)
        x = jax.random.normal(ks[0], (BATCH, SEQ_LEN, DIM), dtype=jnp.float32)
        x_proj = jax.random.normal(ks[1], (DIM, 2 * D_INNER), dtype=jnp.float32) * 0.02
        dt_proj = jax.random.normal(ks[2], (D_INNER, DT_RANK), dtype=jnp.float32) * 0.02
        A_log = jnp.broadcast_to(-jnp.log(jnp.arange(1, D_STATE + 1, dtype=jnp.float32)), (D_INNER, D_STATE))
        B_proj = jax.random.normal(ks[3], (D_INNER, DT_RANK), dtype=jnp.float32) * 0.02
        C_proj = jax.random.normal(ks[4], (D_INNER, DT_RANK), dtype=jnp.float32) * 0.02
        D = jnp.ones((D_INNER,), dtype=jnp.float32)
        out_proj = jax.random.normal(ks[5], (D_INNER, DIM), dtype=jnp.float32) * 0.02
        dt_proj_bias = jnp.ones((DT_RANK,), dtype=jnp.float32)
        return {'x': x, 'x_proj': x_proj, 'dt_proj': dt_proj, 'A_log': A_log, 'B_proj': B_proj, 'C_proj': C_proj, 'D': D, 'out_proj': out_proj, 'dt_proj_bias': dt_proj_bias}
    _L0_attn_all = _L0_attn_setup()
    _L0_attn_in = {k: v for k, v in _L0_attn_all.items() if k in ('x_proj', 'dt_proj', 'A_log', 'B_proj', 'C_proj', 'D', 'out_proj', 'dt_proj_bias')}
    del _L0_attn_all

    def _L0_ffn_setup():
        import jax, jax.numpy as jnp
        import numpy as np
        B, S, H, NH, NE = (4, 256, 64, 4, 4)
        D = H // NH
        EPS = 1e-08

        def layernorm(x, g, b):
            m = jnp.mean(x, axis=-1, keepdims=True)
            v = jnp.mean((x - m) ** 2, axis=-1, keepdims=True)
            return (x - m) / jnp.sqrt(v + EPS) * g + b
        key = jax.random.key(seed)
        ks = jax.random.split(key, 18)
        sc = 0.05
        return {'x': jax.random.normal(ks[0], (B, S, H), jnp.float32), 'hl_w': jax.random.normal(ks[1], (NH, D, H), jnp.float32) * sc, 'hl_b': jax.random.normal(ks[2], (NH, D), jnp.float32) * sc, 'wq': jax.random.normal(ks[3], (NH, NE, D, D), jnp.float32) * sc, 'wk': jax.random.normal(ks[4], (NH, D, D), jnp.float32) * sc, 'wv': jax.random.normal(ks[5], (NH, D, D), jnp.float32) * sc, 'gate_w': jax.random.normal(ks[6], (NH, NE, NE * D), jnp.float32) * sc, 'gate_b': jax.random.normal(ks[7], (NH, NE), jnp.float32) * sc, 'ln_g': jnp.ones((D,), jnp.float32), 'ln_b': jnp.zeros((D,), jnp.float32), 'fc1_w': jax.random.normal(ks[8], (D, D), jnp.float32) * sc, 'fc1_b': jax.random.normal(ks[9], (D,), jnp.float32) * sc, 'fc2_w': jax.random.normal(ks[10], (D, D), jnp.float32) * sc, 'fc2_b': jax.random.normal(ks[11], (D,), jnp.float32) * sc, 'fnorm_g': jnp.ones((D,), jnp.float32), 'fnorm_b': jnp.zeros((D,), jnp.float32), 'fgate_w': jax.random.normal(ks[12], (NH, H), jnp.float32) * sc}
    _L0_ffn_all = _L0_ffn_setup()
    _L0_ffn_in = {k: v for k, v in _L0_ffn_all.items() if k in ('hl_w', 'hl_b', 'wq', 'wk', 'wv', 'gate_w', 'gate_b', 'ln_g', 'ln_b', 'fc1_w', 'fc1_b', 'fc2_w', 'fc2_b', 'fnorm_g', 'fnorm_b', 'fgate_w')}
    del _L0_ffn_all

    def _L1_attn_setup():
        import jax, jax.numpy as jnp
        import numpy as np
        B, N, C = (8, 2048, 64)
        HEADS, DH, KR = (8, 32, 4)
        INNER = HEADS * DH
        FF = 4 * C
        EPS = 1e-05

        def layernorm(x, g, b):
            mu = jnp.mean(x, axis=-1, keepdims=True)
            var = jnp.mean((x - mu) ** 2, axis=-1, keepdims=True)
            return (x - mu) * jax.lax.rsqrt(var + EPS) * g + b
        key = jax.random.key(seed)
        ks = jax.random.split(key, 16)
        s = 0.02
        return {'x': jax.random.normal(ks[0], (B, N, C), jnp.float32), 'ln1_g': jnp.ones((C,), jnp.float32), 'ln1_b': jnp.zeros((C,), jnp.float32), 'Wx': jax.random.normal(ks[1], (C, INNER), jnp.float32) * s, 'bx': jnp.zeros((INNER,), jnp.float32), 'Wq': jax.random.normal(ks[2], (DH, KR), jnp.float32) * s, 'Wk': jax.random.normal(ks[3], (DH, KR), jnp.float32) * s, 'Wv': jax.random.normal(ks[4], (DH, DH), jnp.float32) * s, 'Wo': jax.random.normal(ks[5], (INNER, C), jnp.float32) * s, 'bo': jnp.zeros((C,), jnp.float32), 'ln2_g': jnp.ones((C,), jnp.float32), 'ln2_b': jnp.zeros((C,), jnp.float32), 'W1': jax.random.normal(ks[6], (C, FF), jnp.float32) * s, 'b1': jnp.zeros((FF,), jnp.float32), 'W2': jax.random.normal(ks[7], (FF, C), jnp.float32) * s, 'b2': jnp.zeros((C,), jnp.float32)}
    _L1_attn_all = _L1_attn_setup()
    _L1_attn_in = {k: v for k, v in _L1_attn_all.items() if k in ('ln1_g', 'ln1_b', 'Wx', 'bx', 'Wq', 'Wk', 'Wv', 'Wo', 'bo', 'ln2_g', 'ln2_b', 'W1', 'b1', 'W2', 'b2')}
    del _L1_attn_all

    def _L1_ffn_setup():
        import jax, jax.numpy as jnp
        import numpy as np
        B, T, C = (64, 96, 64)
        NH, NKV = (4, 2)
        HD = C // NH
        NREP = NH // NKV
        NE, TOPK = (8, 2)
        HID = int(8 / 3 * C)
        EPS_RMS = 1e-06

        def _rope_tables(t_len):
            inv_freq = 1.0 / 10000.0 ** (np.arange(0, HD, 2, dtype=np.float32) / HD)
            t = np.arange(t_len, dtype=np.float32)
            freqs = np.outer(t, inv_freq)
            emb = np.concatenate([freqs, freqs], axis=-1)
            return (jnp.asarray(np.cos(emb)), jnp.asarray(np.sin(emb)))

        def _rotate_half(x):
            h = x.shape[-1] // 2
            return jnp.concatenate([-x[..., h:], x[..., :h]], axis=-1)

        def _rmsnorm(v, w):
            return v * jax.lax.rsqrt(jnp.mean(v * v, axis=-1, keepdims=True) + EPS_RMS) * w
        key = jax.random.key(seed)
        ks = jax.random.split(key, 10)
        s = lambda k, shape: jax.random.normal(k, shape, jnp.float32) * 0.02
        return {'x': jax.random.normal(ks[0], (B, T, C), jnp.float32), 'ln1_w': jnp.ones((C,), jnp.float32), 'ln2_w': jnp.ones((C,), jnp.float32), 'wq': s(ks[1], (NH * HD, C)), 'wk': s(ks[2], (NKV * HD, C)), 'wv': s(ks[3], (NKV * HD, C)), 'wo': s(ks[4], (C, C)), 'router_w': s(ks[5], (NE, C)), 'w1': s(ks[6], (NE, HID, C)), 'w2': s(ks[7], (NE, C, HID)), 'w3': s(ks[8], (NE, HID, C))}
    _L1_ffn_all = _L1_ffn_setup()
    _L1_ffn_in = {k: v for k, v in _L1_ffn_all.items() if k in ('ln1_w', 'ln2_w', 'wq', 'wk', 'wv', 'wo', 'router_w', 'w1', 'w2', 'w3')}
    del _L1_ffn_all

    def _L2_attn_setup():
        import jax, jax.numpy as jnp
        import numpy as np
        key = jax.random.key(seed)
        k1, k2, k3 = jax.random.split(key, 3)
        d = 64
        x = jax.random.normal(k1, (8, 512, d), dtype=jnp.float32)
        Wq = jax.random.normal(k2, (d, d), dtype=jnp.float32) * d ** (-0.5)
        Wk = jax.random.normal(k3, (d, d), dtype=jnp.float32) * d ** (-0.5)
        return {'x': x, 'Wq': Wq, 'Wk': Wk}
    _L2_attn_all = _L2_attn_setup()
    _L2_attn_in = {k: v for k, v in _L2_attn_all.items() if k in ('Wq', 'Wk')}
    del _L2_attn_all

    def _L2_ffn_setup():
        import jax, jax.numpy as jnp
        import numpy as np
        INPUT_WIDTH = 64
        DEPTH = 7
        OUTPUT_WIDTH = 64
        N_NODES = 2 ** (DEPTH + 1) - 1
        key = jax.random.key(seed)
        k_x, k_w1, k_w2 = jax.random.split(key, 3)
        init1 = 1.0 / np.sqrt(INPUT_WIDTH)
        x = jax.random.normal(k_x, (2, 256, INPUT_WIDTH), dtype=jnp.float32)
        w1s = jax.random.uniform(k_w1, (N_NODES, INPUT_WIDTH), jnp.float32, -init1, init1)
        b1s = jnp.zeros((N_NODES,), jnp.float32)
        w2s = jax.random.uniform(k_w2, (N_NODES, INPUT_WIDTH, OUTPUT_WIDTH), jnp.float32, -init1, init1)
        b2s = jnp.zeros((N_NODES, OUTPUT_WIDTH), jnp.float32)
        return {'x': x, 'w1s': w1s, 'b1s': b1s, 'w2s': w2s, 'b2s': b2s}
    _L2_ffn_all = _L2_ffn_setup()
    _L2_ffn_in = {k: v for k, v in _L2_ffn_all.items() if k in ('w1s', 'b1s', 'w2s', 'b2s')}
    del _L2_ffn_all

    def _L3_attn_setup():
        import jax, jax.numpy as jnp
        import numpy as np
        B_, L_, DM = (8, 256, 64)
        DS, DC, EX = (16, 4, 2)
        DI = EX * DM
        DTR = max(1, DM // 16)

        def _dw_conv(x, w, b):
            xc = jnp.transpose(x, (0, 2, 1))
            out = jax.lax.conv_general_dilated(xc, w[:, None, :], window_strides=(1,), padding=[(DC - 1, 0)], dimension_numbers=('NCH', 'OIH', 'NCH'), feature_group_count=DI)
            return jnp.transpose(out + b[:, None], (0, 2, 1))

        def _ssm(x, xW, dtW, dtB, ALog, Dp):
            A = -jnp.exp(ALog)
            xdbl = x @ xW
            dlt, Bp, Cp = jnp.split(xdbl, [DTR, DTR + DS], axis=-1)
            delta = jax.nn.softplus(dlt @ dtW + dtB)
            dA = jnp.exp(delta[..., None] * A)
            dBx = (delta * x)[..., None] * Bp[:, :, None, :]

            def step(h, t):
                a, bb, c = t
                h = a * h + bb
                y = jnp.einsum('bdn,bn->bd', h, c)
                return (h, y)
            h0 = jnp.zeros((x.shape[0], DI, DS), x.dtype)
            _, ys = jax.lax.scan(step, h0, (jnp.moveaxis(dA, 1, 0), jnp.moveaxis(dBx, 1, 0), jnp.moveaxis(Cp, 1, 0)))
            return jnp.moveaxis(ys, 0, 1) + Dp * x

        def _mamba(x, inW, convW, convB, xW, dtW, dtB, ALog, Dp, outW):
            xr = x @ inW
            xs, res = jnp.split(xr, 2, axis=-1)
            xs = jax.nn.silu(_dw_conv(xs, convW, convB))
            y = _ssm(xs, xW, dtW, dtB, ALog, Dp)
            return y * jax.nn.silu(res) @ outW
        key = jax.random.key(seed)
        ks = iter(jax.random.split(key, 40))

        def n(shape, s=0.02):
            return jax.random.normal(next(ks), shape, jnp.float32) * s
        inp = {'x': jax.random.normal(next(ks), (B_, L_, DM), jnp.float32)}
        inp['norm_g'] = jnp.ones((DM,), jnp.float32)
        inp['norm_b'] = jnp.zeros((DM,), jnp.float32)
        for m in ('f', 'b'):
            inp[f'inW_{m}'] = n((DM, 2 * DI))
            inp[f'convW_{m}'] = n((DI, DC))
            inp[f'convB_{m}'] = jnp.zeros((DI,), jnp.float32)
            inp[f'xW_{m}'] = n((DI, DTR + 2 * DS))
            inp[f'dtW_{m}'] = n((DTR, DI))
            inp[f'dtB_{m}'] = jnp.zeros((DI,), jnp.float32)
            inp[f'ALog_{m}'] = jnp.log(jnp.tile(jnp.arange(1, DS + 1, dtype=jnp.float32), (DI, 1)))
            inp[f'Dp_{m}'] = jnp.ones((DI,), jnp.float32)
            inp[f'outW_{m}'] = n((DI, DM))
        inp['fusW'] = n((2 * DM, DM))
        inp['fusB'] = jnp.zeros((DM,), jnp.float32)
        return inp
    _L3_attn_all = _L3_attn_setup()
    _L3_attn_in = {k: v for k, v in _L3_attn_all.items() if k in ('norm_g', 'norm_b', 'inW_f', 'convW_f', 'convB_f', 'xW_f', 'dtW_f', 'dtB_f', 'ALog_f', 'Dp_f', 'outW_f', 'inW_b', 'convW_b', 'convB_b', 'xW_b', 'dtW_b', 'dtB_b', 'ALog_b', 'Dp_b', 'outW_b', 'fusW', 'fusB')}
    del _L3_attn_all

    def _L3_ffn_setup():
        import jax, jax.numpy as jnp
        import numpy as np
        E = 8
        K = 2
        D = 64
        H = 128
        DOUT = 64
        EPS = 1e-05
        key = jax.random.key(seed)
        ks = jax.random.split(key, 9)
        s = 0.02
        return {'x': jax.random.normal(ks[0], (4, 2048, D), jnp.float32), 'gamma': 1.0 + 0.05 * jax.random.normal(ks[1], (D,), jnp.float32), 'beta': 0.05 * jax.random.normal(ks[2], (D,), jnp.float32), 'Wr': 0.01 * jax.random.normal(ks[3], (D, E), jnp.float32), 'br': jnp.zeros((E,), jnp.float32), 'W1': s * jax.random.normal(ks[4], (E, D, H), jnp.float32), 'b1': s * jax.random.normal(ks[5], (E, H), jnp.float32), 'W2': s * jax.random.normal(ks[6], (E, H, DOUT), jnp.float32), 'b2': s * jax.random.normal(ks[7], (E, DOUT), jnp.float32)}
    _L3_ffn_all = _L3_ffn_setup()
    _L3_ffn_in = {k: v for k, v in _L3_ffn_all.items() if k in ('gamma', 'beta', 'Wr', 'br', 'W1', 'b1', 'W2', 'b2')}
    del _L3_ffn_all
    return {'x': x, 'L0_tok_weight': _L0_tok_in['weight'], 'L0_tok_bias': _L0_tok_in['bias'], 'L0_attn_x_proj': _L0_attn_in['x_proj'], 'L0_attn_dt_proj': _L0_attn_in['dt_proj'], 'L0_attn_A_log': _L0_attn_in['A_log'], 'L0_attn_B_proj': _L0_attn_in['B_proj'], 'L0_attn_C_proj': _L0_attn_in['C_proj'], 'L0_attn_D': _L0_attn_in['D'], 'L0_attn_out_proj': _L0_attn_in['out_proj'], 'L0_attn_dt_proj_bias': _L0_attn_in['dt_proj_bias'], 'L0_ffn_hl_w': _L0_ffn_in['hl_w'], 'L0_ffn_hl_b': _L0_ffn_in['hl_b'], 'L0_ffn_wq': _L0_ffn_in['wq'], 'L0_ffn_wk': _L0_ffn_in['wk'], 'L0_ffn_wv': _L0_ffn_in['wv'], 'L0_ffn_gate_w': _L0_ffn_in['gate_w'], 'L0_ffn_gate_b': _L0_ffn_in['gate_b'], 'L0_ffn_ln_g': _L0_ffn_in['ln_g'], 'L0_ffn_ln_b': _L0_ffn_in['ln_b'], 'L0_ffn_fc1_w': _L0_ffn_in['fc1_w'], 'L0_ffn_fc1_b': _L0_ffn_in['fc1_b'], 'L0_ffn_fc2_w': _L0_ffn_in['fc2_w'], 'L0_ffn_fc2_b': _L0_ffn_in['fc2_b'], 'L0_ffn_fnorm_g': _L0_ffn_in['fnorm_g'], 'L0_ffn_fnorm_b': _L0_ffn_in['fnorm_b'], 'L0_ffn_fgate_w': _L0_ffn_in['fgate_w'], 'L1_attn_ln1_g': _L1_attn_in['ln1_g'], 'L1_attn_ln1_b': _L1_attn_in['ln1_b'], 'L1_attn_Wx': _L1_attn_in['Wx'], 'L1_attn_bx': _L1_attn_in['bx'], 'L1_attn_Wq': _L1_attn_in['Wq'], 'L1_attn_Wk': _L1_attn_in['Wk'], 'L1_attn_Wv': _L1_attn_in['Wv'], 'L1_attn_Wo': _L1_attn_in['Wo'], 'L1_attn_bo': _L1_attn_in['bo'], 'L1_attn_ln2_g': _L1_attn_in['ln2_g'], 'L1_attn_ln2_b': _L1_attn_in['ln2_b'], 'L1_attn_W1': _L1_attn_in['W1'], 'L1_attn_b1': _L1_attn_in['b1'], 'L1_attn_W2': _L1_attn_in['W2'], 'L1_attn_b2': _L1_attn_in['b2'], 'L1_ffn_ln1_w': _L1_ffn_in['ln1_w'], 'L1_ffn_ln2_w': _L1_ffn_in['ln2_w'], 'L1_ffn_wq': _L1_ffn_in['wq'], 'L1_ffn_wk': _L1_ffn_in['wk'], 'L1_ffn_wv': _L1_ffn_in['wv'], 'L1_ffn_wo': _L1_ffn_in['wo'], 'L1_ffn_router_w': _L1_ffn_in['router_w'], 'L1_ffn_w1': _L1_ffn_in['w1'], 'L1_ffn_w2': _L1_ffn_in['w2'], 'L1_ffn_w3': _L1_ffn_in['w3'], 'L2_attn_Wq': _L2_attn_in['Wq'], 'L2_attn_Wk': _L2_attn_in['Wk'], 'L2_ffn_w1s': _L2_ffn_in['w1s'], 'L2_ffn_b1s': _L2_ffn_in['b1s'], 'L2_ffn_w2s': _L2_ffn_in['w2s'], 'L2_ffn_b2s': _L2_ffn_in['b2s'], 'L3_attn_norm_g': _L3_attn_in['norm_g'], 'L3_attn_norm_b': _L3_attn_in['norm_b'], 'L3_attn_inW_f': _L3_attn_in['inW_f'], 'L3_attn_convW_f': _L3_attn_in['convW_f'], 'L3_attn_convB_f': _L3_attn_in['convB_f'], 'L3_attn_xW_f': _L3_attn_in['xW_f'], 'L3_attn_dtW_f': _L3_attn_in['dtW_f'], 'L3_attn_dtB_f': _L3_attn_in['dtB_f'], 'L3_attn_ALog_f': _L3_attn_in['ALog_f'], 'L3_attn_Dp_f': _L3_attn_in['Dp_f'], 'L3_attn_outW_f': _L3_attn_in['outW_f'], 'L3_attn_inW_b': _L3_attn_in['inW_b'], 'L3_attn_convW_b': _L3_attn_in['convW_b'], 'L3_attn_convB_b': _L3_attn_in['convB_b'], 'L3_attn_xW_b': _L3_attn_in['xW_b'], 'L3_attn_dtW_b': _L3_attn_in['dtW_b'], 'L3_attn_dtB_b': _L3_attn_in['dtB_b'], 'L3_attn_ALog_b': _L3_attn_in['ALog_b'], 'L3_attn_Dp_b': _L3_attn_in['Dp_b'], 'L3_attn_outW_b': _L3_attn_in['outW_b'], 'L3_attn_fusW': _L3_attn_in['fusW'], 'L3_attn_fusB': _L3_attn_in['fusB'], 'L3_ffn_gamma': _L3_ffn_in['gamma'], 'L3_ffn_beta': _L3_ffn_in['beta'], 'L3_ffn_Wr': _L3_ffn_in['Wr'], 'L3_ffn_br': _L3_ffn_in['br'], 'L3_ffn_W1': _L3_ffn_in['W1'], 'L3_ffn_b1': _L3_ffn_in['b1'], 'L3_ffn_W2': _L3_ffn_in['W2'], 'L3_ffn_b2': _L3_ffn_in['b2']}

def reference(x, L0_tok_weight, L0_tok_bias, L0_attn_x_proj, L0_attn_dt_proj, L0_attn_A_log, L0_attn_B_proj, L0_attn_C_proj, L0_attn_D, L0_attn_out_proj, L0_attn_dt_proj_bias, L0_ffn_hl_w, L0_ffn_hl_b, L0_ffn_wq, L0_ffn_wk, L0_ffn_wv, L0_ffn_gate_w, L0_ffn_gate_b, L0_ffn_ln_g, L0_ffn_ln_b, L0_ffn_fc1_w, L0_ffn_fc1_b, L0_ffn_fc2_w, L0_ffn_fc2_b, L0_ffn_fnorm_g, L0_ffn_fnorm_b, L0_ffn_fgate_w, L1_attn_ln1_g, L1_attn_ln1_b, L1_attn_Wx, L1_attn_bx, L1_attn_Wq, L1_attn_Wk, L1_attn_Wv, L1_attn_Wo, L1_attn_bo, L1_attn_ln2_g, L1_attn_ln2_b, L1_attn_W1, L1_attn_b1, L1_attn_W2, L1_attn_b2, L1_ffn_ln1_w, L1_ffn_ln2_w, L1_ffn_wq, L1_ffn_wk, L1_ffn_wv, L1_ffn_wo, L1_ffn_router_w, L1_ffn_w1, L1_ffn_w2, L1_ffn_w3, L2_attn_Wq, L2_attn_Wk, L2_ffn_w1s, L2_ffn_b1s, L2_ffn_w2s, L2_ffn_b2s, L3_attn_norm_g, L3_attn_norm_b, L3_attn_inW_f, L3_attn_convW_f, L3_attn_convB_f, L3_attn_xW_f, L3_attn_dtW_f, L3_attn_dtB_f, L3_attn_ALog_f, L3_attn_Dp_f, L3_attn_outW_f, L3_attn_inW_b, L3_attn_convW_b, L3_attn_convB_b, L3_attn_xW_b, L3_attn_dtW_b, L3_attn_dtB_b, L3_attn_ALog_b, L3_attn_Dp_b, L3_attn_outW_b, L3_attn_fusW, L3_attn_fusB, L3_ffn_gamma, L3_ffn_beta, L3_ffn_Wr, L3_ffn_br, L3_ffn_W1, L3_ffn_b1, L3_ffn_W2, L3_ffn_b2):
    import jax
    import jax.numpy as jnp

    def _L0_tok_ref(x, weight, bias):
        import jax, jax.numpy as jnp
        import numpy as np
        K = 8

        def exp_dilation(n, base=2):
            return [base ** i for i in range(n)]

        def _tap_offsets(k):
            dil = np.asarray(exp_dilation(k - 1), dtype=np.int64)
            return np.concatenate([np.zeros(1, np.int64), np.cumsum(dil)])
        b, l, d = x.shape
        k = K
        offs = _tap_offsets(k)
        g = l - k + 1
        pos = offs[:, None] + np.arange(g)[None, :]
        valid = jnp.asarray(pos < l, x.dtype)
        pos_c = np.minimum(pos, l - 1)
        patches = x[:, pos_c, :] * valid[None, :, :, None]
        Wk = weight.reshape(k, d, -1)
        out = jnp.einsum('bkgd,kdo->bgo', patches, Wk) + bias[0]
        return out

    def _L0_attn_ref(x, x_proj, dt_proj, A_log, B_proj, C_proj, D, out_proj, dt_proj_bias):
        import jax, jax.numpy as jnp
        import numpy as np
        DIM = 64
        D_INNER = 128
        D_STATE = 16
        DT_RANK = 16
        BATCH = 4
        SEQ_LEN = 1024
        x_z = x @ x_proj
        xp, z = jnp.split(x_z, 2, axis=-1)
        u = jax.nn.silu(xp)
        dt = jax.nn.softplus(u @ dt_proj + dt_proj_bias)
        Bm = u @ B_proj
        Cm = u @ C_proj
        A = -jnp.exp(A_log)

        def step(h, inp):
            dt_t, B_t, C_t, u_t = inp
            dA = jnp.exp(dt_t[:, None, :] * A[None])
            dBu = (dt_t * B_t)[:, None, :] * u_t[:, :, None]
            h = dA * h + dBu
            y = jnp.einsum('bds,bs->bd', h, C_t)
            return (h, y)
        h0 = jnp.zeros((x.shape[0], D_INNER, D_STATE), dtype=x.dtype)
        xs = (jnp.swapaxes(dt, 0, 1), jnp.swapaxes(Bm, 0, 1), jnp.swapaxes(Cm, 0, 1), jnp.swapaxes(u, 0, 1))
        _, ys = jax.lax.scan(step, h0, xs)
        y = jnp.swapaxes(ys, 0, 1)
        y = y + u * D
        y = y * jax.nn.silu(z)
        return y @ out_proj

    def _L0_ffn_ref(x, hl_w, hl_b, wq, wk, wv, gate_w, gate_b, ln_g, ln_b, fc1_w, fc1_b, fc2_w, fc2_b, fnorm_g, fnorm_b, fgate_w):
        import jax, jax.numpy as jnp
        import numpy as np
        B, S, H, NH, NE = (4, 256, 64, 4, 4)
        D = H // NH
        EPS = 1e-08

        def layernorm(x, g, b):
            m = jnp.mean(x, axis=-1, keepdims=True)
            v = jnp.mean((x - m) ** 2, axis=-1, keepdims=True)
            return (x - m) / jnp.sqrt(v + EPS) * g + b
        b, s, h = x.shape
        nh, d, _ = wk.shape
        ne = wq.shape[1]
        sx = jnp.einsum('bsh,ndh->bnsd', x, hl_w) + hl_b[None, :, None, :]
        pad = sx == 0
        q = jnp.einsum('bnsd,neod->bneso', sx, wq)
        k = jnp.einsum('bnsd,nod->bnso', sx, wk)
        v = jnp.einsum('bnsd,nod->bnso', sx, wv)
        causal = jnp.where(jnp.tril(jnp.ones((s, s), bool)), 0.0, -jnp.inf).astype(x.dtype)
        scores = jnp.einsum('bnesd,bntd->bnest', q, k) * d ** 0.5 + causal
        att = jax.nn.softmax(scores, axis=-1)
        qkv = jnp.einsum('bnest,bntd->bnesd', att, v)
        qkv = jnp.where(pad[:, :, None], 0.0, qkv)
        out = jnp.transpose(qkv, (0, 1, 3, 2, 4)).reshape(b, nh, s, ne * d)
        gs = jax.nn.softmax(jnp.einsum('bnsf,nef->bnse', out, gate_w) + gate_b[None, :, None, :], axis=-1)
        mixed = jnp.einsum('bnsed,bnse->bnsd', out.reshape(b, nh, s, ne, d), gs)
        resid = sx[jnp.arange(nh), jnp.arange(nh)]
        hn = layernorm(mixed + resid, ln_g, ln_b)
        f_n = jnp.transpose(hn, (0, 2, 1, 3)).reshape(b, s, h)
        fx = f_n.reshape(b, s, nh, d)
        pm = fx == 0
        hx = jnp.where(pm, 0.0, fx @ fc1_w.T + fc1_b)
        hx = jax.nn.relu(hx)
        hx = jnp.where(pm, 0.0, hx @ fc2_w.T + fc2_b)
        hx = layernorm(hx + fx, fnorm_g, fnorm_b)
        fout = hx.reshape(b, s, h)
        fg = jax.nn.softmax(fout @ fgate_w.T, axis=-1)
        return (fout.reshape(b, s, nh, d) * fg[..., None]).reshape(b, s, h)

    def _L1_attn_ref(x, ln1_g, ln1_b, Wx, bx, Wq, Wk, Wv, Wo, bo, ln2_g, ln2_b, W1, b1, W2, b2):
        import jax, jax.numpy as jnp
        import numpy as np
        B, N, C = (8, 2048, 64)
        HEADS, DH, KR = (8, 32, 4)
        INNER = HEADS * DH
        FF = 4 * C
        EPS = 1e-05

        def layernorm(x, g, b):
            mu = jnp.mean(x, axis=-1, keepdims=True)
            var = jnp.mean((x - mu) ** 2, axis=-1, keepdims=True)
            return (x - mu) * jax.lax.rsqrt(var + EPS) * g + b
        b, n, c = x.shape
        h = layernorm(x, ln1_g, ln1_b)
        xm = h @ Wx + bx
        xm = xm.reshape(b, n, HEADS, DH).transpose(0, 2, 1, 3)
        q = jax.nn.softmax(xm @ Wq, axis=-1)
        k = jax.nn.softmax(xm @ Wk, axis=-2)
        v = xm @ Wv
        kv = jnp.einsum('bhnr,bhnd->bhrd', k, v)
        qkv = jnp.einsum('bhnr,bhrd->bhnd', q, kv)
        attn = qkv.transpose(0, 2, 1, 3).reshape(b, n, INNER) @ Wo + bo
        fx = attn + x
        h2 = layernorm(fx, ln2_g, ln2_b)
        m = jax.nn.gelu(h2 @ W1 + b1, approximate=False) @ W2 + b2
        return m + fx

    def _L1_ffn_ref(x, ln1_w, ln2_w, wq, wk, wv, wo, router_w, w1, w2, w3):
        import jax, jax.numpy as jnp
        import numpy as np
        B, T, C = (64, 96, 64)
        NH, NKV = (4, 2)
        HD = C // NH
        NREP = NH // NKV
        NE, TOPK = (8, 2)
        HID = int(8 / 3 * C)
        EPS_RMS = 1e-06

        def _rope_tables(t_len):
            inv_freq = 1.0 / 10000.0 ** (np.arange(0, HD, 2, dtype=np.float32) / HD)
            t = np.arange(t_len, dtype=np.float32)
            freqs = np.outer(t, inv_freq)
            emb = np.concatenate([freqs, freqs], axis=-1)
            return (jnp.asarray(np.cos(emb)), jnp.asarray(np.sin(emb)))

        def _rotate_half(x):
            h = x.shape[-1] // 2
            return jnp.concatenate([-x[..., h:], x[..., :h]], axis=-1)

        def _rmsnorm(v, w):
            return v * jax.lax.rsqrt(jnp.mean(v * v, axis=-1, keepdims=True) + EPS_RMS) * w
        Bx, Tx, Cx = x.shape
        h = _rmsnorm(x, ln1_w)
        q = (h @ wq.T).reshape(Bx, Tx, NH, HD).transpose(0, 2, 1, 3)
        k = (h @ wk.T).reshape(Bx, Tx, NKV, HD).transpose(0, 2, 1, 3)
        v = (h @ wv.T).reshape(Bx, Tx, NKV, HD).transpose(0, 2, 1, 3)
        cos, sin = _rope_tables(Tx)
        cos, sin = (cos[None, None], sin[None, None])
        q = q * cos + _rotate_half(q) * sin
        k = k * cos + _rotate_half(k) * sin
        k = jnp.repeat(k, NREP, axis=1)
        v = jnp.repeat(v, NREP, axis=1)
        scores = jnp.einsum('bhtd,bhsd->bhts', q, k) / jnp.sqrt(jnp.float32(HD))
        causal = jnp.tril(jnp.ones((Tx, Tx), dtype=bool))
        scores = jnp.where(causal[None, None], scores, jnp.float32(-1e+30))
        att = jax.nn.softmax(scores, axis=-1)
        y = jnp.einsum('bhts,bhsd->bhtd', att, v).transpose(0, 2, 1, 3).reshape(Bx, Tx, Cx)
        x = x + y @ wo.T
        flat = _rmsnorm(x, ln2_w).reshape(-1, Cx)
        probs = jax.nn.softmax(flat @ router_w.T, axis=-1)
        tp, ti = jax.lax.top_k(probs, TOPK)
        tp = tp / (jnp.sum(tp, axis=-1, keepdims=True) + 1e-09)
        weights = jnp.sum(tp[..., None] * jax.nn.one_hot(ti, NE, dtype=flat.dtype), axis=1)
        out = jnp.zeros_like(flat)
        for e in range(NE):
            hh = jax.nn.silu(flat @ w1[e].T) * (flat @ w3[e].T)
            out = out + weights[:, e:e + 1] * (hh @ w2[e].T)
        return x + out.reshape(Bx, Tx, Cx)

    def _L2_attn_ref(x, Wq, Wk):
        import jax, jax.numpy as jnp
        import numpy as np
        d = x.shape[-1]
        scale = d ** (-0.5)
        q = jnp.einsum('bnd,ed->bne', x, Wq)
        k = jnp.einsum('bnd,ed->bne', x, Wk)
        sim = jnp.einsum('bid,bjd->bij', q, k) * scale
        attn = jax.nn.softmax(sim, axis=-1)
        out = jnp.einsum('bij,bjd->bid', attn, x)
        return out

    def _L2_ffn_ref(x, w1s, b1s, w2s, b2s):
        import jax, jax.numpy as jnp
        import numpy as np
        INPUT_WIDTH = 64
        DEPTH = 7
        OUTPUT_WIDTH = 64
        N_NODES = 2 ** (DEPTH + 1) - 1
        B, S, D = x.shape
        flat_x = x.reshape(B * S, D)
        T = flat_x.shape[0]
        current = jnp.zeros((T,), dtype=jnp.int32)
        all_nodes = []
        all_logits = []
        for _ in range(DEPTH + 1):
            all_nodes.append(current)
            score = jnp.einsum('td,td->t', flat_x, w1s[current]) + b1s[current]
            all_logits.append(score)
            choice = ((jnp.sign(score) + 1.0) / 2.0).astype(jnp.int32)
            current = current * 2 + choice + 1
        logits = jnp.stack(all_logits, axis=1)
        path_weights = jax.nn.gelu(jnp.abs(logits), approximate=False)
        out = jnp.zeros((T, OUTPUT_WIDTH), dtype=x.dtype)
        for i in range(DEPTH + 1):
            nodes_i = all_nodes[i]
            t_i = jnp.einsum('td,tdo->to', flat_x, w2s[nodes_i]) + b2s[nodes_i]
            out = out + t_i * path_weights[:, i][:, None]
        return out.reshape(B, S, OUTPUT_WIDTH)

    def _L3_attn_ref(x, norm_g, norm_b, inW_f, convW_f, convB_f, xW_f, dtW_f, dtB_f, ALog_f, Dp_f, outW_f, inW_b, convW_b, convB_b, xW_b, dtW_b, dtB_b, ALog_b, Dp_b, outW_b, fusW, fusB):
        import jax, jax.numpy as jnp
        import numpy as np
        B_, L_, DM = (8, 256, 64)
        DS, DC, EX = (16, 4, 2)
        DI = EX * DM
        DTR = max(1, DM // 16)

        def _dw_conv(x, w, b):
            xc = jnp.transpose(x, (0, 2, 1))
            out = jax.lax.conv_general_dilated(xc, w[:, None, :], window_strides=(1,), padding=[(DC - 1, 0)], dimension_numbers=('NCH', 'OIH', 'NCH'), feature_group_count=DI)
            return jnp.transpose(out + b[:, None], (0, 2, 1))

        def _ssm(x, xW, dtW, dtB, ALog, Dp):
            A = -jnp.exp(ALog)
            xdbl = x @ xW
            dlt, Bp, Cp = jnp.split(xdbl, [DTR, DTR + DS], axis=-1)
            delta = jax.nn.softplus(dlt @ dtW + dtB)
            dA = jnp.exp(delta[..., None] * A)
            dBx = (delta * x)[..., None] * Bp[:, :, None, :]

            def step(h, t):
                a, bb, c = t
                h = a * h + bb
                y = jnp.einsum('bdn,bn->bd', h, c)
                return (h, y)
            h0 = jnp.zeros((x.shape[0], DI, DS), x.dtype)
            _, ys = jax.lax.scan(step, h0, (jnp.moveaxis(dA, 1, 0), jnp.moveaxis(dBx, 1, 0), jnp.moveaxis(Cp, 1, 0)))
            return jnp.moveaxis(ys, 0, 1) + Dp * x

        def _mamba(x, inW, convW, convB, xW, dtW, dtB, ALog, Dp, outW):
            xr = x @ inW
            xs, res = jnp.split(xr, 2, axis=-1)
            xs = jax.nn.silu(_dw_conv(xs, convW, convB))
            y = _ssm(xs, xW, dtW, dtB, ALog, Dp)
            return y * jax.nn.silu(res) @ outW
        mu = x.mean(-1, keepdims=True)
        var = ((x - mu) ** 2).mean(-1, keepdims=True)
        xn = (x - mu) * jax.lax.rsqrt(var + 1e-05) * norm_g + norm_b
        xf = _mamba(xn, inW_f, convW_f, convB_f, xW_f, dtW_f, dtB_f, ALog_f, Dp_f, outW_f)
        xb = _mamba(jnp.flip(xn, 1), inW_b, convW_b, convB_b, xW_b, dtW_b, dtB_b, ALog_b, Dp_b, outW_b)
        xb = jnp.flip(xb, 1)
        fused = jnp.concatenate([xf, xb], axis=-1) @ fusW + fusB
        return x + fused

    def _L3_ffn_ref(x, gamma, beta, Wr, br, W1, b1, W2, b2):
        import jax, jax.numpy as jnp
        import numpy as np
        E = 8
        K = 2
        D = 64
        H = 128
        DOUT = 64
        EPS = 1e-05
        mu = jnp.mean(x, axis=-1, keepdims=True)
        var = jnp.mean(jnp.square(x - mu), axis=-1, keepdims=True)
        xn = (x - mu) * jax.lax.rsqrt(var + EPS) * gamma + beta
        logits = jnp.einsum('bsd,de->bse', xn, Wr) + br
        top_vals, top_idx = jax.lax.top_k(logits, K)
        w = jax.nn.softmax(top_vals, axis=-1)
        w_full = jnp.einsum('bsk,bske->bse', w, jax.nn.one_hot(top_idx, E, dtype=w.dtype))
        y = jnp.zeros(x.shape[:-1] + (DOUT,), x.dtype)
        for e in range(E):
            h = jax.nn.gelu(jnp.einsum('bsd,dh->bsh', xn, W1[e]) + b1[e], approximate=False)
            y_e = jnp.einsum('bsh,hd->bsd', h, W2[e]) + b2[e]
            y = y + y_e * w_full[..., e, None]
        return y
    h = _L0_tok_ref(x, L0_tok_weight, L0_tok_bias)
    h = h + _L0_attn_ref(_layernorm(h, axis=-1), L0_attn_x_proj, L0_attn_dt_proj, L0_attn_A_log, L0_attn_B_proj, L0_attn_C_proj, L0_attn_D, L0_attn_out_proj, L0_attn_dt_proj_bias)
    h = h + _L0_ffn_ref(_layernorm(h, axis=-1), L0_ffn_hl_w, L0_ffn_hl_b, L0_ffn_wq, L0_ffn_wk, L0_ffn_wv, L0_ffn_gate_w, L0_ffn_gate_b, L0_ffn_ln_g, L0_ffn_ln_b, L0_ffn_fc1_w, L0_ffn_fc1_b, L0_ffn_fc2_w, L0_ffn_fc2_b, L0_ffn_fnorm_g, L0_ffn_fnorm_b, L0_ffn_fgate_w)
    h = h + _L1_attn_ref(_layernorm(h, axis=-1), L1_attn_ln1_g, L1_attn_ln1_b, L1_attn_Wx, L1_attn_bx, L1_attn_Wq, L1_attn_Wk, L1_attn_Wv, L1_attn_Wo, L1_attn_bo, L1_attn_ln2_g, L1_attn_ln2_b, L1_attn_W1, L1_attn_b1, L1_attn_W2, L1_attn_b2)
    h = h + _L1_ffn_ref(_layernorm(h, axis=-1), L1_ffn_ln1_w, L1_ffn_ln2_w, L1_ffn_wq, L1_ffn_wk, L1_ffn_wv, L1_ffn_wo, L1_ffn_router_w, L1_ffn_w1, L1_ffn_w2, L1_ffn_w3)
    h = h + _L2_attn_ref(_layernorm(h, axis=-1), L2_attn_Wq, L2_attn_Wk)
    h = h + _L2_ffn_ref(_layernorm(h, axis=-1), L2_ffn_w1s, L2_ffn_b1s, L2_ffn_w2s, L2_ffn_b2s)
    h = h + _L3_attn_ref(_layernorm(h, axis=-1), L3_attn_norm_g, L3_attn_norm_b, L3_attn_inW_f, L3_attn_convW_f, L3_attn_convB_f, L3_attn_xW_f, L3_attn_dtW_f, L3_attn_dtB_f, L3_attn_ALog_f, L3_attn_Dp_f, L3_attn_outW_f, L3_attn_inW_b, L3_attn_convW_b, L3_attn_convB_b, L3_attn_xW_b, L3_attn_dtW_b, L3_attn_dtB_b, L3_attn_ALog_b, L3_attn_Dp_b, L3_attn_outW_b, L3_attn_fusW, L3_attn_fusB)
    h = h + _L3_ffn_ref(_layernorm(h, axis=-1), L3_ffn_gamma, L3_ffn_beta, L3_ffn_Wr, L3_ffn_br, L3_ffn_W1, L3_ffn_b1, L3_ffn_W2, L3_ffn_b2)
    return h

_drawn_inputs = setup_inputs


def setup_inputs(seed=0):
    import zlib

    import numpy as np

    out = dict(_drawn_inputs(seed))
    spreads = {'L0_attn_D': (1.0, 0.6),
     'L0_attn_dt_proj_bias': (1.0, 0.6),
     'L0_ffn_ln_g': (1.0, 0.2),
     'L0_ffn_ln_b': (0.0, 0.1),
     'L0_ffn_fnorm_g': (1.0, 0.2),
     'L0_ffn_fnorm_b': (0.0, 0.1),
     'L1_attn_ln1_g': (1.0, 0.6),
     'L1_attn_ln1_b': (0.0, 0.663),
     'L1_attn_bx': (0.0, 0.27),
     'L1_attn_bo': (0.0, 0.1),
     'L1_attn_ln2_g': (1.0, 0.563),
     'L1_attn_ln2_b': (0.0, 0.385),
     'L1_attn_b1': (0.0, 0.1),
     'L1_attn_b2': (0.0, 0.1),
     'L1_ffn_ln1_w': (1.0, 0.6),
     'L1_ffn_ln2_w': (1.0, 0.6),
     'L2_ffn_b1s': (0.0, 0.1),
     'L2_ffn_b2s': (0.0, 0.1),
     'L3_attn_norm_g': (1.0, 0.6),
     'L3_attn_norm_b': (0.0, 0.8),
     'L3_attn_convB_f': (0.0, 0.8),
     'L3_attn_dtB_f': (0.0, 0.8),
     'L3_attn_Dp_f': (1.0, 0.6),
     'L3_attn_convB_b': (0.0, 0.8),
     'L3_attn_dtB_b': (0.0, 0.8),
     'L3_attn_Dp_b': (1.0, 0.6),
     'L3_attn_fusB': (0.0, 0.292),
     'L3_ffn_br': (0.0, 0.8)}
    factors = {'L0_attn_dt_proj': 8.0,
     'L0_attn_A_log': 8.0,
     'L0_attn_B_proj': 8.0,
     'L0_attn_C_proj': 8.0,
     'L0_attn_out_proj': 2.844,
     'L0_ffn_wq': 3.104,
     'L0_ffn_wk': 2.805,
     'L0_ffn_gate_w': 8.0,
     'L0_ffn_gate_b': 6.278,
     'L1_attn_Wx': 5.304,
     'L1_attn_Wq': 8.0,
     'L1_attn_Wk': 8.0,
     'L1_attn_Wo': 2.801,
     'L1_ffn_wq': 8.0,
     'L1_ffn_wk': 8.0,
     'L1_ffn_wo': 3.36,
     'L1_ffn_router_w': 4.153,
     'L1_ffn_w1': 3.583,
     'L1_ffn_w2': 4.071,
     'L1_ffn_w3': 4.69,
     'L3_attn_inW_f': 8.0,
     'L3_attn_convW_f': 8.0,
     'L3_attn_xW_f': 8.0,
     'L3_attn_ALog_f': 8.0,
     'L3_attn_outW_f': 8.0,
     'L3_attn_inW_b': 8.0,
     'L3_attn_convW_b': 8.0,
     'L3_attn_xW_b': 8.0,
     'L3_attn_ALog_b': 8.0,
     'L3_attn_outW_b': 8.0,
     'L3_attn_fusW': 8.0,
     'L3_ffn_gamma': 8.0,
     'L3_ffn_beta': 8.0,
     'L3_ffn_Wr': 8.0,
     'L3_ffn_W1': 8.0,
     'L3_ffn_b1': 42.758,
     'L3_ffn_W2': 8.0,
     'L3_ffn_b2': 57.88,
     'L3_attn_dtW_f': 3.942}
    for name, (base, spread) in spreads.items():
        noise = np.random.default_rng([zlib.crc32(name.encode()), seed]).standard_normal(out[name].shape)
        drawn = base * np.exp(spread * noise) if base else spread * noise
        out[name] = jnp.asarray(drawn.astype(out[name].dtype))
    for name, factor in factors.items():
        out[name] = (out[name] * factor).astype(out[name].dtype)
    return out
```

```python
from contextlib import ExitStack

import numpy as np

import concourse.bass as bass
from concourse import mybir

F32 = mybir.dt.float32
BF16 = mybir.dt.bfloat16
U8 = mybir.dt.uint8
ALU = mybir.AluOpType
ACT = mybir.ActivationFunctionType
AX = mybir.AxisListType

B, LX, D = 4, 750, 64
TAPS = [0, 1, 3, 7, 15, 31, 63, 127]
L = LX - len(TAPS) + 1
P0, TB = 124, 6
LB = P0 * TB
CH, CT = 372, 3
NB = 1
NIT = B // NB
T, W, NC = TB * NB, LB * NB, 2 * NB
TAIL = LX - LB
XW = LB + TAPS[-1] + 1
MASKED = -1e30

NH, HD = 4, 16
E0 = 4
NE, HID = 8, 170
KT1 = -(-NE * HID // 128)
NODES = 255
DS = 16

SPEC = [
    ("ident", 128, 128), ("mask_qk", P0, P0), ("mask_kq", P0, P0),
    ("sel_sum", 128, 4 * 32), ("split1", 96, 1), ("split2", 96, 1),
    ("tok_w", 64, 512), ("tok_b", P0, 64),
    ("a0_xp", 64, 256), ("a0_dt", 128, 128), ("a0_B", 128, 128), ("a0_C", 128, 128),
    ("a0_dtb", 128, 1), ("a0_Alog", 128, 16), ("a0_D", 128, 1), ("a0_out", 128, 64),
    ("f0_hl", 64, 64), ("f0_hlb", 64, 1), ("f0_hlb_bc", P0, 64), ("f0_wq", 64, 4 * 128),
    ("f0_wk", 64, 128), ("f0_wv", 64, 128), ("minus", 128, 3), ("ones_col", P0, 128),
    ("f0_gate", 128, 2 * 16), ("f0_gateb", P0, 16), ("f0_lng", P0, 64), ("f0_lnb", P0, 64),
    ("f0_fc1", 64, 64), ("f0_fc1b", 64, 1), ("f0_fc2", 64, 64), ("f0_fc2b", P0, 64),
    ("f0_fng", P0, 64), ("f0_fnb", P0, 64), ("f0_fg", 64, 4),
    ("a1_g1", 64, 1), ("a1_b1", 64, 1), ("a1_Wx", 64, 256), ("a1_bx", 128, 2), ("a1_bx_bc", P0, 256),
    ("a1_qk", 128, 2 * 64), ("a1_blk", 32, 256), ("a1_Wv", 128, 128), ("a1_Wo", 128, 128),
    ("a1_bo", P0, 64), ("a1_g2", 64, 1), ("a1_b2", 64, 1), ("a1_W1", 64, 256), ("a1_W1b", 128, 2),
    ("a1_W2", 128, 128), ("a1_W2b", P0, 64),
    ("f1_ln1", 64, 1), ("f1_ln2", 64, 1), ("f1_wq", 64, 128), ("f1_wk", 64, 128),
    ("f1_wq_r", 64, 64), ("f1_wk_r", 32, 64), ("rot_q", 64, 128), ("rot_k", 32, 128),
    ("cos", 128, LB), ("sin", 128, LB), ("f1_wv", 64, 128), ("f1_wo", 64, 64),
    ("f1_rt", 64, 8), ("f1_w1", 64, KT1 * 128), ("f1_w3", 64, KT1 * 128), ("f1_w2", 128, KT1 * 64),
    ("rev", P0, 8),
    ("a2_q", 64, 65), ("a2_k", 64, 64),
    ("f2_w1", 64, 256), ("f2_b1", P0, 256), ("f2_b2", 128, 128),
    ("a3_g", 64, 1), ("a3_b", 64, 1), ("a3_fus", 128, 64), ("a3_fusb", P0, 64),
    ("a3f_in", 64, 256), ("a3f_cw", 128, 4), ("a3f_cb", 128, 1), ("a3f_dl", 128, 4),
    ("a3f_bc", 128, 96), ("a3f_dt", 4, 128), ("a3f_dtb", 128, 1), ("a3f_Alog", 128, 16),
    ("a3f_Dp", 128, 1), ("a3f_out", 128, 64),
    ("a3b_in", 64, 256), ("a3b_cw", 128, 4), ("a3b_cb", 128, 1), ("a3b_dl", 128, 4),
    ("a3b_bc", 128, 96), ("a3b_dt", 4, 128), ("a3b_dtb", 128, 1), ("a3b_Alog", 128, 16),
    ("a3b_Dp", 128, 1), ("a3b_out", 128, 64),
    ("f3_g", 64, 1), ("f3_b", 64, 1), ("f3_rt", 64, 8), ("f3_rtb", P0, 8),
    ("f3_w1", 64, 8 * 128), ("f3_b1", 128, 8), ("f3_w2", 128, 8 * 64), ("f3_b2", 8, 64),
]
OFF = {}
WCOLS = 0
for _n, _r, _c in SPEC:
    OFF[_n] = (_r, WCOLS, _c)
    WCOLS += _c


class Channel:

    def __init__(self, full, free, slots):
        self.full, self.free, self.slots = full, free, slots
        self.n_put = self.n_got = 0

    def put(self):
        k = self.n_put
        self.n_put += 1
        return self.slots[k % len(self.slots)], k - len(self.slots) + 1

    def get(self):
        k = self.n_got
        self.n_got += 1
        return self.slots[k % len(self.slots)], k + 1


def audio_tower(nc, x, pack, selectors, w2s, out):
    ctx = ExitStack()
    with ctx:
        LOOP_OF = dict(x=0, conv=0, a0=0, sx=0, A=0, f0=1, a1=1, f1=2, f1e=2,
                       a2=3, f2=3, a3=4, a3f=4, a3b=4, f3=4, f3e=4, h=4, out=4)
        pool_of_sems, named = [], [{} for _ in range(5)]

        def S(name):
            names = named[LOOP_OF[name.split("_")[0]]]
            if name not in names:
                if len(names) == len(pool_of_sems):
                    pool_of_sems.append(ctx.enter_context(nc.semaphore(f"signal{len(names)}")))
                names[name] = pool_of_sems[len(names)]
            return names[name]

        def sb(name, shape, dt=F32):
            return ctx.enter_context(nc.sbuf_tensor(name, shape, dt))

        arrive, go, weights_in, w2_in = (ctx.enter_context(nc.semaphore(n)) for n in
                                         ("engines_arrived", "iteration_over", "weights_in", "w2_in"))
        consts_ready = ctx.enter_context(nc.semaphore("consts_ready"))

        WP = sb("weights", [128, WCOLS])
        W2N = sb("tree_w2", [128, 2, 4096])

        def P(name, a=0, b=None):
            r, o, c = OFF[name]
            return WP[0:r, o + a:o + (c if b is None else b)]

        PS = ctx.enter_context(nc.psum_tensor("psum", [128, 8, 512], F32))

        def singles(lo, hi):
            return [PS[:, i, :] for i in range(lo, hi)]

        def pairs(lo, hi):
            return [PS[:, i:i + 2, :] for i in range(lo, hi, 2)]

        channels = {}

        def chan(name, slots):
            if name not in channels:
                channels[name] = Channel(S(name + "_full"), S(name + "_free"), slots)
            return channels[name]

        identb = sb("identb", [128, 128], BF16)
        maskqk = sb("maskqk", [P0, P0], BF16)
        maskkq = sb("maskkq", [P0, P0], BF16)
        selrep = sb("selrep", [128, 4 * 128], BF16)
        selmoe = sb("selmoe", [96, KT1 * 128], BF16)
        selbn = sb("selbn", [96, 32 * 128], BF16)
        nA0 = sb("nA0", [128, 16])
        nA3 = sb("nA3", [128, 2, 16])
        h_all = sb("h_all", [P0, B * TB, D])
        sx_all = sb("sx_all", [P0, B * TB, D])
        xtail = sb("xtail", [TAIL, NB, D])
        h = sb("h", [P0, T, D])
        X = sb("X", [P0, T, D + 1])
        Xs = X[:, :, 0:D]
        xn = sb("xn", [P0, T, D])
        sq = sb("sq", [P0, T, D])
        fx = sb("fx", [P0, T, D])
        xtok = fx
        st_sum = sb("st_sum", [P0, T * 4])
        st_mean = sb("st_mean", [P0, T * 4])
        st_var = sb("st_var", [P0, T * 4])
        st_std = sb("st_std", [P0, T * 4])
        st_rstd = sb("st_rstd", [P0, T * 8])
        FB = sb("FB", [128, 13 * W])
        F = [FB[:, i * W:(i + 1) * W] for i in range(13)]
        xT = FB[0:D, 9 * W:9 * W + NB * XW].rearrange("p (b n) -> p b n", b=NB)
        Hb = [sb(f"Hb{i}", [128, W], BF16) for i in range(3)]
        SCB = sb("SCB", [128, 8 * LB])
        RA, RB, RS, RC = ([SCB[:, (2 * r + i) * LB:(2 * r + i + 1) * LB] for i in range(2)] for r in range(4))
        otok = SCB[0:P0, 0:T * 256].rearrange("p (t n) -> p t n", n=256)
        otok2 = SCB[0:P0, T * 256:T * 512].rearrange("p (t n) -> p t n", n=256)
        PT = [SCB[0:P0, 2 * CH * i:2 * CH * (i + 1)].rearrange("p (m n) -> p m n", m=2) for i in range(4)]
        O0 = [SCB[:, (4 + e) * LB:(5 + e) * LB] for e in range(E0)]
        ok0, gk0 = (FB[0:P0, 7 * W + i * T * 256:7 * W + (i + 1) * T * 256].rearrange("p (t n) -> p t n", n=256)
                    for i in range(2))
        vtok = sb("vtok", [P0, T, 128])
        Q6 = FB[0:99, 3 * W:11 * W].bitcast(BF16).rearrange("p (h n) -> p h n", n=LB)
        K6 = FB[0:99, 11 * W:13 * W].bitcast(BF16).rearrange("p (h n) -> p h n", n=LB)
        part_r = [SCB[:, (2 + i) * LB:(3 + i) * LB] for i in range(2)]
        part_h, part_m, part_a, part_z = ([SCB[:, (4 + k) * LB:(5 + k) * LB].bitcast(BF16)[:, i * LB:(i + 1) * LB]
                                           for i in range(2)] for k in range(4))
        M3 = sb("M3", [P0, TB, 48], BF16)
        MR = sb("MR", [48, LB], BF16)

        def part_x(tag, s):
            return SCB[:, (s % 2) * LB:(s % 2 + 1) * LB]

        def strips(s):
            i = s % 2
            return (part_a[i], part_z[i], part_m[i]) if s == 0 else (part_h[i], part_a[i], part_z[i])

        mx = sb("mx", [P0, E0, NH, 2, TB])
        m2 = sb("m2", [P0, E0, NH, TB])
        qtok, ktok = (z[:, :, :].rearrange("p t f -> p (t f)")[:, 0:T * 32].rearrange("p (t r) -> p t r", r=32)
                      for z in (fx, xn))
        W96 = otok2.rearrange("p t n -> p (t n)")[:, 0:T * 96].rearrange("p (t n) -> p t n", n=96)
        SAr = [SCB[:, i * CH:(i + 1) * CH] for i in range(3)]
        HH = [SCB[:, (3 + i) * CH:(4 + i) * CH] for i in range(3)]
        rl = sb("rl", [P0, T, 4])
        lg = sb("lg", [P0, T, 16])
        lg2 = sb("lg2", [P0, T, 16])
        sm = sb("sm", [P0, T * 8])
        pad0 = sb("pad0", [P0, T, D])
        eqb = [sb(f"eq{i}", [P0, T, 8]) for i in range(5)]
        r8 = [sb(f"r8_{i}", [P0, T]) for i in range(6)]
        xsp = FB[:, 11 * W:11 * W + NB * (LB + 6)].rearrange("p (b n) -> p b n", b=NB)
        ksm = sb("ksm", [64, 8])
        kvs, kvs2 = (F[12][:, 64 * i:64 * i + 64].rearrange("p (t r) -> p t r", t=2) for i in range(2))
        Mh, kxm = F[12][0:32, 128:192], F[12][0:32, 192:448]
        wrq, wrk = F[11][0:64, 0:128], F[11][0:64, 128:256]
        prod = [FB[0:P0, 3 * W:3 * W + 4096], SCB[0:P0, 0:4096]]
        Lg, Ag = (FB[0:P0, 3 * W + 4096 + i * T * 256:3 * W + 4096 + (i + 1) * T * 256].rearrange(
            "p (t n) -> p t n", n=256) for i in range(2))

        def bc(ap, n):
            return ap.unsqueeze(len(ap.shape)).broadcast_to(list(ap.shape) + [n])

        def bt(ap, n):
            return ap.unsqueeze(1).broadcast_to([ap.shape[0], n, ap.shape[1]])

        def cols(c):
            return slice(c * CH, (c + 1) * CH)

        def tcols(t):
            return slice(t * P0, (t + 1) * P0)


        def dve_norm(dve, src, dst, n, f, eps, tag, centre=True):
            s, m, v, d, r = (z[:, 0:n] for z in (st_sum, st_mean, st_var, st_std, st_rstd))
            sqv = sq[:, :, :].rearrange("p t f -> p (t f)").rearrange("p (n f) -> p n f", f=f)
            src_c = src
            if centre:
                dve.tensor_reduce(s, src, AX.X, ALU.add)
                dve.drain()
                dve.tensor_scalar(m, s, 1.0 / f, None, ALU.mult)
                dve.drain()
                dve.tensor_tensor(dst, src, bc(m, f), ALU.subtract)
                dve.drain()
                src_c = dst
            dve.tensor_tensor(sqv, src_c, src_c, ALU.mult)
            dve.drain()
            dve.tensor_reduce(s, sqv, AX.X, ALU.add)
            dve.drain()
            dve.tensor_scalar(v, s, 1.0 / f, eps, ALU.mult, ALU.add).then_inc(S(tag + "_var"), 1)
            dve.wait_ge(S(tag + "_std"), 1)
            dve.reciprocal(r, d)
            dve.drain()
            return dve.tensor_tensor(dst, src_c, bc(r, f), ALU.mult)

        def act_norm(act, n, tag):
            act.wait_ge(S(tag + "_var"), 1)
            act.activation(st_std[:, 0:n], st_var[:, 0:n], ACT.Sqrt).then_inc(S(tag + "_std"), 1)

        def pe_turn(pe, A, src, f, ready):
            if ready:
                pe.wait_ge(S(ready), 1)
            for c in range(NC):
                ps, w = A.put()
                if w > 0:
                    pe.wait_ge(A.free, w)
                for k in range(CT):
                    ins = pe.transpose(ps[0:f, tcols(k)], src[:, c * CT + k, 0:f], P("ident")[0:P0, 0:P0])
                ins.then_inc(A.full, 1)

        def pe_project(pe, A, weights, src, rows):
            for c in range(NC):
                ps, w = A.put()
                if w > 0:
                    pe.wait_ge(A.free, w)
                pe.matmul(ps[0:rows, 0:CH], weights, src[:, cols(c)], start=True, stop=True).then_inc(A.full, 1)

        def act_empty(act, A, dst, rows, func=ACT.Identity, scale=1.0, bias=0.0, signal=None):
            for c in range(NC):
                ps, w = A.get()
                act.wait_ge(A.full, w)
                act.activation(dst[0:rows, cols(c)], ps[0:rows, 0:CH], func, scale=scale, bias=bias).then_inc(A.free, 1)
            if signal:
                act.drain().then_inc(S(signal), 1)

        def pe_tokens(pe, A, terms, n):
            for b in range(NB):
                ps, w = A.put()
                if w > 0:
                    pe.wait_ge(A.free, w)
                for j in range(TB):
                    for i, (src, rhs) in enumerate(terms):
                        ins = pe.matmul(ps[0:P0, j * n:(j + 1) * n], src[:, tcols(b * TB + j)], rhs,
                                        start=(i == 0), stop=(i == len(terms) - 1))
                ins.then_inc(A.full, 1)

        def tok(ps, n):
            return ps[0:P0, 0:TB * n].rearrange("p (t n) -> p t n", n=n)

        def tiles(b):
            return slice(b * TB, (b + 1) * TB)

        def dve_softmax(dve, src, dst, n, f, tag):
            s = sm[:, 0:n]
            dve.tensor_reduce(s, src, AX.X, ALU.max)
            dve.drain()
            dve.tensor_tensor(dst, src, bc(s, f), ALU.subtract).then_inc(S(tag + "_sub"), 1)
            dve.wait_ge(S(tag + "_exp"), 1)
            dve.tensor_reduce(s, dst, AX.X, ALU.add)
            dve.drain()
            dve.reciprocal(st_rstd[:, 0:n], s)
            dve.drain()
            return dve.tensor_tensor(dst, dst, bc(st_rstd[:, 0:n], f), ALU.mult)

        def act_softmax(act, dst, tag):
            act.wait_ge(S(tag + "_sub"), 1)
            act.activation(dst, dst, ACT.Exp).then_inc(S(tag + "_exp"), 1)

        def softplus_act(act, t, a, l, tag):
            act.activation(a, t, ACT.Abs)
            act.drain()
            act.activation(a, a, ACT.Exp, scale=-1.0)
            act.drain()
            act.activation(l, a, ACT.Ln, bias=1.0).then_inc(S(tag), 1)

        def softplus_dve(dve, t, a, l, tmp, mask, tag):
            dve.wait_ge(S(tag), 1)
            dve.tensor_scalar(tmp, a, 1.0 / 3.0, -0.5, ALU.mult, ALU.add)
            dve.tensor_scalar(mask, a, 2.0 ** -6, None, ALU.is_lt)
            dve.drain()
            dve.tensor_tensor(tmp, tmp, a, ALU.mult)
            dve.drain()
            dve.scalar_tensor_tensor(out=tmp, in0=tmp, scalar=1.0, in1=a, op0=ALU.add, op1=ALU.mult)
            dve.drain()
            dve.copy_predicated(l, mask, tmp)
            dve.drain()
            return dve.scalar_tensor_tensor(out=l, in0=t, scalar=0.0, in1=l, op0=ALU.max, op1=ALU.add)

        mask8 = sb("mask8", [128, W], U8)


        def conv_sp(sp, it):
            for b in range(NB):
                src = x[bass.ds(it * NB + b, 1), :, :]
                sp.dma_start(xtok[:, tiles(b), :],
                             src[:, 0:LB, :].rearrange("b (j p) f -> p (b j) f", p=P0)).then_inc(S("x_in"), 16)
                sp.dma_start(xtail[:, b:b + 1, :],
                             src[:, LB:LX, :].rearrange("b p f -> p b f")).then_inc(S("x_in"), 16)

        def conv_pe(pe):
            A = chan("conv_turned", singles(0, 4))
            pe.wait_ge(S("x_in"), 32 * NB)
            pe_turn(pe, A, xtok, D, None)
            for b in range(NB):
                ps, w = A.put()
                if w > 0:
                    pe.wait_ge(A.free, w)
                pe.transpose(ps[0:D, 0:TAIL], xtail[:, b, :], P("ident")[0:TAIL, 0:TAIL]).then_inc(A.full, 1)
            pe.wait_ge(S("conv_xT"), 1)
            pe.wait_ge(S("conv_padded"), 1)
            Y = chan("conv_out", singles(4, 8))
            for b in range(NB):
                ps, w = Y.put()
                if w > 0:
                    pe.wait_ge(Y.free, w)
                for j in range(TB):
                    for k, o in enumerate(TAPS):
                        ins = pe.matmul(ps[0:P0, j * D:(j + 1) * D], xT[:, b, j * P0 + o:(j + 1) * P0 + o],
                                        P("tok_w", k * D, (k + 1) * D), start=(k == 0), stop=(k == 7))
                ins.then_inc(Y.full, 1)

        def conv_act(act):
            A = chan("conv_turned", None)
            for c in range(NC):
                ps, w = A.get()
                act.wait_ge(A.full, w)
                act.activation(xT[:, c // 2, (c % 2) * CH:(c % 2 + 1) * CH], ps[0:D, 0:CH], ACT.Identity).then_inc(A.free, 1)
            for b in range(NB):
                ps, w = A.get()
                act.wait_ge(A.full, w)
                act.activation(xT[:, b, LB:LX], ps[0:D, 0:TAIL], ACT.Identity).then_inc(A.free, 1)
            act.drain().then_inc(S("conv_xT"), 1)

        def conv_dve(dve):
            dve.memset(xT[:, :, LX:XW], 0.0).then_inc(S("conv_padded"), 1)
            Y = chan("conv_out", None)
            for b in range(NB):
                ps, w = Y.get()
                dve.wait_ge(Y.full, w)
                dve.tensor_tensor(h[:, tiles(b), :], tok(ps, D), bt(P("tok_b"), TB), ALU.add).then_inc(Y.free, 1)
            dve.drain()


        A0 = dict(xT=F[0], u=F[1], sz=F[2], dt=F[3], Bm=F[4], Cm=F[5], t=F[6], a=F[7], y=F[8])

        def scan0_pe(pe):
            A = chan("a0_proj", singles(0, 4))
            pe_turn(pe, A, xn, D, "a0_normed")
            pe.wait_ge(S("a0_xT"), 1)
            pe_project(pe, A, P("a0_xp", 0, 128), A0["xT"][0:D, :], 128)
            pe_project(pe, A, P("a0_xp", 128, 256), A0["xT"][0:D, :], 128)
            pe.wait_ge(S("a0_u"), 1)
            for n in ("a0_dt", "a0_B", "a0_C"):
                pe_project(pe, A, P(n), A0["u"], 128)
            pe.wait_ge(S("a0_split"), 1)
            pe.wait_ge(A.free, A.n_put)
            R = chan("a0_rep", pairs(0, 6))
            Y = chan("a0_sum", pairs(6, 8))
            n = 16 * NB
            for k in range(n + 3):
                if k < n:
                    b, g = divmod(k, 16)
                    q, r = slice(32 * (g // 4), 32 * (g // 4) + 32), g % 4
                    ps, w = R.put()
                    if w > 0:
                        pe.wait_ge(R.free, w)
                    for c in range(2):
                        for i in range(3):
                            ins = pe.matmul(ps[:, c, 0:CH], selrep[q, r * 128:(r + 1) * 128],
                                            Hb[i][q, cols(2 * b + c)], start=(i == 0), stop=(i == 2))
                    ins.then_inc(R.full, 1)
                if k >= 3:
                    i = k - 3
                    q, r = i % 16 // 4, i % 4
                    if i % 16 == 0:
                        y, w = Y.put()
                        if w > 0:
                            pe.wait_ge(Y.free, w)
                    pe.wait_ge(S("a0_read"), i + 1)
                    for c in range(2):
                        ins = pe.matmul(y[32 * q:32 * q + 32, c, 0:CH], P("sel_sum", 32 * r, 32 * r + 32),
                                        RC[i % 2][:, cols(c)], start=(r == 0), stop=(r == 3))
                    ins.then_inc(S("a0_summed"), 1)
                    if i % 16 == 15:
                        pe.drain().then_inc(Y.full, 1)
            pe.wait_ge(S("a0_y"), 1)
            Y2 = chan("a0_out", singles(0, 4))
            pe_tokens(pe, Y2, [(A0["y"], P("a0_out"))], D)

        def scan0_act(act):
            act_norm(act, T, "a0")
            A = chan("a0_proj", None)
            act_empty(act, A, A0["xT"], D, signal="a0_xT")
            act_empty(act, A, A0["u"], 128, func=ACT.Silu, signal="a0_u")
            act_empty(act, A, A0["sz"], 128, func=ACT.Silu)
            act_empty(act, A, A0["t"], 128, bias=P("a0_dtb"))
            act_empty(act, A, A0["Bm"], 128)
            act_empty(act, A, A0["Cm"], 128, signal="a0_BC")
            softplus_act(act, A0["t"], A0["a"], A0["dt"], "a0_ln")
            act.wait_ge(S("a0_dt"), 1)
            for k in range(16 * NB):
                b, g = divmod(k, 16)
                if k >= 2:
                    act.wait_ge(S("a0_scanned"), k - 1)
                act.activation(RA[k % 2], A0["dt"][:, b * LB:(b + 1) * LB], ACT.Exp,
                               scale=nA0[:, g:g + 1]).then_inc(S("a0_decay"), 1)

        def dve_split(dve, src, parts, tmp):
            dve.tensor_copy(parts[0], src)
            dve.drain()
            dve.tensor_tensor(tmp, src, parts[0], ALU.subtract)
            dve.drain()
            dve.tensor_copy(parts[1], tmp)
            dve.drain()
            dve.tensor_tensor(tmp, tmp, parts[1], ALU.subtract)
            dve.drain()
            return dve.tensor_copy(parts[2], tmp)

        def scan0_dve(dve):
            dve_norm(dve, h[:, :, :], xn[:, :, :], T, D, 1e-5, "a0").then_inc(S("a0_normed"), 1)
            dve.wait_ge(S("a0_u"), 1)
            dve_split(dve, A0["u"][:, :], [z[:, :] for z in Hb], F[9][:, :]).then_inc(S("a0_split"), 1)
            dve.wait_ge(S("a0_BC"), 1)
            softplus_dve(dve, A0["t"][:, :], A0["a"][:, :], A0["dt"][:, :], F[10][:, :], mask8[:, :],
                         "a0_ln").then_inc(S("a0_dt"), 1)
            dve.drain()
            dve.tensor_tensor(A0["Bm"][:, :], A0["Bm"][:, :], A0["dt"][:, :], ALU.mult)
            dve.drain()
            R = chan("a0_rep", None)
            n = 16 * NB
            for k in range(n + 2):
                if k < n:
                    b = k // 16
                    ps, w = R.get()
                    dve.wait_ge(R.full, w)
                    dve.tensor_tensor(RB[k % 2][:, :].rearrange("p (c n) -> p c n", c=2), ps[:, :, 0:CH],
                                      A0["Bm"][:, b * LB:(b + 1) * LB].rearrange("p (c n) -> p c n", c=2),
                                      ALU.mult).then_inc(R.free, 1)
                if 1 <= k <= n:
                    i = k - 1
                    dve.wait_ge(S("a0_decay"), i + 1)
                    dve.tensor_tensor_scan(RS[i % 2][:, :], RA[i % 2][:, :], RB[i % 2][:, :], 0.0, ALU.mult,
                                           ALU.add).then_inc(S("a0_scanned"), 1)
                if k >= 2:
                    i = k - 2
                    b = i // 16
                    if i >= 2:
                        dve.wait_ge(S("a0_summed"), i - 1)
                    dve.tensor_tensor(RC[i % 2][:, :], RS[i % 2][:, :], A0["Cm"][:, b * LB:(b + 1) * LB],
                                      ALU.mult).then_inc(S("a0_read"), 1)
                dve.drain()
                if k >= 2 and (k - 2) % 16 == 15:
                    b = (k - 2) // 16
                    Y = chan("a0_sum", None)
                    ps, w = Y.get()
                    cs = slice(b * LB, (b + 1) * LB)
                    dve.wait_ge(Y.full, w)
                    v = lambda z: z[:, cs].rearrange("p (c n) -> p c n", c=2)
                    dve.scalar_tensor_tensor(out=v(A0["y"]), in0=v(A0["u"]), scalar=P("a0_D"), in1=ps[:, :, 0:CH],
                                             op0=ALU.mult, op1=ALU.add).then_inc(Y.free, 1)
                    dve.drain()
                    ins = dve.tensor_tensor(A0["y"][:, cs], A0["y"][:, cs], A0["sz"][:, cs], ALU.mult)
            ins.then_inc(S("a0_y"), 1)
            dve.drain()
            dve_residual(dve, "a0_out")

        def dve_residual(dve, name):
            Y2 = chan(name, None)
            for b in range(NB):
                ps, w = Y2.get()
                dve.wait_ge(Y2.full, w)
                dve.tensor_tensor(h[:, tiles(b), :], h[:, tiles(b), :], tok(ps, D), ALU.add).then_inc(Y2.free, 1)
            dve.drain()


        def sx_pe(pe):
            A = chan("sx_turned", singles(4, 8))
            pe_turn(pe, A, X, D, "sx_normed")
            pe.wait_ge(S("sx_xT"), 1)
            Y = chan("sx_out", singles(0, 4))
            pe_tokens(pe, Y, [(F[0][0:D, :], P("f0_hl"))], D)

        def sx_act(act):
            act_norm(act, T, "sx")
            act_empty(act, chan("sx_turned", None), F[0], D, signal="sx_xT")

        def sx_dve(dve, it):
            dve_norm(dve, h[:, :, :], Xs, T, D, 1e-5, "sx").then_inc(S("sx_normed"), 1)
            dve.tensor_copy(h_all[:, bass.ds(it * T, T), :], h[:, :, :])
            Y = chan("sx_out", None)
            for b in range(NB):
                ps, w = Y.get()
                dve.wait_ge(Y.full, w)
                dve.tensor_tensor(fx[:, tiles(b), :], tok(ps, D), bt(P("f0_hlb_bc"), TB), ALU.add).then_inc(Y.free, 1)
            dve.drain()
            dve.tensor_copy(sx_all[:, bass.ds(it * T, T), :], fx[:, :, :])
            dve.drain()


        def pe_stack(pe, tag, nt, project):
            SP = [chan(f"{tag}_stack{i}", pairs(4 + 2 * i, 6 + 2 * i)) for i in range(2)]
            project(0)
            for s in range(nt):
                if s + 1 < nt:
                    project(s + 1)
                pe.wait_ge(S(f"{tag}_parts"), s + 1)
                for n in range(NH):
                    C = SP[n % 2]
                    ps, w = C.put()
                    if w > 0:
                        pe.wait_ge(C.free, w)
                    for c in range(2):
                        for i in range(3):
                            ins = pe.matmul(ps[32 * i:32 * i + 32, c, 0:CH], identb[:, 32 * n:32 * n + 32],
                                            strips(s)[i][:, cols(c)], start=True, stop=True)
                    ins.then_inc(C.full, 1)

        def stack_copy(eng, copy, tag, s, i):
            C = chan(f"{tag}_stack{i}", None)
            for n in (i, i + 2):
                dst = K6[0:96, n, :] if s == 0 else Q6[0:96, (s - 1) * NH + n, :]
                ps, w = C.get()
                eng.wait_ge(C.full, w)
                copy(dst.rearrange("p (c n) -> p c n", c=2), ps[0:96, :, 0:CH]).then_inc(C.free, 1)

        def act_stack(act, tag, nt, fill):
            for s in range(nt + 1):
                if s < nt:
                    if s >= 2:
                        act.wait_ge(S(f"{tag}_parts"), s - 1)
                    fill(s)
                    if s >= 2:
                        for i in range(2):
                            act.wait_ge(chan(f"{tag}_stack{i}", None).full, 2 * (s - 1))
                    act.activation(part_h[s % 2][:, :], part_x(tag, s), ACT.Identity).then_inc(S(f"{tag}_high"), 1)
                if s >= 1:
                    stack_copy(act, lambda o, i: act.activation(o, i, ACT.Identity), tag, s - 1, 0)
            act.drain().then_inc(S(f"{tag}_stacked"), 1)

        def dve_stack(dve, tag, nt):
            dve.memset(K6[96:99, :, :], 1.0)
            for s in range(nt + 1):
                if s < nt:
                    x, hi, lo = part_x(tag, s), part_h[s % 2], part_m[s % 2]
                    a, z, r = part_a[s % 2], part_z[s % 2], part_r[s % 2]
                    first, both = P("minus", 0, 1), P("minus", 2, 3)
                    second = P("minus", 1, 2)
                    dve.wait_ge(S(f"{tag}_high"), s + 1)
                    dve.scalar_tensor_tensor(out=r, in0=hi[:, :], scalar=first if s == 0 else both, in1=x,
                                             op0=ALU.mult, op1=ALU.add)
                    dve.scalar_tensor_tensor(out=a[:, :], in0=hi[:, :], scalar=second, in1=x, op0=ALU.mult, op1=ALU.add)
                    dve.drain()
                    dve.tensor_copy(lo[:, :], r)
                    dve.drain()
                    dve.scalar_tensor_tensor(out=z[:, :], in0=lo[:, :], scalar=first if s == 0 else second, in1=r,
                                             op0=ALU.mult, op1=ALU.add)
                    dve.drain().then_inc(S(f"{tag}_parts"), 1)
                if s >= 1:
                    stack_copy(dve, dve.tensor_copy, tag, s - 1, 1)
            dve.drain().then_inc(S(f"{tag}_stacked"), 1)

        def attend_pe(pe, tag, ne):
            for i in range(2):
                C = chan(f"{tag}_stack{i}", None)
                pe.wait_ge(C.free, C.n_put)
            pe.wait_ge(S(f"{tag}_stacked"), 2)
            SA = chan(f"{tag}_score", pairs(0, 8))
            for e in range(ne):
                for i in range(TB):
                    for kc in range(1 + (i >= CT)):
                        wd = min(CH, P0 * (i + 1) - kc * CH)
                        diag = i // CT == kc
                        for p in range(2):
                            ps, w = SA.put()
                            if w > 0:
                                pe.wait_ge(SA.free, w)
                            for m in range(2):
                                n = 2 * p + m
                                ins = pe.matmul(ps[0:P0, m, 0:wd], Q6[0:96, e * NH + n, tcols(i)],
                                                K6[0:96, n, kc * CH:kc * CH + wd], start=True, stop=True)
                                if diag:
                                    ins = pe.matmul(ps[0:P0, m, wd - P0:wd], identb[0:P0, 0:P0], maskqk[:, :],
                                                    start=False, stop=True, skip_group_check=True)
                            ins.then_inc(SA.full, 1)
            M = chan(f"{tag}_mrows", pairs(0, 2))
            ps, w = M.put()
            pe.wait_ge(S(f"{tag}_maxima"), 1)
            for i in range(TB):
                ins = pe.matmul(ps[0:3 * NH * ne, i // CT, (i % CT) * P0:(i % CT + 1) * P0], M3[:, i, 0:3 * NH * ne],
                                identb[0:P0, 0:P0], start=True, stop=True)
            ins.then_inc(M.full, 1)
            SB = chan(f"{tag}_scoreT", pairs(0, 6))
            OC = chan(f"{tag}_o", singles(6, 8))
            pe.wait_ge(S(f"{tag}_mplaced"), 48)
            groups = [(e, c, j) for e in range(ne) for c in range(2) for j in range(CT * c + CT)]
            obank = None
            for g in range(len(groups) + 1):
                if g < len(groups):
                    e, c, j = groups[g]
                    off = max(0, j - CT * c) * P0
                    wd = CH - off
                    for p in range(2):
                        ps, w = SB.put()
                        if w > 0:
                            pe.wait_ge(SB.free, w)
                        for m in range(2):
                            n = 2 * p + m
                            ins = pe.matmul(ps[0:P0, m, 0:wd], K6[0:99, n, tcols(j)],
                                            Q6[0:99, e * NH + n, c * CH + off:(c + 1) * CH], start=True, stop=True)
                            if j >= CT * c:
                                ins = pe.matmul(ps[0:P0, m, 0:P0], identb[0:P0, 0:P0], maskkq[:, :],
                                                start=False, stop=True, skip_group_check=True)
                        ins.then_inc(SB.full, 1)
                if g >= 1:
                    e, c, j = groups[g - 1]
                    off = max(0, j - CT * c) * P0
                    if j == 0:
                        obank, w = OC.put()
                        if w > 0:
                            pe.wait_ge(OC.free, w)
                    pe.wait_ge(SB.free, 2 * g)
                    for n in range(NH):
                        ins = pe.matmul(obank[32 * n:32 * n + 32, off:CH], vtok[:, j, 32 * n:32 * n + 32],
                                        PT[(2 * g - 2 + n // 2) % 4][:, n % 2, 0:CH - off], start=(j == 0),
                                        stop=(j == CT * c + CT - 1))
                    ins.then_inc(S(f"{tag}_probs_used"), 1)
                    if j == CT * c + CT - 1:
                        pe.drain().then_inc(OC.full, 1)

        def attend_sp(sp, tag, ne):
            sp.wait_ge(S(f"{tag}_mrow"), 1)
            for i in range(3):
                sp.dma_start(Q6[96 + i:97 + i, 0:NH * ne, :], MR[NH * ne * i:NH * ne * (i + 1), :]).then_inc(S(f"{tag}_mplaced"), 16)

        def attend_act(act, tag, ne):
            M = chan(f"{tag}_mrows", None)
            ps, w = M.get()
            act.wait_ge(M.full, w)
            act.activation(MR[0:3 * NH * ne, :].rearrange("p (c n) -> p c n", c=2), ps[0:3 * NH * ne, :, 0:CH],
                           ACT.Identity).then_inc(S(f"{tag}_mrow"), 1)
            SB = chan(f"{tag}_scoreT", None)
            ku = 0
            for e in range(ne):
                for c in range(2):
                    for j in range(CT * c + CT):
                        for p in range(2):
                            wd = CH - max(0, j - CT * c) * P0
                            ps, w = SB.get()
                            act.wait_ge(SB.full, w)
                            if ku >= 4:
                                act.wait_ge(S(f"{tag}_probs_used"), ku // 2 - 1)
                            act.activation(PT[ku % 4][:, :, 0:wd], ps[0:P0, :, 0:wd], ACT.Exp).then_inc(SB.free, 1)
                            ku += 1

        def attend_dve(dve, tag, oT, ne):
            SA = chan(f"{tag}_score", None)
            dve.memset(mx[:, :, :, 1, 0:CT], -3e38)
            for e in range(ne):
                for i in range(TB):
                    for kc in range(1 + (i >= CT)):
                        wd = min(CH, P0 * (i + 1) - kc * CH)
                        for p in range(2):
                            ps, w = SA.get()
                            dve.wait_ge(SA.full, w)
                            dve.tensor_reduce(mx[:, e, 2 * p:2 * p + 2, kc, i], ps[0:P0, :, 0:wd], AX.X,
                                              ALU.max).then_inc(SA.free, 1)
            dve.drain()
            n = NH * ne
            for e in range(ne):
                dve.tensor_tensor(m2[:, e, :, :], mx[:, e, :, 0, :], mx[:, e, :, 1, :], ALU.max)
            dve.drain()
            mv = m2[:, :, :, :].rearrange("p e n i -> p i (e n)")[:, :, 0:n]
            for i in range(3):
                dve.tensor_scalar(M3[:, :, i * n:(i + 1) * n], mv, -1.0, None, ALU.mult)
                if i < 2:
                    dve.drain()
                    dve.tensor_tensor(mv, mv, M3[:, :, i * n:(i + 1) * n], ALU.add)
                    dve.drain()
            dve.drain().then_inc(S(f"{tag}_maxima"), 1)
            OC = chan(f"{tag}_o", None)
            for e in range(ne):
                for c in range(2):
                    ps, w = OC.get()
                    dve.wait_ge(OC.full, w)
                    dve.tensor_copy(oT[e][:, cols(c)], ps[:, 0:CH]).then_inc(OC.free, 1)
            dve.drain().then_inc(S(f"{tag}_gathered"), 1)

        def ffn0_pe(pe):
            A = chan("f0_proj", singles(0, 2))
            pe_turn(pe, A, X, D, "f0_normed")
            pe.wait_ge(S("f0_xT"), 1)
            pe_project(pe, A, P("f0_hl"), F[0][0:D, :], D)
            pe.wait_ge(S("f0_sxT"), 1)
            V = chan("f0_v", singles(2, 4))
            for c in range(NC):
                ps, w = V.put()
                if w > 0:
                    pe.wait_ge(V.free, w)
                for k in range(CT):
                    ins = pe.matmul(ps[0:P0, k * 128:(k + 1) * 128], F[1][0:D, tcols(c * CT + k)], P("f0_wv"),
                                    start=True, stop=True)
                ins.then_inc(V.full, 1)
            pe_stack(pe, "f0", 1 + E0, lambda s: pe_project(
                pe, A, P("f0_wk") if s == 0 else P("f0_wq", (s - 1) * 128, s * 128), F[1][0:D, :], 128))
            pe.wait_ge(S("f0_vtok"), 1)
            attend_pe(pe, "f0", E0)
            pe.wait_ge(S("f0_gathered"), NB)
            G = chan("f0_oback", singles(0, 4))
            for e in range(E0):
                for c in range(NC):
                    ps, w = G.put()
                    if w > 0:
                        pe.wait_ge(G.free, w)
                    for k in range(CT):
                        ins = pe.transpose(ps[0:P0, k * 128:(k + 1) * 128], O0[e][:, tcols(c * CT + k)], P("ident"))
                    ins.then_inc(G.full, 1)
            pe.wait_ge(S("f0_masked"), 1)
            H = chan("f0_oturn", singles(4, 8))
            for hh in range(2):
                for c in range(NC):
                    ps, w = H.put()
                    if w > 0:
                        pe.wait_ge(H.free, w)
                    for k in range(CT):
                        ins = pe.transpose(ps[:, tcols(k)], ok0[:, c * CT + k, hh * 128:(hh + 1) * 128],
                                           P("ident")[0:P0, 0:P0])
                    ins.then_inc(H.full, 1)
            pe.wait_ge(S("f0_oturned"), 1)
            pe_tokens(pe, chan("f0_gates", singles(0, 4)),
                      [(F[3], P("f0_gate", 0, 16)), (F[4], P("f0_gate", 16, 32))], 16)
            Z = chan("f0_fc", singles(4, 8))
            pe_turn(pe, Z, fx, D, "f0_fx")
            pe.wait_ge(S("f0_fxT"), 1)
            pe_project(pe, Z, P("f0_fc1"), F[5][0:D, :], D)
            pe.wait_ge(S("f0_h1"), 1)
            pe_tokens(pe, chan("f0_fc2", singles(0, 4)), [(F[6][0:D, :], P("f0_fc2"))], D)
            pe_turn(pe, Z, xn, D, "f0_fout")
            pe.wait_ge(S("f0_foutT"), 1)
            pe_tokens(pe, chan("f0_fg", singles(0, 4)), [(F[7][0:D, :], P("f0_fg"))], 4)

        def ffn0_act(act):
            act_norm(act, T, "f0")
            A = chan("f0_proj", None)
            act_empty(act, A, F[0], D, signal="f0_xT")
            act_empty(act, A, F[1], D, bias=P("f0_hlb"), signal="f0_sxT")

            def fill(s):
                act_empty(act, A, part_x("f0", s), 128, scale=4.0 if s == 0 else 1.0)
                act.drain()

            act_stack(act, "f0", 1 + E0, fill)
            attend_act(act, "f0", E0)
            H = chan("f0_oturn", None)
            act_empty(act, H, F[3], 128)
            act_empty(act, H, F[4], 128, signal="f0_oturned")
            act_softmax(act, lg2[:, :, :], "f0_gs")
            act_norm(act, T * 4, "f0_ln")
            Z = chan("f0_fc", None)
            act_empty(act, Z, F[5], D, signal="f0_fxT")
            act_empty(act, Z, F[6], D, func=ACT.Relu, bias=P("f0_fc1b"), signal="f0_h1r")
            act_norm(act, T * 4, "f0_fn")
            act_empty(act, Z, F[7], D, signal="f0_foutT")
            act_softmax(act, lg2[:, :, 0:4], "f0_fgs")

        def ffn0_dve(dve, it):
            dve.tensor_copy(fx[:, :, :], sx_all[:, bass.ds(it * T, T), :])
            dve.drain()
            dve.tensor_scalar(pad0[:, :, :], fx[:, :, :], 0.0, None, ALU.not_equal)
            dve_norm(dve, h[:, :, :], Xs, T, D, 1e-5, "f0").then_inc(S("f0_normed"), 1)
            V = chan("f0_v", None)
            for c in range(NC):
                ps, w = V.get()
                dve.wait_ge(V.full, w)
                dve.tensor_tensor(vtok[:, c * CT:(c + 1) * CT, :], ps[0:P0, 0:CT * 128].rearrange("p (t n) -> p t n", n=128),
                                  bt(P("ones_col"), CT), ALU.add).then_inc(V.free, 1)
            dve.drain().then_inc(S("f0_vtok"), 1)
            dve_stack(dve, "f0", 1 + E0)
            attend_dve(dve, "f0", O0, E0)
            G = chan("f0_oback", None)
            ov = ok0[:, :, :].rearrange("p t (n e d) -> p t n e d", n=NH, e=E0)
            for e in range(E0):
                for c in range(NC):
                    ps, w = G.get()
                    dve.wait_ge(G.full, w)
                    pv = ps[0:P0, 0:CT * 128].rearrange("p (t n d) -> p t n d", n=NH, d=32)
                    ts = slice(c * CT, (c + 1) * CT)
                    dve.reciprocal(rl[:, ts, :], pv[:, :, :, HD])
                    dve.drain()
                    dve.tensor_tensor(ov[:, ts, :, e, :], pv[:, :, :, 0:HD], bc(rl[:, ts, :], HD), ALU.mult).then_inc(G.free, 1)
                    dve.drain()
            o3 = ok0[:, :, :].rearrange("p t (n e d) -> p (t n) e d", n=NH, e=E0)
            p3 = pad0[:, :, :].rearrange("p t (n d) -> p (t n) d", n=NH)
            dve.tensor_tensor(o3, o3, p3.unsqueeze(2).broadcast_to([P0, T * NH, E0, HD]), ALU.mult).then_inc(S("f0_masked"), 1)
            Gt = chan("f0_gates", None)
            for b in range(NB):
                ps, w = Gt.get()
                dve.wait_ge(Gt.full, w)
                dve.tensor_tensor(lg[:, tiles(b), :], tok(ps, 16), bt(P("f0_gateb"), TB), ALU.add).then_inc(Gt.free, 1)
            dve.drain()
            l3 = lg[:, :, :].rearrange("p t (n e) -> p (t n) e", e=E0)
            g3 = lg2[:, :, :].rearrange("p t (n e) -> p (t n) e", e=E0)
            dve_softmax(dve, l3, g3, T * NH, E0, "f0_gs")
            dve.drain()
            q3 = gk0[:, :, :].rearrange("p t (n e d) -> p (t n) e d", n=NH, e=E0)
            dve.tensor_tensor(q3, o3, bc(g3, HD), ALU.mult)
            dve.drain()
            f3 = fx[:, :, :].rearrange("p t (n d) -> p (t n) d", n=NH)
            dve.tensor_reduce(f3, q3.rearrange("p t e d -> p t d e"), AX.X, ALU.add)
            dve.drain()
            for b in range(NB):
                for n in range(NH):
                    hs = slice(n * HD, (n + 1) * HD)
                    dve.tensor_tensor(fx[:, tiles(b), hs], fx[:, tiles(b), hs], sx_all[:, n * TB:(n + 1) * TB, hs], ALU.add)
            dve.drain()
            dve_norm(dve, f3, f3, T * NH, HD, 1e-8, "f0_ln")
            dve.drain()
            dve.tensor_tensor(fx[:, :, :], fx[:, :, :], bt(P("f0_lng"), T), ALU.mult)
            dve.drain()
            dve.tensor_tensor(fx[:, :, :], fx[:, :, :], bt(P("f0_lnb"), T), ALU.add)
            dve.drain().then_inc(S("f0_fx"), 1)
            dve.tensor_scalar(pad0[:, :, :], fx[:, :, :], 0.0, None, ALU.not_equal)
            dve.wait_ge(S("f0_fxT"), 1)
            dve.tensor_scalar(F[8][0:D, :], F[5][0:D, :], 0.0, None, ALU.not_equal)
            dve.wait_ge(S("f0_h1r"), 1)
            dve.drain()
            dve.tensor_tensor(F[6][0:D, :], F[6][0:D, :], F[8][0:D, :], ALU.mult).then_inc(S("f0_h1"), 1)
            Y = chan("f0_fc2", None)
            for b in range(NB):
                ps, w = Y.get()
                dve.wait_ge(Y.full, w)
                dve.tensor_tensor(xn[:, tiles(b), :], tok(ps, D), bt(P("f0_fc2b"), TB), ALU.add).then_inc(Y.free, 1)
            dve.drain()
            dve.tensor_tensor(xn[:, :, :], xn[:, :, :], pad0[:, :, :], ALU.mult)
            dve.drain()
            dve.tensor_tensor(xn[:, :, :], xn[:, :, :], fx[:, :, :], ALU.add)
            dve.drain()
            x3 = xn[:, :, :].rearrange("p t (n d) -> p (t n) d", n=NH)
            dve_norm(dve, x3, x3, T * NH, HD, 1e-8, "f0_fn")
            dve.drain()
            dve.tensor_tensor(xn[:, :, :], xn[:, :, :], bt(P("f0_fng"), T), ALU.mult)
            dve.drain()
            dve.tensor_tensor(xn[:, :, :], xn[:, :, :], bt(P("f0_fnb"), T), ALU.add)
            dve.drain().then_inc(S("f0_fout"), 1)
            Y = chan("f0_fg", None)
            for b in range(NB):
                ps, w = Y.get()
                dve.wait_ge(Y.full, w)
                dve.tensor_copy(lg[:, tiles(b), 0:4], tok(ps, 4)).then_inc(Y.free, 1)
            dve.drain()
            dve_softmax(dve, lg[:, :, 0:4], lg2[:, :, 0:4], T, 4, "f0_fgs")
            dve.drain()
            for n in range(NH):
                hs = slice(n * HD, (n + 1) * HD)
                dve.tensor_tensor(xn[:, :, hs], xn[:, :, hs], bc(lg2[:, :, n], HD), ALU.mult)
            dve.drain()
            dve.tensor_tensor(h[:, :, :], h[:, :, :], xn[:, :, :], ALU.add)
            dve.drain()


        def pe_back(pe, A, src, rows, n, ready):
            pe.wait_ge(S(ready), 1)
            for b in range(NB):
                ps, w = A.put()
                if w > 0:
                    pe.wait_ge(A.free, w)
                for j in range(TB):
                    ins = pe.transpose(ps[0:P0, j * n:(j + 1) * n], src[0:rows, tcols(b * TB + j)],
                                       P("ident")[0:rows, 0:rows])
                ins.then_inc(A.full, 1)

        def attn1_pe(pe):
            A = chan("a1_proj", singles(0, 4))
            pe_turn(pe, A, xn, D, "a1_normed")
            pe.wait_ge(S("a1_xT"), 1)
            pe_project(pe, A, P("a1_Wx", 0, 128), F[0][0:D, :], 128)
            pe_project(pe, A, P("a1_Wx", 128, 256), F[0][0:D, :], 128)
            V = chan("a1_xm_tok", singles(4, 8))
            for t in range(T):
                ps, w = V.put()
                if w > 0:
                    pe.wait_ge(V.free, w)
                pe.matmul(ps[0:P0, 0:256], F[0][0:D, tcols(t)], P("a1_Wx"), start=True, stop=True).then_inc(V.full, 1)
            pe.wait_ge(S("a1_xm"), 1)
            pe.wait_ge(V.free, V.n_put)
            Q = chan("a1_qk", singles(4, 8))
            for c in range(NC):
                ps, w = Q.put()
                if w > 0:
                    pe.wait_ge(Q.free, w)
                pe.matmul(ps[0:64, 0:CH], P("a1_qk", 0, 64), F[1][:, cols(c)], start=True, stop=False)
                pe.matmul(ps[0:64, 0:CH], P("a1_qk", 64, 128), F[2][:, cols(c)], start=False, stop=True).then_inc(Q.full, 1)
            G = chan("a1_back", singles(0, 2))
            pe_back(pe, G, F[4], 64, 64, "a1_kexp")
            pe.wait_ge(S("a1_ktok"), 1)
            K = chan("a1_kx", singles(2, 4))
            U = chan("a1_attn", singles(0, 2))
            for b in range(NB):
                ps, w = K.put()
                if w > 0:
                    pe.wait_ge(K.free, w)
                for j in range(TB):
                    t = b * TB + j
                    ins = pe.matmul(ps[0:32, 0:256], ktok[:, t, :], otok[:, t, :], start=(j == 0), stop=(j == TB - 1))
                ins.then_inc(K.full, 1)
                pe.wait_ge(S("a1_kxm"), b + 1)
                ps, w = K.put()
                if w > 0:
                    pe.wait_ge(K.free, w)
                for k in range(2):
                    ins = pe.transpose(ps[:, 32 * k:32 * k + 32], kxm[:, 128 * k:128 * k + 128], P("ident")[0:32, 0:32])
                ins.then_inc(K.full, 1)
                pe.wait_ge(S("a1_kvs"), b + 1)
                ps, w = K.put()
                if w > 0:
                    pe.wait_ge(K.free, w)
                ins = pe.matmul(ps[:, 0:64], P("a1_Wv"), kvs[:, :, :].rearrange("p t r -> p (t r)"), start=True, stop=True)
                ins.then_inc(K.full, 1)
                pe.wait_ge(S("a1_kvs2"), b + 1)
                ps, w = K.put()
                if w > 0:
                    pe.wait_ge(K.free, w)
                for k in range(2):
                    ins = pe.matmul(ps[0:32, 0:64], kvs2[:, k, :], P("a1_Wo", 64 * k, 64 * k + 64), start=(k == 0), stop=(k == 1))
                ins.then_inc(K.full, 1)
                if b == 0:
                    Z = chan("a1_q", singles(4, 8))
                    pe.wait_ge(S("a1_qsoft"), 1)
                    pe.wait_ge(Q.free, Q.n_put)
                    for c in range(NC):
                        zs, w = Z.put()
                        if w > 0:
                            pe.wait_ge(Z.free, w)
                        for k in range(CT):
                            ins = pe.transpose(zs[0:32, tcols(k)], qtok[:, c * CT + k, :], P("ident")[0:P0, 0:P0])
                        ins.then_inc(Z.full, 1)
                    pe.wait_ge(S("a1_qT"), 1)
                    pe.wait_ge(G.free, G.n_put)
                pe.wait_ge(S("a1_M"), b + 1)
                us, w = U.put()
                if w > 0:
                    pe.wait_ge(U.free, w)
                for j in range(TB):
                    ins = pe.matmul(us[0:P0, j * D:(j + 1) * D], F[5][0:32, tcols(b * TB + j)], Mh, start=True, stop=True)
                ins.then_inc(U.full, 1)
            M = chan("a1_mlp", singles(2, 6))
            pe.wait_ge(Z.free, Z.n_put)
            pe.wait_ge(K.free, K.n_put)
            pe_turn(pe, M, xn, D, "a1_n2")
            pe.wait_ge(S("a1_x2T"), 1)
            pe_project(pe, M, P("a1_W1", 0, 128), F[0][0:D, :], 128)
            pe_project(pe, M, P("a1_W1", 128, 256), F[0][0:D, :], 128)
            pe.wait_ge(S("a1_gelu"), 1)
            pe_tokens(pe, chan("a1_out", singles(6, 8)), [(F[1], P("a1_W2", 0, 64)), (F[2], P("a1_W2", 64, 128))], D)

        def attn1_act(act):
            act_norm(act, T, "a1_x")
            act_norm(act, T, "a1_n")
            A = chan("a1_proj", None)
            act_empty(act, A, F[0], D, scale=P("a1_g1"), bias=P("a1_b1"), signal="a1_xT")
            act_empty(act, A, F[1], 128, bias=P("a1_bx", 0, 1))
            act_empty(act, A, F[2], 128, bias=P("a1_bx", 1, 2), signal="a1_xm")
            act.wait_ge(S("a1_kmax"), 1)
            for b in range(NB):
                act.activation(F[4][32:64, b * LB:b * LB + L], F[3][32:64, b * LB:b * LB + L], ACT.Exp,
                               bias=ksm[32:64, b:b + 1], accum_out=ksm[32:64, 4 + b:5 + b])
            act.activation(F[4][0:32, :], F[3][0:32, :], ACT.Identity)
            act.drain().then_inc(S("a1_ke"), 1)
            act_softmax(act, qtok.rearrange("p t (h r) -> p (t h) r", r=4), "a1_qs")
            K = chan("a1_kx", None)
            Z = chan("a1_q", None)
            act_empty(act, Z, F[5], 32, signal="a1_qT")
            act_norm(act, T, "a1_m")
            M = chan("a1_mlp", None)
            act_empty(act, M, F[0], D, scale=P("a1_g2"), bias=P("a1_b2"), signal="a1_x2T")
            act_empty(act, M, F[1], 128, func=ACT.Gelu, bias=P("a1_W1b", 0, 1))
            act_empty(act, M, F[2], 128, func=ACT.Gelu, bias=P("a1_W1b", 1, 2), signal="a1_gelu")

        def attn1_dve(dve):
            dve_norm(dve, h[:, :, :], Xs, T, D, 1e-5, "a1_x")
            dve.drain()
            dve_norm(dve, Xs, xn[:, :, :], T, D, 1e-5, "a1_n").then_inc(S("a1_normed"), 1)
            V = chan("a1_xm_tok", None)
            for t in range(T):
                ps, w = V.get()
                dve.wait_ge(V.full, w)
                dve.tensor_tensor(otok[:, t, :], ps[0:P0, 0:256], P("a1_bx_bc"), ALU.add).then_inc(V.free, 1)
            Q = chan("a1_qk", None)
            for c in range(NC):
                ps, w = Q.get()
                dve.wait_ge(Q.full, w)
                dve.tensor_copy(F[3][0:64, cols(c)], ps[0:64, 0:CH]).then_inc(Q.free, 1)
            dve.drain()
            for b in range(NB):
                dve.tensor_reduce(ksm[32:64, 2 + b:3 + b], F[3][32:64, b * LB:b * LB + L], AX.X, ALU.max)
            dve.drain()
            dve.tensor_scalar(ksm[32:64, 0:NB], ksm[32:64, 2:2 + NB], -1.0, None, ALU.mult).then_inc(S("a1_kmax"), 1)
            dve.wait_ge(S("a1_ke"), 1)
            dve.reciprocal(ksm[32:64, 6:6 + NB], ksm[32:64, 4:4 + NB])
            dve.drain()
            for b in range(NB):
                dve.memset(F[4][32:64, b * LB + L:(b + 1) * LB], 0.0)
                ins = dve.tensor_scalar(F[4][32:64, b * LB:b * LB + L], F[4][32:64, b * LB:b * LB + L],
                                        ksm[32:64, 6 + b:7 + b], None, ALU.mult)
            dve.drain().then_inc(S("a1_kexp"), 1)
            G = chan("a1_back", None)
            for b in range(NB):
                ps, w = G.get()
                dve.wait_ge(G.full, w)
                pv = tok(ps, 64)
                dve.tensor_copy(qtok[:, tiles(b), :], pv[:, :, 0:32])
                dve.tensor_copy(ktok[:, tiles(b), :], pv[:, :, 32:64]).then_inc(G.free, 1)
            dve.drain().then_inc(S("a1_ktok"), 1)
            q3 = qtok.rearrange("p t (h r) -> p (t h) r", r=4)
            dve_softmax(dve, q3, q3, T * 8, 4, "a1_qs").then_inc(S("a1_qsoft"), 1)
            K = chan("a1_kx", None)
            U = chan("a1_attn", None)
            for b in range(NB):
                ps, w = K.get()
                dve.wait_ge(K.full, w)
                if b >= 1:
                    dve.drain()
                dve.tensor_tensor(kxm, ps[0:32, 0:256], P("a1_blk"), ALU.mult).then_inc(K.free, 1)
                dve.drain().then_inc(S("a1_kxm"), 1)
                ps, w = K.get()
                dve.wait_ge(K.full, w)
                dve.tensor_copy(kvs.rearrange("p t r -> p (t r)"), ps[:, 0:64]).then_inc(K.free, 1)
                dve.drain().then_inc(S("a1_kvs"), 1)
                ps, w = K.get()
                dve.wait_ge(K.full, w)
                dve.tensor_copy(kvs2.rearrange("p t r -> p (t r)"), ps[:, 0:64]).then_inc(K.free, 1)
                dve.drain().then_inc(S("a1_kvs2"), 1)
                ps, w = K.get()
                dve.wait_ge(K.full, w)
                dve.tensor_copy(Mh, ps[0:32, 0:64]).then_inc(K.free, 1)
                dve.drain().then_inc(S("a1_M"), 1)
                ps, w = U.get()
                dve.wait_ge(U.full, w)
                dve.tensor_tensor(fx[:, tiles(b), :], tok(ps, D), bt(P("a1_bo"), TB), ALU.add).then_inc(U.free, 1)
            dve.drain()
            dve.tensor_tensor(fx[:, :, :], fx[:, :, :], Xs, ALU.add)
            dve.drain()
            dve_norm(dve, fx[:, :, :], xn[:, :, :], T, D, 1e-5, "a1_m").then_inc(S("a1_n2"), 1)
            dve.tensor_tensor(h[:, :, :], h[:, :, :], fx[:, :, :], ALU.add)
            dve.drain()
            dve.tensor_tensor(h[:, :, :], h[:, :, :], bt(P("a1_W2b"), T), ALU.add)
            dve.drain()
            dve_residual(dve, "a1_out")


        def top2_dve(dve, v):
            rev = bt(P("rev"), T)
            cur = v
            for n in range(2):
                m, c = r8[n][:, :], r8[2][:, :]
                dve.tensor_reduce(m, cur, AX.X, ALU.max)
                dve.drain()
                dve.tensor_tensor(eqb[2][:, :, :], cur, bc(m, 8), ALU.is_equal)
                dve.drain()
                dve.tensor_tensor(eqb[2][:, :, :], eqb[2][:, :, :], rev, ALU.mult)
                dve.drain()
                dve.tensor_reduce(c, eqb[2][:, :, :], AX.X, ALU.max)
                dve.drain()
                dve.tensor_tensor(eqb[n][:, :, :], rev, bc(c, 8), ALU.is_equal)
                dve.drain()
                if n == 0:
                    dve.scalar_tensor_tensor(out=eqb[3][:, :, :], in0=eqb[0][:, :, :], scalar=MASKED, in1=v,
                                             op0=ALU.mult, op1=ALU.add)
                    dve.drain()
                    cur = eqb[3][:, :, :]

        def spread_weights_dve(dve, signal):
            dve.memset(W96, 0.0)
            dve.tensor_tensor(eqb[2][:, :, :], eqb[0][:, :, :], bc(r8[3][:, :], 8), ALU.mult)
            dve.tensor_tensor(eqb[3][:, :, :], eqb[1][:, :, :], bc(r8[4][:, :], 8), ALU.mult)
            dve.drain()
            for j in range(3):
                dve.tensor_tensor(W96[:, :, 32 * j:32 * j + 8], eqb[2][:, :, :], eqb[3][:, :, :], ALU.add)
            dve.drain().then_inc(S(signal), 1)

        def split_rows_dve(dve, src, tmp, ready, signal, n=1):
            dve.wait_ge(S(ready), n)
            r = slice(0, 96)
            dve.tensor_copy(Hb[0][r, :], src[r, :])
            dve.drain()
            dve.scalar_tensor_tensor(out=tmp[r, :], in0=Hb[0][r, :], scalar=P("split1"), in1=src[r, :], op0=ALU.mult, op1=ALU.add)
            dve.drain()
            dve.tensor_copy(Hb[1][r, :], tmp[r, :])
            dve.drain()
            dve.scalar_tensor_tensor(out=tmp[r, :], in0=Hb[1][r, :], scalar=P("split2"), in1=tmp[r, :], op0=ALU.mult, op1=ALU.add)
            dve.drain()
            dve.tensor_copy(Hb[2][r, :], tmp[r, :])
            dve.drain().then_inc(S(signal), 1)

        def experts_pe(pe, tag, n, w1, w3, sel, w2, b2):
            CA = chan(f"{tag}_up", singles(0, 2))
            CB = chan(f"{tag}_side", singles(2, 6))
            CY = chan(f"{tag}_y", singles(6, 8))
            for k in range(n * NC + 2):
                if k < n * NC:
                    c, t = divmod(k, n)
                    ps, w = CA.put()
                    if w > 0:
                        pe.wait_ge(CA.free, w)
                    pe.matmul(ps[:, 0:CH], P(w1, t * 128, t * 128 + 128), F[0][0:D, cols(c)], start=True, stop=True).then_inc(CA.full, 1)
                    if w3:
                        ps, w = CB.put()
                        if w > 0:
                            pe.wait_ge(CB.free, w)
                        pe.matmul(ps[:, 0:CH], P(w3, t * 128, t * 128 + 128), F[0][0:D, cols(c)], start=True, stop=True).then_inc(CB.full, 1)
                    ps, w = CB.put()
                    if w > 0:
                        pe.wait_ge(CB.free, w)
                    pe.matmul(ps[:, 0:CH], sel[:, t * 128:(t + 1) * 128], Hb[2][0:96, cols(c)], start=True, stop=True).then_inc(CB.full, 1)
                if k >= 2:
                    i = k - 2
                    c, t = divmod(i, n)
                    if t == 0:
                        y, w = CY.put()
                        if w > 0:
                            pe.wait_ge(CY.free, w)
                    pe.wait_ge(S(f"{tag}_hidden"), i + 1)
                    for j in range(CT):
                        yj = y[0:P0, j * D:(j + 1) * D]
                        ins = pe.matmul(yj, HH[i % 3][:, tcols(j)], P(w2, t * D, t * D + D),
                                        start=(t == 0 and j == 0), stop=True, skip_group_check=True)
                        if b2 and t == n - 1:
                            pe.matmul(yj, F[1][0:8, tcols(c * CT + j)], P(b2), start=False, stop=True, skip_group_check=True)
                    ins.then_inc(S(f"{tag}_hidden_used"), 1)
                    if t == n - 1:
                        pe.drain().then_inc(CY.full, 1)

        def experts_act(act, tag, n, func, bias):
            CA = chan(f"{tag}_up", None)
            for k in range(n * NC):
                ps, w = CA.get()
                act.wait_ge(CA.full, w)
                if k >= 3:
                    act.wait_ge(S(f"{tag}_act_used"), k - 2)
                act.activation(SAr[k % 3], ps[:, 0:CH], func, bias=P(bias, k % n, k % n + 1) if bias else 0.0).then_inc(CA.free, 1)
                act.drain().then_inc(S(f"{tag}_act"), 1)

        def experts_dve(dve, tag, n, gated):
            CB = chan(f"{tag}_side", None)
            CY = chan(f"{tag}_y", None)
            for k in range(n * NC):
                dve.wait_ge(S(f"{tag}_act"), k + 1)
                src = SAr[k % 3]
                if gated:
                    ps, w = CB.get()
                    dve.wait_ge(CB.full, w)
                    dve.tensor_tensor(SAr[k % 3], SAr[k % 3], ps[:, 0:CH], ALU.mult).then_inc(CB.free, 1)
                    dve.drain()
                ps, w = CB.get()
                dve.wait_ge(CB.full, w)
                if k >= 3:
                    dve.wait_ge(S(f"{tag}_hidden_used"), k - 2)
                dve.tensor_tensor(HH[k % 3], SAr[k % 3], ps[:, 0:CH], ALU.mult).then_inc(CB.free, 1)
                dve.drain().then_inc(S(f"{tag}_hidden"), 1)
                dve.sem_inc(S(f"{tag}_act_used"), 1)
                if k % n == n - 1:
                    c = k // n
                    ps, w = CY.get()
                    dve.wait_ge(CY.full, w)
                    ts = slice(c * CT, (c + 1) * CT)
                    dve.tensor_tensor(h[:, ts, :], h[:, ts, :], ps[0:P0, 0:CT * D].rearrange("p (t n) -> p t n", n=D),
                                      ALU.add).then_inc(CY.free, 1)
            dve.drain()

        def ffn1_pe(pe):
            A = chan("f1_proj", singles(0, 2))
            R = chan("f1_rot", pairs(2, 6))
            V = chan("f1_v", singles(6, 8))
            pe.matmul(PS[0:64, 6, 0:128], P("f1_wq_r"), P("rot_q"), start=True, stop=True)
            pe.matmul(PS[0:64, 7, 0:128], P("f1_wk_r"), P("rot_k"), start=True, stop=True).then_inc(S("f1_wrot"), 1)
            pe_turn(pe, A, xn, D, "f1_normed")
            pe.wait_ge(S("f1_xT"), 1)
            pe.wait_ge(S("f1_wr"), 1)
            for plain, rot in ((P("f1_wk"), wrk), (P("f1_wq"), wrq)):
                for c in range(NC):
                    ps, w = R.put()
                    if w > 0:
                        pe.wait_ge(R.free, w)
                    pe.matmul(ps[:, 0, 0:CH], plain, F[0][0:D, cols(c)], start=True, stop=True)
                    pe.matmul(ps[:, 1, 0:CH], rot, F[0][0:D, cols(c)], start=True, stop=True).then_inc(R.full, 1)
            for c in range(NC):
                ps, w = V.put()
                if w > 0:
                    pe.wait_ge(V.free, w)
                for k in range(CT):
                    ins = pe.matmul(ps[0:P0, k * 128:(k + 1) * 128], F[0][0:D, tcols(c * CT + k)], P("f1_wv"), start=True, stop=True)
                ins.then_inc(V.full, 1)
            pe.wait_ge(V.free, V.n_put)
            pe.wait_ge(R.free, R.n_put)
            pe_stack(pe, "f1", 2, lambda s: None)
            pe.wait_ge(S("f1_vtok"), 1)
            attend_pe(pe, "f1", 1)
            pe.wait_ge(S("f1_gathered"), NB)
            G = chan("f1_oback", singles(0, 4))
            for c in range(NC):
                ps, w = G.put()
                if w > 0:
                    pe.wait_ge(G.free, w)
                for k in range(CT):
                    ins = pe.transpose(ps[0:P0, k * 128:(k + 1) * 128], O0[0][:, tcols(c * CT + k)], P("ident"))
                ins.then_inc(G.full, 1)
            H = chan("f1_turn", singles(4, 6))
            pe_turn(pe, H, fx, D, "f1_y")
            pe.wait_ge(S("f1_yT"), 1)
            pe.wait_ge(G.free, G.n_put)
            pe_tokens(pe, chan("f1_wo", singles(0, 2)), [(F[8][0:D, :], P("f1_wo"))], D)
            pe_turn(pe, H, xn, D, "f1_n2")
            pe.wait_ge(S("f1_x2T"), 1)
            pe_tokens(pe, chan("f1_rt", singles(2, 4)), [(F[0][0:D, :], P("f1_rt"))], 8)
            pe_turn(pe, H, W96, 96, "f1_w96")
            pe.wait_ge(S("f1_wsplit"), 1)
            experts_pe(pe, "f1e", KT1, "f1_w1", "f1_w3", selmoe, "f1_w2", None)

        def ffn1_act(act):
            act_norm(act, T, "f1_x")
            act_norm(act, T, "f1_n")
            act.wait_ge(S("f1_wrot"), 1)
            act.activation(wrq, PS[0:64, 6, 0:128], ACT.Identity)
            act.activation(wrk, PS[0:64, 7, 0:128], ACT.Identity)
            act.drain().then_inc(S("f1_wr"), 1)
            A = chan("f1_proj", None)
            act_empty(act, A, F[0], D, scale=P("f1_ln1"), signal="f1_xT")

            def fill(s):
                act.wait_ge(S("f1_rotated"), s + 1)
                if s == 0:
                    act.activation(part_x("f1", 0), part_x("f1", 0), ACT.Identity, scale=0.25)
                    act.drain().then_inc(S("f1_scaled"), 1)

            act_stack(act, "f1", 2, fill)
            attend_act(act, "f1", 1)
            H = chan("f1_turn", None)
            act_empty(act, H, F[8], D, signal="f1_yT")
            act_norm(act, T, "f1_m")
            act_empty(act, H, F[0], D, scale=P("f1_ln2"), signal="f1_x2T")
            act_softmax(act, lg2[:, :, 0:8], "f1_ps")
            act_empty(act, H, F[1], 96, signal="f1_w96T")
            experts_act(act, "f1e", KT1, ACT.Silu, None)

        def ffn1_dve(dve):
            dve_norm(dve, h[:, :, :], Xs, T, D, 1e-5, "f1_x")
            dve.drain()
            dve_norm(dve, Xs, xn[:, :, :], T, D, 1e-6, "f1_n", centre=False).then_inc(S("f1_normed"), 1)
            R = chan("f1_rot", None)
            for s in range(2):
                for c in range(NC):
                    ps, w = R.get()
                    dve.wait_ge(R.full, w)
                    cs = slice((c % 2) * CH, (c % 2 + 1) * CH)
                    dve.tensor_tensor(F[1][:, cols(c)], ps[:, 0, 0:CH], P("cos")[:, cs], ALU.mult)
                    dve.tensor_tensor(F[2][:, cols(c)], ps[:, 1, 0:CH], P("sin")[:, cs], ALU.mult).then_inc(R.free, 1)
                dve.drain()
                dve.tensor_tensor(part_x("f1", s), F[1][:, :], F[2][:, :], ALU.add).then_inc(S("f1_rotated"), 1)
                dve.drain()
            V = chan("f1_v", None)
            for c in range(NC):
                ps, w = V.get()
                dve.wait_ge(V.full, w)
                dve.tensor_tensor(vtok[:, c * CT:(c + 1) * CT, :], ps[0:P0, 0:CT * 128].rearrange("p (t n) -> p t n", n=128),
                                  bt(P("ones_col"), CT), ALU.add).then_inc(V.free, 1)
            dve.drain().then_inc(S("f1_vtok"), 1)
            dve.wait_ge(S("f1_scaled"), 1)
            dve_stack(dve, "f1", 2)
            attend_dve(dve, "f1", O0, 1)
            G = chan("f1_oback", None)
            for c in range(NC):
                ps, w = G.get()
                dve.wait_ge(G.full, w)
                pv = ps[0:P0, 0:CT * 128].rearrange("p (t n d) -> p t n d", n=NH, d=32)
                ts = slice(c * CT, (c + 1) * CT)
                dve.reciprocal(rl[:, ts, :], pv[:, :, :, HD])
                dve.drain()
                dve.tensor_tensor(fx[:, ts, :].rearrange("p t (n d) -> p t n d", n=NH), pv[:, :, :, 0:HD],
                                  bc(rl[:, ts, :], HD), ALU.mult).then_inc(G.free, 1)
            dve.drain().then_inc(S("f1_y"), 1)
            Y = chan("f1_wo", None)
            for b in range(NB):
                ps, w = Y.get()
                dve.wait_ge(Y.full, w)
                dve.tensor_tensor(X[:, tiles(b), 0:D], X[:, tiles(b), 0:D], tok(ps, D), ALU.add).then_inc(Y.free, 1)
            dve.drain()
            dve_norm(dve, Xs, xn[:, :, :], T, D, 1e-6, "f1_m", centre=False).then_inc(S("f1_n2"), 1)
            dve.tensor_tensor(h[:, :, :], h[:, :, :], Xs, ALU.add)
            Y = chan("f1_rt", None)
            for b in range(NB):
                ps, w = Y.get()
                dve.wait_ge(Y.full, w)
                dve.tensor_copy(lg[:, tiles(b), 0:8], tok(ps, 8)).then_inc(Y.free, 1)
            dve.drain()
            pr = lg2[:, :, 0:8]
            dve_softmax(dve, lg[:, :, 0:8], pr, T, 8, "f1_ps")
            dve.drain()
            top2_dve(dve, pr)
            dve.tensor_tensor(r8[2][:, :], r8[0][:, :], r8[1][:, :], ALU.add)
            dve.drain()
            dve.tensor_scalar(r8[2][:, :], r8[2][:, :], 1e-9, None, ALU.add)
            dve.drain()
            dve.reciprocal(r8[5][:, :], r8[2][:, :])
            dve.drain()
            dve.tensor_tensor(r8[3][:, :], r8[0][:, :], r8[5][:, :], ALU.mult)
            dve.tensor_tensor(r8[4][:, :], r8[1][:, :], r8[5][:, :], ALU.mult)
            dve.drain()
            spread_weights_dve(dve, "f1_w96")
            split_rows_dve(dve, F[1], F[2], "f1_w96T", "f1_wsplit")
            experts_dve(dve, "f1e", KT1, True)


        def attn2_pe(pe):
            A = chan("a2_proj", singles(0, 2))
            pe_turn(pe, A, X, D, "a2_normed")
            pe.wait_ge(S("a2_xT"), 1)
            pe_project(pe, A, P("a2_q"), F[0][0:D, :], 65)
            pe_project(pe, A, P("a2_k"), F[0][0:D, :], D)
            pe.wait_ge(S("a2_qk"), 1)
            SA = chan("a2_score", pairs(2, 8))
            for t in range(T):
                o = t // TB * LB
                ps, w = SA.put()
                if w > 0:
                    pe.wait_ge(SA.free, w)
                for m, ko in enumerate((0, L - CH)):
                    ins = pe.matmul(ps[0:P0, m, 0:CH], F[1][0:D, tcols(t)], F[2][0:D, o + ko:o + ko + CH], start=True, stop=True)
                ins.then_inc(SA.full, 1)
            pe.wait_ge(S("a2_maxima"), 1)
            for c in range(NC):
                ps, w = A.put()
                if w > 0:
                    pe.wait_ge(A.free, w)
                pe.matmul(ps[0:65, 0:CH], P("a2_q"), F[0][0:D, cols(c)], start=True, stop=True)
                for k in range(CT):
                    ins = pe.matmul(ps[0:65, tcols(k)], W96[:, c * CT + k, 0:65], P("ident")[0:P0, 0:P0], start=False, stop=True,
                                    skip_group_check=True)
                ins.then_inc(A.full, 1)
            pe.wait_ge(S("a2_qmaxed"), 1)
            pe.wait_ge(SA.free, SA.n_put)
            SB = chan("a2_scoreT", pairs(2, 8))
            OC = chan("a2_o", singles(0, 2))
            units = [(c, p) for c in range(NC) for p in range(3)]
            for u in range(len(units) + 2):
                if u < len(units):
                    c, p = units[u]
                    o = c // 2 * LB
                    ps, w = SB.put()
                    if w > 0:
                        pe.wait_ge(SB.free, w)
                    for m in range(2):
                        j = 2 * p + m
                        ins = pe.matmul(ps[0:P0, m, 0:CH], F[2][0:65, o + j * P0:o + (j + 1) * P0], F[1][0:65, cols(c)],
                                        start=True, stop=True)
                    ins.then_inc(SB.full, 1)
                if u >= 2:
                    i = u - 2
                    c, p = units[i]
                    if p == 0:
                        ob, w = OC.put()
                        if w > 0:
                            pe.wait_ge(OC.free, w)
                    pe.wait_ge(S("a2_probs"), i + 1)
                    for m in range(2):
                        j = 2 * p + m
                        kn = P0 if j < TB - 1 else L - (TB - 1) * P0
                        ins = pe.matmul(ob[0:65, 0:CH], X[0:kn, c // 2 * TB + j, :], PT[i % 3][0:kn, m, :],
                                        start=(j == 0), stop=(j == TB - 1))
                    ins.then_inc(S("a2_probs_used"), 1)
                    if p == 2:
                        pe.drain().then_inc(OC.full, 1)
            pe.wait_ge(S("a2_gathered"), 1)
            pe_back(pe, chan("a2_back", singles(0, 2)), F[3], 65, 65, "a2_gathered")

        def attn2_act(act):
            act_norm(act, T, "a2")
            A = chan("a2_proj", None)
            act_empty(act, A, F[0], D, signal="a2_xT")
            act_empty(act, A, F[1], 65)
            act_empty(act, A, F[2], D, scale=0.125, signal="a2_qk")
            act_empty(act, A, F[1], 65, signal="a2_qmaxed")
            SB = chan("a2_scoreT", None)
            for k in range(3 * NC):
                ps, w = SB.get()
                act.wait_ge(SB.full, w)
                if k >= 3:
                    act.wait_ge(S("a2_probs_used"), k - 2)
                act.activation(PT[k % 3], ps[0:P0, :, 0:CH], ACT.Exp).then_inc(SB.free, 1)
                act.drain().then_inc(S("a2_probs"), 1)

        def attn2_dve(dve):
            dve.memset(W96, 0.0)
            dve.memset(F[2][64:65, :], 1.0)
            dve_norm(dve, h[:, :, :], Xs, T, D, 1e-5, "a2")
            dve.drain().then_inc(S("a2_normed"), 1)
            SA = chan("a2_score", None)
            for t in range(T):
                ps, w = SA.get()
                dve.wait_ge(SA.full, w)
                dve.tensor_reduce(r8[0][:, t:t + 1], ps[0:P0, :, 0:CH], AX.XY, ALU.max).then_inc(SA.free, 1)
            dve.drain()
            dve.tensor_scalar(W96[:, :, 64], r8[0][:, :], -1.0, None, ALU.mult).then_inc(S("a2_maxima"), 1)
            OC = chan("a2_o", None)
            for c in range(NC):
                ps, w = OC.get()
                dve.wait_ge(OC.full, w)
                dve.tensor_copy(F[3][0:65, cols(c)], ps[0:65, 0:CH]).then_inc(OC.free, 1)
            dve.drain().then_inc(S("a2_gathered"), 1)
            G = chan("a2_back", None)
            for b in range(NB):
                ps, w = G.get()
                dve.wait_ge(G.full, w)
                pv = tok(ps, 65)
                dve.reciprocal(r8[1][:, tiles(b)], pv[:, :, 64])
                dve.drain()
                dve.tensor_tensor(fx[:, tiles(b), :], pv[:, :, 0:64], bc(r8[1][:, tiles(b)], D), ALU.mult).then_inc(G.free, 1)
            dve.drain()
            dve.tensor_tensor(h[:, :, :], h[:, :, :], fx[:, :, :], ALU.add)
            dve.drain()


        def ffn2_pe(pe):
            A = chan("f2_turn", singles(0, 2))
            pe_turn(pe, A, X, D, "f2_normed")
            pe.wait_ge(S("f2_xT"), 1)
            V = chan("f2_logit", singles(2, 4))
            for t in range(T):
                ps, w = V.put()
                if w > 0:
                    pe.wait_ge(V.free, w)
                pe.matmul(ps[0:P0, 0:256], F[0][0:D, tcols(t)], P("f2_w1"), start=True, stop=True).then_inc(V.full, 1)
            pe_turn(pe, A, Ag[:, :, 0:128], 128, "f2_weights")
            pe_turn(pe, A, Ag[:, :, 128:256], 128, None)
            pe.wait_ge(S("f2_aT"), 1)
            pe.wait_ge(V.free, V.n_put)
            pe_tokens(pe, chan("f2_b2", singles(0, 2)), [(F[1], P("f2_b2", 0, 64)), (F[2], P("f2_b2", 64, 128))], D)
            pe.wait_ge(w2_in, 32)
            M = chan("f2_matrix", singles(2, 8))
            for t in range(T):
                for m in range(8):
                    ps, w = M.put()
                    if w > 0:
                        pe.wait_ge(M.free, w)
                    pe.matmul(ps[0:P0, :], F[1][:, tcols(t)], W2N[:, 0, 512 * m:512 * m + 512], start=True, stop=False)
                    pe.matmul(ps[0:P0, :], F[2][0:127, tcols(t)], W2N[0:127, 1, 512 * m:512 * m + 512],
                              start=False, stop=True).then_inc(M.full, 1)

        def ffn2_act(act):
            act_norm(act, T, "f2")
            A = chan("f2_turn", None)
            act_empty(act, A, F[0], D, signal="f2_xT")
            act.wait_ge(S("f2_path"), 1)
            act.activation(Lg[:, :, :], Lg[:, :, :], ACT.Abs)
            act.drain()
            act.activation(Lg[:, :, :], Lg[:, :, :], ACT.Gelu).then_inc(S("f2_gelu"), 1)
            act_empty(act, A, F[1], 128)
            act_empty(act, A, F[2], 128, signal="f2_aT")

        def ffn2_dve(dve):
            dve_norm(dve, h[:, :, :], Xs, T, D, 1e-5, "f2").then_inc(S("f2_normed"), 1)
            dve.memset(Ag[:, :, 0:1], 1.0)
            dve.memset(Ag[:, :, 255:256], 0.0)
            V = chan("f2_logit", None)
            for t in range(T):
                ps, w = V.get()
                dve.wait_ge(V.full, w)
                dve.tensor_tensor(Lg[:, t, :], ps[0:P0, 0:256], P("f2_b1"), ALU.add).then_inc(V.free, 1)
            dve.drain()
            for lv in range(7):
                s, n = 2 ** lv - 1, 2 ** lv
                c0 = 2 * n - 1
                left, right = Ag[:, :, c0:c0 + 2 * n:2], Ag[:, :, c0 + 1:c0 + 2 * n:2]
                dve.scalar_tensor_tensor(out=right, in0=Lg[:, :, s:s + n], scalar=0.0, in1=Ag[:, :, s:s + n],
                                         op0=ALU.is_gt, op1=ALU.mult)
                dve.drain()
                dve.tensor_tensor(left, Ag[:, :, s:s + n], right, ALU.subtract)
                dve.drain()
            dve.sem_inc(S("f2_path"), 1)
            dve.wait_ge(S("f2_gelu"), 1)
            dve.tensor_tensor(Ag[:, :, :], Ag[:, :, :], Lg[:, :, :], ALU.mult).then_inc(S("f2_weights"), 1)
            dve_residual(dve, "f2_b2")
            M = chan("f2_matrix", None)
            for t in range(T):
                pv = prod[t % 2].rearrange("p (d o) -> p d o", o=D)
                if t >= 2:
                    dve.wait_ge(S("f2_summed"), t - 1)
                for m in range(8):
                    ps, w = M.get()
                    dve.wait_ge(M.full, w)
                    ins = dve.tensor_tensor(pv[:, 8 * m:8 * m + 8, :], ps[0:P0, :].rearrange("p (d o) -> p d o", o=D),
                                            bc(X[:, t, 8 * m:8 * m + 8], D), ALU.mult).then_inc(M.free, 1)
                dve.drain().then_inc(S("f2_prod"), 1)
            dve.wait_ge(S("f2_summed"), T)
            dve.tensor_tensor(h[:, :, :], h[:, :, :], xn[:, :, :], ALU.add)
            dve.drain()

        def ffn2_pool(pool):
            for t in range(T):
                pool.wait_ge(S("f2_prod"), t + 1)
                n = 2048
                while n > D:
                    pool.tensor_tensor(prod[t % 2][:, 0:n], prod[t % 2][:, 0:n], prod[t % 2][:, n:2 * n], ALU.add)
                    pool.drain()
                    n //= 2
                pool.tensor_tensor(xn[:, t, :], prod[t % 2][:, 0:D], prod[t % 2][:, D:2 * D], ALU.add)\
                    .then_inc(S("f2_summed"), 1)

        A3 = dict(x=F[0], sz=F[1], t=F[2], u=F[3], dl=F[4], y=[F[5], F[8]], a=F[6], delta=F[7], tmp=F[8], bc=F[9], dx=F[10])

        def scan3_pe(pe):
            A = chan("a3_proj", singles(0, 4))
            pe_turn(pe, A, xn, D, "a3_normed")
            pe.wait_ge(S("a3_xT"), 1)
            for di, dn in enumerate("fb"):
                w3 = f"a3{dn}_"
                pe_project(pe, A, P(w3 + "in", 0, 128), A3["x"][0:D, :], 128)
                pe_project(pe, A, P(w3 + "in", 128, 256), A3["x"][0:D, :], 128)
                pe.wait_ge(S("a3_u"), di + 1)
                pe_project(pe, A, P(w3 + "dl"), A3["u"], 4)
                pe_project(pe, A, P(w3 + "bc"), A3["u"], 96)
                pe.wait_ge(S("a3_dl"), di + 1)
                pe_project(pe, A, P(w3 + "dt"), A3["dl"][0:4, :], 128)
                pe.wait_ge(S("a3_split"), di + 1)
                pe.wait_ge(A.free, A.n_put)
                R = chan(f"a3{dn}_rep", pairs(0, 6))
                Y = chan(f"a3{dn}_sum", pairs(6, 8))
                n = DS * NB
                for k in range(n + 4):
                    for i, o in ((k, 0), (k - 2, 16)):
                        if 0 <= i < n:
                            b, g = divmod(i, DS)
                            ps, w = R.put()
                            if w > 0:
                                pe.wait_ge(R.free, w)
                            for c in range(2):
                                ins = pe.matmul(ps[:, c, 0:CH], selbn[:, (g + o) * 128:(g + o + 1) * 128],
                                                Hb[2][0:96, cols(2 * b + c)], start=True, stop=True)
                            ins.then_inc(R.full, 1)
                    if k >= 4:
                        i = k - 4
                        if i % DS == 0:
                            y, w = Y.put()
                            if w > 0:
                                pe.wait_ge(Y.free, w)
                        pe.wait_ge(S(f"a3{dn}_read"), i + 1)
                        for c in range(2):
                            ins = pe.matmul(y[:, c, 0:CH], P("ident"), RC[i % 2][:, cols(c)],
                                            start=(i % DS == 0), stop=(i % DS == DS - 1))
                        ins.then_inc(S(f"a3{dn}_summed"), 1)
                        if i % DS == DS - 1:
                            pe.drain().then_inc(Y.full, 1)
            pe.wait_ge(S("a3_y"), 2)
            O = chan("a3_fold", singles(0, 4))
            for c in range(NC):
                ps, w = O.put()
                if w > 0:
                    pe.wait_ge(O.free, w)
                pe.matmul(ps[0:64, 0:CH], P("a3f_out"), A3["y"][0][:, cols(c)], start=True, stop=True)
                pe.matmul(ps[64:128, 0:CH], P("a3b_out"), A3["y"][1][:, cols(c)], start=True, stop=True).then_inc(O.full, 1)
            pe.wait_ge(S("a3_folded"), 1)
            pe_tokens(pe, chan("a3_out", singles(4, 6)), [(F[9], P("a3_fus"))], D)

        def scan3_act(act):
            act_norm(act, T, "a3_x")
            act_norm(act, T, "a3_n")
            A = chan("a3_proj", None)
            act_empty(act, A, A3["x"], D, scale=P("a3_g"), bias=P("a3_b"), signal="a3_xT")
            for di, dn in enumerate("fb"):
                w3 = f"a3{dn}_"
                if di == 1:
                    act.wait_ge(S("a3_y"), 1)
                act.wait_ge(S("a3_bordered"), 1)
                for c in range(NC):
                    ps, w = A.get()
                    act.wait_ge(A.full, w)
                    n = CH if c % 2 == 0 else CH - 1
                    o = 3 + (c % 2) * CH
                    act.activation(xsp[:, c // 2, o:o + n], ps[:, 0:n], ACT.Identity).then_inc(A.free, 1)
                act.drain().then_inc(S("a3_xs"), 1)
                act_empty(act, A, A3["sz"], 128, func=ACT.Silu)
                act.wait_ge(S("a3_conv"), di + 1)
                act.activation(A3["u"][:, :], A3["t"][:, :], ACT.Silu, bias=P(w3 + "cb")).then_inc(S("a3_u"), 1)
                act_empty(act, A, A3["dl"], 4, signal="a3_dl")
                act_empty(act, A, A3["bc"], 96, signal="a3_bc")
                act_empty(act, A, A3["t"], 128, bias=P(w3 + "dtb"))
                act.drain()
                softplus_act(act, A3["t"][:, :], A3["a"][:, :], A3["delta"][:, :], f"a3{dn}_ln")
                act.wait_ge(S("a3_delta"), di + 1)
                for k in range(DS * NB):
                    b, g = divmod(k, DS)
                    if k >= 2:
                        act.wait_ge(S(f"a3{dn}_scanned"), k - 1)
                    act.activation(RA[k % 2][:, 0:L], A3["delta"][:, b * LB:b * LB + L], ACT.Exp,
                                   scale=nA3[:, di, g:g + 1]).then_inc(S(f"a3{dn}_decay"), 1)
            O = chan("a3_fold", None)
            act_empty(act, O, F[9], 128, signal="a3_folded")

        def scan3_dve(dve):
            dve_norm(dve, h[:, :, :], Xs, T, D, 1e-5, "a3_x")
            dve.drain()
            dve_norm(dve, Xs, xn[:, :, :], T, D, 1e-5, "a3_n").then_inc(S("a3_normed"), 1)
            dve.memset(xsp[:, :, 0:3], 0.0)
            dve.memset(xsp[:, :, 3 + L:LB + 6], 0.0)
            for z in RS:
                dve.memset(z[:, L:LB], 0.0)
            dve.drain().then_inc(S("a3_bordered"), 1)
            for di, dn in enumerate("fb"):
                w3 = f"a3{dn}_"
                v2 = lambda z: z.rearrange("p (b n) -> p b n", b=NB)
                dve.wait_ge(S("a3_xs"), di + 1)
                for j in range(4):
                    o = j if di == 0 else 6 - j
                    src = xsp[:, :, o:o + LB]
                    if j == 0:
                        dve.tensor_scalar(v2(A3["t"][:, :]), src, P(w3 + "cw", 0, 1), None, ALU.mult)
                    else:
                        dve.scalar_tensor_tensor(out=v2(A3["t"][:, :]), in0=src, scalar=P(w3 + "cw", j, j + 1),
                                                 in1=v2(A3["t"][:, :]), op0=ALU.mult, op1=ALU.add)
                    dve.drain()
                dve.sem_inc(S("a3_conv"), 1)
                split_rows_dve(dve, A3["bc"], A3["tmp"], "a3_bc", "a3_split", di + 1)
                softplus_dve(dve, A3["t"][:, :], A3["a"][:, :], A3["delta"][:, :], A3["dx"][:, :], mask8[:, :],
                             f"a3{dn}_ln").then_inc(S("a3_delta"), 1)
                dve.drain()
                dve.tensor_tensor(A3["dx"][:, :], A3["delta"][:, :], A3["u"][:, :], ALU.mult)
                dve.drain()
                R = chan(f"a3{dn}_rep", None)
                Y = chan(f"a3{dn}_sum", None)
                n = DS * NB
                fl = (lambda z: z[:, 0:L]) if di == 0 else (lambda z: z[:, L - 1::-1])
                for k in range(n + 2):
                    if k < n:
                        b = k // DS
                        ps, w = R.get()
                        dve.wait_ge(R.full, w)
                        dve.tensor_tensor(RB[k % 2].rearrange("p (c n) -> p c n", c=2), ps[:, :, 0:CH],
                                          A3["dx"][:, b * LB:(b + 1) * LB].rearrange("p (c n) -> p c n", c=2),
                                          ALU.mult).then_inc(R.free, 1)
                    if 1 <= k <= n:
                        i = k - 1
                        dve.wait_ge(S(f"a3{dn}_decay"), i + 1)
                        dve.tensor_tensor_scan(fl(RS[i % 2]), fl(RA[i % 2]), fl(RB[i % 2]), 0.0, ALU.mult,
                                               ALU.add).then_inc(S(f"a3{dn}_scanned"), 1)
                    if k >= 2:
                        i = k - 2
                        ps, w = R.get()
                        dve.wait_ge(R.full, w)
                        if i >= 2:
                            dve.wait_ge(S(f"a3{dn}_summed"), i - 1)
                        dve.tensor_tensor(RC[i % 2].rearrange("p (c n) -> p c n", c=2),
                                          RS[i % 2].rearrange("p (c n) -> p c n", c=2), ps[:, :, 0:CH],
                                          ALU.mult).then_inc(R.free, 1)
                        dve.drain().then_inc(S(f"a3{dn}_read"), 1)
                    else:
                        dve.drain()
                    if k >= 2 and (k - 2) % DS == DS - 1:
                        b = (k - 2) // DS
                        ps, w = Y.get()
                        cs = slice(b * LB, (b + 1) * LB)
                        y = A3["y"][di]
                        dve.wait_ge(Y.full, w)
                        v = lambda z: z[:, cs].rearrange("p (c n) -> p c n", c=2)
                        dve.scalar_tensor_tensor(out=v(y), in0=v(A3["u"]), scalar=P(w3 + "Dp"), in1=ps[:, :, 0:CH],
                                                 op0=ALU.mult, op1=ALU.add).then_inc(Y.free, 1)
                        dve.drain()
                        dve.tensor_tensor(y[:, cs], y[:, cs], A3["sz"][:, cs], ALU.mult)
                dve.drain().then_inc(S("a3_y"), 1)
            dve.tensor_tensor(h[:, :, :], h[:, :, :], Xs, ALU.add)
            dve.drain()
            dve.tensor_tensor(h[:, :, :], h[:, :, :], bt(P("a3_fusb"), T), ALU.add)
            dve.drain()
            dve_residual(dve, "a3_out")


        def ffn3_pe(pe):
            A = chan("f3_turn", singles(0, 2))
            pe_turn(pe, A, xn, D, "f3_normed")
            pe.wait_ge(S("f3_xT"), 1)
            pe_tokens(pe, chan("f3_rt", singles(2, 4)), [(F[0][0:D, :], P("f3_rt"))], 8)
            pe_turn(pe, A, W96, 96, "f3_w96")
            pe.wait_ge(S("f3_wsplit"), 1)
            experts_pe(pe, "f3e", NE, "f3_w1", None, selbn, "f3_w2", "f3_b2")

        def ffn3_act(act):
            act_norm(act, T, "f3_x")
            act_norm(act, T, "f3_n")
            A = chan("f3_turn", None)
            act_empty(act, A, F[0], D, scale=P("f3_g"), bias=P("f3_b"), signal="f3_xT")
            act.wait_ge(S("f3_gap"), 1)
            act.activation(r8[2][:, :], r8[2][:, :], ACT.Exp).then_inc(S("f3_gapexp"), 1)
            act_empty(act, A, F[1], 96, signal="f3_w96T")
            experts_act(act, "f3e", NE, ACT.Gelu, "f3_b1")

        def ffn3_dve(dve):
            dve_norm(dve, h[:, :, :], Xs, T, D, 1e-5, "f3_x")
            dve.drain()
            dve_norm(dve, Xs, xn[:, :, :], T, D, 1e-5, "f3_n").then_inc(S("f3_normed"), 1)
            Y = chan("f3_rt", None)
            for b in range(NB):
                ps, w = Y.get()
                dve.wait_ge(Y.full, w)
                dve.tensor_tensor(lg[:, tiles(b), 0:8], tok(ps, 8), bt(P("f3_rtb"), TB), ALU.add).then_inc(Y.free, 1)
            dve.drain()
            top2_dve(dve, lg[:, :, 0:8])
            dve.tensor_tensor(r8[2][:, :], r8[1][:, :], r8[0][:, :], ALU.subtract).then_inc(S("f3_gap"), 1)
            dve.wait_ge(S("f3_gapexp"), 1)
            dve.tensor_scalar(r8[5][:, :], r8[2][:, :], 1.0, None, ALU.add)
            dve.drain()
            dve.reciprocal(r8[3][:, :], r8[5][:, :])
            dve.drain()
            dve.tensor_tensor(r8[4][:, :], r8[2][:, :], r8[3][:, :], ALU.mult)
            dve.drain()
            spread_weights_dve(dve, "f3_w96")
            split_rows_dve(dve, F[1], F[2], "f3_w96T", "f3_wsplit")
            experts_dve(dve, "f3e", NE, False)

        block = ctx.enter_context(nc.Block())

        def part_over(e, at):
            e.drain().then_inc(arrive, 1)
            e.wait_ge(go, at)

        @block.tensor
        def _(pe):
            pe.wait_ge(weights_in, 16 * (WCH + 2))
            pe.wait_ge(consts_ready, 1)
            with pe.Fori(0, NIT) as it:
                conv_pe(pe)
                scan0_pe(pe)
                sx_pe(pe)
                part_over(pe, it + 1)
            with pe.Fori(0, NIT) as it:
                ffn0_pe(pe)
                attn1_pe(pe)
                part_over(pe, it + (NIT + 1))
            with pe.Fori(0, NIT) as it:
                ffn1_pe(pe)
                part_over(pe, it + (2 * NIT + 1))
            with pe.Fori(0, NIT) as it:
                attn2_pe(pe)
                ffn2_pe(pe)
                part_over(pe, it + (3 * NIT + 1))
            with pe.Fori(0, NIT) as it:
                scan3_pe(pe)
                ffn3_pe(pe)
                part_over(pe, it + (4 * NIT + 1))

        @block.scalar
        def _(act):
            act.wait_ge(weights_in, 16 * (WCH + 2))
            act.activation(nA0[:, :], P("a0_Alog"), ACT.Exp)
            act.activation(nA3[:, 0, :], P("a3f_Alog"), ACT.Exp)
            act.activation(nA3[:, 1, :], P("a3b_Alog"), ACT.Exp)
            act.drain().then_inc(S("A_exp"), 1)
            act.wait_ge(consts_ready, 1)
            with act.Fori(0, NIT) as it:
                conv_act(act)
                scan0_act(act)
                sx_act(act)
                part_over(act, it + 1)
            with act.Fori(0, NIT) as it:
                ffn0_act(act)
                attn1_act(act)
                part_over(act, it + (NIT + 1))
            with act.Fori(0, NIT) as it:
                ffn1_act(act)
                part_over(act, it + (2 * NIT + 1))
            with act.Fori(0, NIT) as it:
                attn2_act(act)
                ffn2_act(act)
                part_over(act, it + (3 * NIT + 1))
            with act.Fori(0, NIT) as it:
                scan3_act(act)
                ffn3_act(act)
                part_over(act, it + (4 * NIT + 1))

        @block.vector
        def _(dve):
            dve.memset(X[:, :, D:D + 1], 1.0)
            dve.wait_ge(weights_in, 16 * (WCH + 2))
            dve.tensor_copy(identb[:, :], P("ident"))
            dve.tensor_copy(maskqk[:, :], P("mask_qk"))
            dve.tensor_copy(maskkq[:, :], P("mask_kq"))
            dve.tensor_copy(selrep[:, :], W2N[:, 0, 0:512])
            dve.tensor_copy(selbn[:, :], W2N[0:96, 1, :])
            dve.tensor_copy(selmoe[:, :], W2N[0:96, 0, 512:512 + KT1 * 128])
            dve.wait_ge(S("A_exp"), 1)
            dve.tensor_scalar(nA0[:, :], nA0[:, :], -1.0, None, ALU.mult)
            dve.tensor_scalar(nA3[:, :, :], nA3[:, :, :], -1.0, None, ALU.mult)
            dve.drain().then_inc(consts_ready, 1)
            with dve.Fori(0, NIT) as it:
                conv_dve(dve)
                scan0_dve(dve)
                sx_dve(dve, it)
                part_over(dve, it + 1)
            with dve.Fori(0, NIT) as it:
                dve.tensor_copy(h[:, :, :], h_all[:, bass.ds(it * T, T), :])
                dve.drain()
                ffn0_dve(dve, it)
                attn1_dve(dve)
                dve.tensor_copy(h_all[:, bass.ds(it * T, T), :], h[:, :, :])
                part_over(dve, it + (NIT + 1))
            with dve.Fori(0, NIT) as it:
                dve.tensor_copy(h[:, :, :], h_all[:, bass.ds(it * T, T), :])
                dve.drain()
                ffn1_dve(dve)
                dve.tensor_copy(h_all[:, bass.ds(it * T, T), :], h[:, :, :])
                part_over(dve, it + (2 * NIT + 1))
            with dve.Fori(0, NIT) as it:
                dve.tensor_copy(h[:, :, :], h_all[:, bass.ds(it * T, T), :])
                dve.drain()
                attn2_dve(dve)
                ffn2_dve(dve)
                dve.tensor_copy(h_all[:, bass.ds(it * T, T), :], h[:, :, :])
                part_over(dve, it + (3 * NIT + 1))
            with dve.Fori(0, NIT) as it:
                dve.tensor_copy(h[:, :, :], h_all[:, bass.ds(it * T, T), :])
                dve.drain()
                scan3_dve(dve)
                ffn3_dve(dve)
                dve.drain().then_inc(S("h_done"), 1)
                part_over(dve, it + (4 * NIT + 1))

        @block.gpsimd
        def _(pool):
            with pool.Fori(0, NIT) as it:
                part_over(pool, it + 1)
            with pool.Fori(0, NIT) as it:
                part_over(pool, it + (NIT + 1))
            with pool.Fori(0, NIT) as it:
                part_over(pool, it + (2 * NIT + 1))
            with pool.Fori(0, NIT) as it:
                ffn2_pool(pool)
                part_over(pool, it + (3 * NIT + 1))
            with pool.Fori(0, NIT) as it:
                part_over(pool, it + (4 * NIT + 1))

        @block.sync
        def _(sp):
            step = -(-WCOLS // WCH)
            for i in range(WCH):
                a, b = i * step, min(WCOLS, (i + 1) * step)
                sp.dma_start(WP[:, a:b], pack[:, a:b]).then_inc(weights_in, 16)
            sp.dma_start(W2N[:, 1, :], selectors[:, 0:4096]).then_inc(weights_in, 16)
            sp.dma_start(W2N[:, 0, 0:(4 + KT1) * 128], selectors[:, 4096:(36 + KT1) * 128]).then_inc(weights_in, 16)
            sp.wait_ge(consts_ready, 1)
            sp.dma_start(W2N[:, 0, :], w2s[0:128, :]).then_inc(w2_in, 16)
            sp.dma_start(W2N[0:127, 1, :], w2s[128:NODES, :]).then_inc(w2_in, 16)
            S("x_in"), S("out_done")
            counted = pool_of_sems + [arrive]

            def iteration_end(engines):
                sp.wait_ge(arrive, engines)
                nums = sorted({s.num for s in counted})
                runs = []
                for n in nums:
                    if runs and runs[-1][1] == n:
                        runs[-1][1] = n + 1
                    else:
                        runs.append([n, n + 1])
                for a, b in runs:
                    sp.sem_clear(range(a, b))
                sp.drain().then_inc(go, 1)

            with sp.Fori(0, NIT) as it:
                conv_sp(sp, it)
                iteration_end(4)
            with sp.Fori(0, NIT):
                attend_sp(sp, "f0", E0)
                iteration_end(4)
            with sp.Fori(0, NIT):
                attend_sp(sp, "f1", 1)
                iteration_end(4)
            with sp.Fori(0, NIT):
                iteration_end(4)
            with sp.Fori(0, NIT) as it:
                sp.wait_ge(S("h_done"), 1)
                for b in range(NB):
                    dst = out[bass.ds(it * NB + b, 1), :, :]
                    sp.dma_start(dst[:, 0:LB - P0, :].rearrange("b (j p) f -> p (b j) f", p=P0),
                                 h[:, b * TB:b * TB + TB - 1, :]).then_inc(S("out_done"), 16)
                    sp.dma_start(dst[:, LB - P0:L, :].rearrange("b p f -> p b f"),
                                 h[0:L - (LB - P0), b * TB + TB - 1:(b + 1) * TB, :]).then_inc(S("out_done"), 16)
                sp.wait_ge(S("out_done"), 32 * NB)
                iteration_end(4)
            sp.wait_ge(w2_in, 32)


WCH = 4


def selector_bits():
    a = np.zeros((128, 36 + KT1, 128), np.float32)
    k = np.arange(128)
    for n in range(32):
        a[n:96:32, n, :] = 1
    for q in range(4):
        for r in range(4):
            a[32 * q + 8 * r + k // 16, 32 + r, k] = 1
    e = np.arange(KT1 * 128) // HID
    for j in range(3):
        a[32 * j:32 * j + 8, 36:, :] = (np.arange(8)[:, None] == e).reshape(8, KT1, 128)
    return a.reshape(128, -1)


def pack_weights(i):
    a = np.zeros((128, WCOLS), np.float32)

    def put(name, v):
        r, o, c = OFF[name]
        v = np.asarray(v)
        if v.ndim == 1:
            v = v[:, None]
        assert v.shape == (r, c), (name, v.shape, (r, c))
        a[0:r, o:o + c] = v

    def row(v, n=P0):
        return np.broadcast_to(np.asarray(v)[None, :], (n, len(v)))

    k = np.arange(128)
    put("ident", np.eye(128))
    m = np.where(np.arange(P0)[None, :] > np.arange(P0)[:, None], MASKED, 0.0)
    put("mask_qk", m)
    put("mask_kq", m.T)
    sums = np.zeros((128, 4, 32))
    for r in range(4):
        sums[k, r, 8 * r + k // 16] = 1
    put("sel_sum", sums.reshape(128, -1))
    put("split1", (np.arange(96) >= 32) * -1.0)
    put("split2", (np.arange(96) >= 64) * -1.0)
    put("tok_w", i["L0_tok_weight"].reshape(8, 64, 64).transpose(1, 0, 2).reshape(64, 512))
    put("tok_b", row(i["L0_tok_bias"][0]))
    put("a0_xp", i["L0_attn_x_proj"])
    for n, s in (("a0_dt", "dt_proj"), ("a0_B", "B_proj"), ("a0_C", "C_proj")):
        put(n, np.tile(i["L0_attn_" + s], (1, 8)))
    put("a0_dtb", np.tile(i["L0_attn_dt_proj_bias"], 8))
    put("a0_Alog", i["L0_attn_A_log"].reshape(16, 8, 16).transpose(1, 2, 0).reshape(128, 16))
    put("a0_D", i["L0_attn_D"])
    put("a0_out", i["L0_attn_out_proj"])

    hl = i["L0_ffn_hl_w"]
    put("f0_hl", hl.reshape(64, 64).T)
    put("f0_hlb", i["L0_ffn_hl_b"].reshape(64))
    put("f0_hlb_bc", row(i["L0_ffn_hl_b"].reshape(64)))
    wq = np.zeros((64, 4, 128), np.float32)
    wk = np.zeros((64, 128), np.float32)
    wv = np.zeros((64, 128), np.float32)
    gate = np.zeros((2, 128, 16), np.float32)
    fc1 = np.zeros((64, 64), np.float32)
    fc2 = np.zeros((64, 64), np.float32)
    for n in range(4):
        r = slice(16 * n, 16 * n + 16)
        s = slice(32 * n, 32 * n + 16)
        for d in (s, slice(32 * n + 16, 32 * n + 32)):
            for e in range(4):
                wq[r, e, d] = i["L0_ffn_wq"][n, e].T
            wk[r, d] = i["L0_ffn_wk"][n].T
        wv[r, s] = i["L0_ffn_wv"][n].T
        gate[n // 2, (n % 2) * 64:(n % 2) * 64 + 64, n * 4:n * 4 + 4] = i["L0_ffn_gate_w"][n].T
        fc1[r, r] = i["L0_ffn_fc1_w"].T
        fc2[r, r] = i["L0_ffn_fc2_w"].T
    put("f0_wq", wq.reshape(64, 512))
    put("f0_wk", wk)
    put("f0_wv", wv)
    one = (k % 32 == HD) * 1.0
    put("minus", -np.stack([k % 32 < 16, k % 32 >= 16, k >= 0], 1).astype(np.float32))
    put("ones_col", row(one))
    put("f0_gate", np.concatenate([gate[0], gate[1]], 1))
    put("f0_gateb", row(i["L0_ffn_gate_b"].reshape(16)))
    for n, s in (("f0_lng", "ln_g"), ("f0_lnb", "ln_b"), ("f0_fng", "fnorm_g"), ("f0_fnb", "fnorm_b"), ("f0_fc2b", "fc2_b")):
        put(n, row(np.tile(i["L0_ffn_" + s], 4)))
    put("f0_fc1", fc1)
    put("f0_fc1b", np.tile(i["L0_ffn_fc1_b"], 4))
    put("f0_fc2", fc2)
    put("f0_fg", i["L0_ffn_fgate_w"].T)

    put("a1_g1", i["L1_attn_ln1_g"])
    put("a1_b1", i["L1_attn_ln1_b"])
    put("a1_Wx", i["L1_attn_Wx"])
    put("a1_bx", i["L1_attn_bx"].reshape(2, 128).T)
    put("a1_bx_bc", row(i["L1_attn_bx"]))
    qk = np.zeros((2, 128, 64), np.float32)
    bv = np.zeros((128, 128), np.float32)
    for hd in range(8):
        r = slice(32 * (hd % 4), 32 * (hd % 4) + 32)
        qk[hd // 4, r, 4 * hd:4 * hd + 4] = i["L1_attn_Wq"]
        qk[hd // 4, r, 32 + 4 * hd:36 + 4 * hd] = i["L1_attn_Wk"]
        bv[r, r] = i["L1_attn_Wv"]
    put("a1_qk", np.concatenate([qk[0], qk[1]], 1))
    put("a1_blk", (np.arange(32)[:, None] // 4 == np.arange(256)[None, :] // 32) * 1.0)
    put("a1_Wv", bv)
    put("a1_Wo", i["L1_attn_Wo"].reshape(2, 128, 64).transpose(1, 0, 2).reshape(128, 128))
    put("a1_bo", row(i["L1_attn_bo"]))
    put("a1_g2", i["L1_attn_ln2_g"])
    put("a1_b2", i["L1_attn_ln2_b"])
    put("a1_W1", i["L1_attn_W1"])
    put("a1_W1b", i["L1_attn_b1"].reshape(2, 128).T)
    put("a1_W2", i["L1_attn_W2"].reshape(2, 128, 64).transpose(1, 0, 2).reshape(128, 128))
    put("a1_W2b", row(i["L1_attn_b2"]))

    put("f1_ln1", i["L1_ffn_ln1_w"])
    put("f1_ln2", i["L1_ffn_ln2_w"])
    q = np.zeros((64, 128), np.float32)
    kk = np.zeros((64, 128), np.float32)
    v = np.zeros((64, 128), np.float32)
    rq = np.zeros((64, 128), np.float32)
    rk = np.zeros((32, 128), np.float32)
    rot = np.zeros((16, 16), np.float32)
    for d in range(8):
        rot[d + 8, d] = -1
        rot[d, d + 8] = 1
    for n in range(4):
        s = slice(32 * n, 32 * n + 16)
        g = n // 2
        for d in (s, slice(32 * n + 16, 32 * n + 32)):
            q[:, d] = i["L1_ffn_wq"][16 * n:16 * n + 16].T
            kk[:, d] = i["L1_ffn_wk"][16 * g:16 * g + 16].T
            rq[16 * n:16 * n + 16, d] = rot
            rk[16 * g:16 * g + 16, d] = rot
        v[:, s] = i["L1_ffn_wv"][16 * g:16 * g + 16].T
    put("f1_wq", q)
    put("f1_wk", kk)
    put("f1_wv", v)
    put("f1_wq_r", i["L1_ffn_wq"])
    put("f1_wk_r", i["L1_ffn_wk"])
    put("rot_q", rq)
    put("rot_k", rk)
    inv = 1.0 / 10000.0 ** (np.arange(0, HD, 2, dtype=np.float32) / HD)
    fr = np.outer(np.arange(LB, dtype=np.float32), inv)
    emb = np.concatenate([fr, fr], -1)
    cs = np.zeros((2, 128, LB), np.float32)
    for n in range(8):
        cs[0, 16 * n:16 * n + 16] = np.cos(emb).T
        cs[1, 16 * n:16 * n + 16] = np.sin(emb).T
    put("cos", cs[0])
    put("sin", cs[1])
    put("f1_wo", i["L1_ffn_wo"].T)
    put("f1_rt", i["L1_ffn_router_w"].T)
    z = np.zeros((64, KT1 * 128), np.float32)
    z[:, :NE * HID] = i["L1_ffn_w1"].reshape(NE * HID, 64).T
    put("f1_w1", z)
    z = np.zeros((64, KT1 * 128), np.float32)
    z[:, :NE * HID] = i["L1_ffn_w3"].reshape(NE * HID, 64).T
    put("f1_w3", z)
    z = np.zeros((KT1 * 128, 64), np.float32)
    z[:NE * HID] = i["L1_ffn_w2"].transpose(0, 2, 1).reshape(NE * HID, 64)
    put("f1_w2", z.reshape(KT1, 128, 64).transpose(1, 0, 2).reshape(128, -1))
    put("rev", row(8.0 - np.arange(8)))

    z = np.zeros((64, 65), np.float32)
    z[:, :64] = i["L2_attn_Wq"].T
    put("a2_q", z)
    put("a2_k", i["L2_attn_Wk"].T)
    z = np.zeros((64, 256), np.float32)
    z[:, :NODES] = i["L2_ffn_w1s"].T
    put("f2_w1", z)
    z = np.zeros(256, np.float32)
    z[:NODES] = i["L2_ffn_b1s"]
    put("f2_b1", row(z))
    z = np.zeros((256, 64), np.float32)
    z[:NODES] = i["L2_ffn_b2s"]
    put("f2_b2", z.reshape(2, 128, 64).transpose(1, 0, 2).reshape(128, 128))

    put("a3_g", i["L3_attn_norm_g"])
    put("a3_b", i["L3_attn_norm_b"])
    put("a3_fus", i["L3_attn_fusW"])
    put("a3_fusb", row(i["L3_attn_fusB"]))
    for d in "fb":
        w = lambda n: i[f"L3_attn_{n}_{d}"]
        put(f"a3{d}_in", w("inW"))
        put(f"a3{d}_cw", w("convW"))
        put(f"a3{d}_cb", w("convB"))
        put(f"a3{d}_dl", w("xW")[:, 0:4])
        put(f"a3{d}_bc", np.tile(w("xW")[:, 4:36], (1, 3)))
        put(f"a3{d}_dt", w("dtW"))
        put(f"a3{d}_dtb", w("dtB"))
        put(f"a3{d}_Alog", w("ALog"))
        put(f"a3{d}_Dp", w("Dp"))
        put(f"a3{d}_out", w("outW"))

    put("f3_g", i["L3_ffn_gamma"])
    put("f3_b", i["L3_ffn_beta"])
    put("f3_rt", i["L3_ffn_Wr"])
    put("f3_rtb", row(i["L3_ffn_br"]))
    put("f3_w1", i["L3_ffn_W1"].transpose(1, 0, 2).reshape(64, -1))
    put("f3_b1", i["L3_ffn_b1"].T)
    put("f3_w2", i["L3_ffn_W2"].transpose(1, 0, 2).reshape(128, -1))
    put("f3_b2", i["L3_ffn_b2"])
    return a


def kernel(**inputs):
    import concourse.bacc as _bacc
    from concourse.bass_utils import run_bass_kernel_spmd as _run

    i = {n: np.asarray(v) for n, v in inputs.items()}
    arrays = {
        "x_dram": np.ascontiguousarray(i["x"]),
        "pack_dram": pack_weights(i),
        "selectors_dram": selector_bits(),
        "w2s_dram": np.ascontiguousarray(i["L2_ffn_w2s"].reshape(NODES, 4096)),
    }
    nc = _bacc.Bacc("TRN2", target_bir_lowering=False, num_devices=1)
    args = [nc.dram_tensor(n, a.shape, F32, kind="ExternalInput").ap() for n, a in arrays.items()]
    args.append(nc.dram_tensor("out_dram", (B, L, D), F32, kind="ExternalOutput").ap())
    audio_tower(nc, *args)
    r = _run(nc, [arrays], core_ids=[0])
    return r.results[0]["out_dram"]
```

```python
from contextlib import ExitStack

import numpy as np

import concourse.bass as bass
from concourse import mybir

F32 = mybir.dt.float32
BF16 = mybir.dt.bfloat16
U8 = mybir.dt.uint8
ALU = mybir.AluOpType
ACT = mybir.ActivationFunctionType
AX = mybir.AxisListType

B, LX, D = 4, 750, 64
TAPS = [0, 1, 3, 7, 15, 31, 63, 127]
L = LX - len(TAPS) + 1
P0, TB = 124, 6
LB = P0 * TB
CH, CT = 372, 3
NB = 1
NIT = B // NB
T, W, NC = TB * NB, LB * NB, 2 * NB
TAIL = LX - LB
XW = LB + TAPS[-2]
MASKED = -1e30

NH, HD = 4, 16
E0 = 4
NE, HID = 8, 170
KT1 = -(-NE * HID // 128)
NODES = 255
DS = 16

SPEC = [
    ("ident", 128, 128), ("mask_qk", P0, P0), ("mask_kq", P0, P0),
    ("sel_sum", 128, 4 * 32), ("split1", 96, 1), ("split2", 96, 1),
    ("tok_w", 128, 256), ("tok_b", P0, 64),
    ("a0_xp", 64, 256), ("a0_dt", 128, 128), ("a0_B", 128, 128), ("a0_C", 128, 128),
    ("a3f_Alog", 128, 16), ("a3b_Alog", 128, 16), ("a0_dtb", 128, 1), ("a0_Alog", 128, 16), ("a0_D", 128, 1), ("a0_out", 128, 64),
    ("f0_hl", 64, 64), ("f0_hlb_bc", P0, 64), ("f0_wq", 64, 4 * 128),
    ("f0_wk", 64, 128), ("f0_wv", 64, 128), ("minus", 128, 3), ("ones_col", P0, 128),
    ("f0_gate", 128, 2 * 16), ("f0_gateb", P0, 16), ("f0_lng", P0, 64), ("f0_lnb", P0, 64),
    ("f0_fc1", 64, 64), ("f0_fc1b", 64, 1), ("f0_fc2", 64, 64), ("f0_fc2b", P0, 64),
    ("f0_fng", P0, 64), ("f0_fnb", P0, 64), ("f0_fg", 64, 4),
    ("a1_g1", 64, 1), ("a1_b1", 64, 1), ("a1_Wx", 64, 256), ("a1_bx", 128, 2), ("a1_bx_bc", P0, 256),
    ("a1_qk", 128, 2 * 64), ("a1_blk", 32, 256), ("a1_Wv", 128, 128), ("a1_Wo", 128, 128),
    ("a1_bo", P0, 64), ("a1_g2", 64, 1), ("a1_b2", 64, 1), ("a1_W1", 64, 256), ("a1_W1b", 128, 2),
    ("a1_W2", 128, 128), ("a1_W2b", P0, 64),
    ("f1_ln1", 64, 1), ("f1_ln2", 128, 1), ("f1_wq", 64, 128), ("f1_wk", 64, 128),
    ("f1_wq_r", 64, 64), ("f1_wk_r", 32, 64), ("rot_q", 64, 128), ("rot_k", 32, 128),
    ("cos", 128, LB), ("sin", 128, LB), ("f1_wv", 64, 128), ("f1_wo", 64, 64),
    ("f1_rt", 64, 8), ("f1_w2", 128, KT1 * 64), ("minus64", 128, 2),
    ("rev", P0, 8),
    ("a2_q", 64, 128), ("a2_k", 64, 128),
    ("f2_w1", 64, 256), ("f2_b1", P0, 256), ("f2_b2", 128, 128),
    ("a3_g", 64, 1), ("a3_b", 64, 1), ("a3_fus", 128, 64), ("a3_fusb", P0, 64),
    ("a3f_in", 64, 256), ("a3f_cw", 128, 4), ("a3f_cb", 128, 1), ("a3f_dl", 128, 4),
    ("a3f_bc", 128, 96), ("a3f_dt", 4, 128), ("a3f_dtb", 128, 1),
    ("a3f_Dp", 128, 1), ("a3f_out", 128, 64),
    ("a3b_in", 64, 256), ("a3b_cw", 128, 4), ("a3b_cb", 128, 1), ("a3b_dl", 128, 4),
    ("a3b_bc", 128, 96), ("a3b_dt", 4, 128), ("a3b_dtb", 128, 1),
    ("a3b_Dp", 128, 1), ("a3b_out", 128, 64),
    ("f3_g", 128, 1), ("f3_b", 128, 1), ("f3_rt", 64, 8), ("f3_rtb", P0, 8),
    ("f3_b1", 128, 8), ("f3_w2", 128, 8 * 64), ("f3_b2", 8, 64),
]
UP1, UP3, UPX, ECOLS = 0, KT1 * 128, 2 * KT1 * 128, (2 * KT1 + NE) * 128
OFF = {}
WCOLS = 0
for _n, _r, _c in SPEC:
    OFF[_n] = (_r, WCOLS, _c)
    WCOLS += _c


class Channel:

    def __init__(self, full, free, slots):
        self.full, self.free, self.slots = full, free, slots
        self.n_put = self.n_got = 0

    def put(self):
        k = self.n_put
        self.n_put += 1
        return self.slots[k % len(self.slots)], k - len(self.slots) + 1

    def get(self):
        k = self.n_got
        self.n_got += 1
        return self.slots[k % len(self.slots)], k + 1


def audio_tower(nc, x, pack, selectors, w2s, ups, out):
    ctx = ExitStack()
    with ctx:
        LOOP_OF = dict(x=0, conv=0, a0=0, sx=0, A=0, f0=1, a1=1, f1=2, f1e=2,
                       a2=2, f2=2, a3=3, a3f=3, a3b=3, f3=3, f3e=3, h=3)
        pool_of_sems, named = [], [{} for _ in range(4)]

        def S(name):
            names = named[LOOP_OF[name.split("_")[0]]]
            if name not in names:
                if len(names) == len(pool_of_sems):
                    pool_of_sems.append(ctx.enter_context(nc.semaphore(f"signal{len(names)}")))
                names[name] = pool_of_sems[len(names)]
            return names[name]

        def sb(name, shape, dt=F32):
            return ctx.enter_context(nc.sbuf_tensor(name, shape, dt))

        arrive, go, first_in, weights_in, selectors_in, w2_in, x_in = (ctx.enter_context(nc.semaphore(n)) for n in (
            "engines_arrived", "iteration_over", "first_weights_in", "weights_in", "selectors_in", "w2_in", "x_in"))
        out_done = ctx.enter_context(nc.semaphore("out_done"))
        selectors_ready = ctx.enter_context(nc.semaphore("selectors_ready"))
        ups_in, ups_split = (ctx.enter_context(nc.semaphore(n)) for n in ("expert_weights_in", "expert_weights_split"))
        consts_ready = ctx.enter_context(nc.semaphore("consts_ready"))

        WP = sb("weights", [128, WCOLS])
        W2N = sb("tree_w2", [128, 2, 4096])
        EW = sb("expert_w1", [128, 3, ECOLS], BF16)

        def P(name, a=0, b=None):
            r, o, c = OFF[name]
            return WP[0:r, o + a:o + (c if b is None else b)]

        PS = ctx.enter_context(nc.psum_tensor("psum", [128, 8, 512], F32))

        def singles(lo, hi):
            return [PS[:, i, :] for i in range(lo, hi)]

        def pairs(lo, hi):
            return [PS[:, i:i + 2, :] for i in range(lo, hi, 2)]

        channels = {}

        def chan(name, slots):
            if name not in channels:
                channels[name] = Channel(S(name + "_full"), S(name + "_free"), slots)
            return channels[name]

        identb = sb("identb", [128, 128], BF16)
        maskqk = sb("maskqk", [P0, P0], BF16)
        maskkq = sb("maskkq", [P0, P0], BF16)
        selrep = sb("selrep", [128, 4 * 128], BF16)
        selmoe = sb("selmoe", [96, KT1 * 128], BF16)
        selbn = sb("selbn", [96, 32 * 128], BF16)
        nA0 = sb("nA0", [128, 16])
        nA3 = sb("nA3", [128, 2, 16])
        h_all = sb("h_all", [P0, B * TB, D])
        sx_all = sb("sx_all", [P0, B * TB, D])
        xtail = sb("xtail", [TAIL, 2 * D])
        h = sb("h", [P0, T, D])
        X = sb("X", [P0, T, D + 1])
        Xs = X[:, :, 0:D]
        xn = sb("xn", [P0, T, D])
        sq = sb("sq", [P0, T, D])
        fx = sb("fx", [P0, T, D])
        st_sum = sb("st_sum", [P0, T * 4])
        st_mean = sb("st_mean", [P0, T * 4])
        st_var = sb("st_var", [P0, T * 4])
        st_std = sb("st_std", [P0, T * 4])
        st_rstd = sb("st_rstd", [P0, T * 8])
        FB = sb("FB", [128, 13 * W])
        F = [FB[:, i * W:(i + 1) * W] for i in range(13)]
        xT = FB[:, 9 * W:9 * W + XW + TAPS[-1] - TAPS[-2]]
        xP = [FB[:, k * XW:(k + 1) * XW] for k in range(4)]
        Hb = [sb(f"Hb{i}", [128, W], BF16) for i in range(3)]
        SCB = sb("SCB", [128, 8 * LB])
        RA, RB, RS, RC = ([SCB[:, (2 * r + i) * LB:(2 * r + i + 1) * LB] for i in range(2)] for r in range(4))
        otok = SCB[0:P0, 0:T * 256].rearrange("p (t n) -> p t n", n=256)
        otok2 = SCB[0:P0, T * 256:T * 512].rearrange("p (t n) -> p t n", n=256)
        PT = [SCB[0:P0, 2 * CH * i:2 * CH * (i + 1)].rearrange("p (m n) -> p m n", m=2) for i in range(4)]
        O0 = [SCB[:, (4 + e) * LB:(5 + e) * LB] for e in range(E0)]
        ok0, gk0 = (FB[0:P0, 7 * W + i * T * 256:7 * W + (i + 1) * T * 256].rearrange("p (t n) -> p t n", n=256)
                    for i in range(2))
        vtok = sb("vtok", [P0, T, 128])
        Q6 = FB[0:99, 3 * W:11 * W].bitcast(BF16).rearrange("p (h n) -> p h n", n=LB)
        K6 = FB[0:99, 11 * W:13 * W].bitcast(BF16).rearrange("p (h n) -> p h n", n=LB)
        part_r = [SCB[:, (2 + i) * LB:(3 + i) * LB] for i in range(2)]
        part_h, part_m, part_a, part_z = ([SCB[:, (4 + k) * LB:(5 + k) * LB].bitcast(BF16)[:, i * LB:(i + 1) * LB]
                                           for i in range(2)] for k in range(4))
        M3 = sb("M3", [P0, TB, 48], BF16)
        MR = sb("MR", [48, LB], BF16)
        ones3 = sb("ones3", [3, P0], BF16)

        def part_x(tag, s):
            return SCB[:, (s % 2) * LB:(s % 2 + 1) * LB]

        def strips(s):
            i = s % 2
            return (part_a[i], part_z[i], part_m[i]) if s == 0 else (part_h[i], part_a[i], part_z[i])

        mx = sb("mx", [P0, E0, NH, 2, TB])
        m2 = sb("m2", [P0, E0, NH, TB])
        qtok, ktok = (z[:, :, :].rearrange("p t f -> p (t f)")[:, 0:T * 32].rearrange("p (t r) -> p t r", r=32)
                      for z in (fx, xn))
        W96 = otok2.rearrange("p t n -> p (t n)")[:, 0:T * 96].rearrange("p (t n) -> p t n", n=96)
        SAr = [SCB[:, i * CH:(i + 1) * CH] for i in range(3)]
        HH = [SCB[:, (3 + i) * CH:(4 + i) * CH] for i in range(3)]
        bn6 = sb("bn6", [P0, T, 6])
        bn2 = sb("bn2", [P0, T, 2])
        tbl = sb("tbl", [P0, 64])
        preloads = iter(range(1, 64))
        rl = sb("rl", [P0, T, 4])
        lg = sb("lg", [P0, T, 16])
        lg2 = sb("lg2", [P0, T, 16])
        sm = sb("sm", [P0, T * 8])
        pad0 = sb("pad0", [P0, T, D])
        eqb = [sb(f"eq{i}", [P0, T, 8]) for i in range(5)]
        r8 = [sb(f"r8_{i}", [P0, T]) for i in range(6)]
        xsp = FB[:, 11 * W:11 * W + NB * (LB + 6)].rearrange("p (b n) -> p b n", b=NB)
        ksm = sb("ksm", [64, 8])
        kvs, kvs2 = (F[12][:, 64 * i:64 * i + 64].rearrange("p (t r) -> p t r", t=2) for i in range(2))
        Mh, kxm = F[12][0:32, 128:192], F[12][0:32, 192:448]
        wrq, wrk = F[11][0:64, 0:128], F[11][0:64, 128:256]
        prod = [FB[0:P0, 3 * W:3 * W + 4096], SCB[0:P0, 0:4096]]
        Xa, Xb = (F[3].bitcast(BF16)[:, i * LB:(i + 1) * LB] for i in range(2))
        x2tok = vtok
        Lg, Ag = (FB[0:P0, 3 * W + 4096 + i * T * 256:3 * W + 4096 + (i + 1) * T * 256].rearrange(
            "p (t n) -> p t n", n=256) for i in range(2))

        def bc(ap, n):
            return ap.unsqueeze(len(ap.shape)).broadcast_to(list(ap.shape) + [n])

        def bt(ap, n):
            return ap.unsqueeze(1).broadcast_to([ap.shape[0], n, ap.shape[1]])

        def cols(c):
            return slice(c * CH, (c + 1) * CH)

        def tcols(t):
            return slice(t * P0, (t + 1) * P0)


        def dve_norm(dve, src, dst, n, f, eps, tag, centre=True):
            s, m, v, d, r = (z[:, 0:n] for z in (st_sum, st_mean, st_var, st_std, st_rstd))
            if f == D:
                for t in range(n):
                    dve.bn_stats(bn6[:, t, :], src[:, t, :])
                dve.drain()
                for t in range(n):
                    dve.bn_aggr(bn2[:, t, :], bn6[:, t, :])
                dve.drain()
                if centre:
                    dve.tensor_scalar(v, bn2[:, :, 1], eps, None, ALU.add).then_inc(S(tag + "_var"), 1)
                    dve.tensor_tensor(dst, src, bc(bn2[:, :, 0], f), ALU.subtract)
                else:
                    dve.tensor_tensor(s, bn2[:, :, 0], bn2[:, :, 0], ALU.mult)
                    dve.drain()
                    dve.scalar_tensor_tensor(out=v, in0=s, scalar=eps, in1=bn2[:, :, 1], op0=ALU.add,
                                             op1=ALU.add).then_inc(S(tag + "_var"), 1)
                dve.wait_ge(S(tag + "_std"), 1)
                dve.reciprocal(r, d)
                dve.drain()
                return dve.tensor_tensor(dst, dst if centre else src, bc(r, f), ALU.mult)
            sqv = sq[:, :, :].rearrange("p t f -> p (t f)").rearrange("p (n f) -> p n f", f=f)
            src_c = src
            if centre:
                dve.tensor_reduce(s, src, AX.X, ALU.add)
                dve.drain()
                dve.tensor_scalar(m, s, 1.0 / f, None, ALU.mult)
                dve.drain()
                dve.tensor_tensor(dst, src, bc(m, f), ALU.subtract)
                dve.drain()
                src_c = dst
            dve.tensor_tensor(sqv, src_c, src_c, ALU.mult)
            dve.drain()
            dve.tensor_reduce(s, sqv, AX.X, ALU.add)
            dve.drain()
            dve.tensor_scalar(v, s, 1.0 / f, eps, ALU.mult, ALU.add).then_inc(S(tag + "_var"), 1)
            dve.wait_ge(S(tag + "_std"), 1)
            dve.reciprocal(r, d)
            dve.drain()
            return dve.tensor_tensor(dst, src_c, bc(r, f), ALU.mult)

        def act_table(act, func):
            k = next(preloads)
            act.activation(tbl[:, k:k + 1], tbl[:, 0:1], func)

        def act_norm(act, n, tag, then=None):
            act_table(act, ACT.Sqrt)
            act.wait_ge(S(tag + "_var"), 1)
            act.activation(st_std[:, 0:n], st_var[:, 0:n], ACT.Sqrt).then_inc(S(tag + "_std"), 1)
            if then:
                act_table(act, then)

        def pe_turn(pe, A, src, f, ready):
            if ready:
                pe.wait_ge(S(ready), 1)
            for c in range(NC):
                ps, w = A.put()
                if w > 0:
                    pe.wait_ge(A.free, w)
                for k in range(CT):
                    ins = pe.transpose(ps[0:f, tcols(k)], src[:, c * CT + k, 0:f], P("ident")[0:P0, 0:P0])
                ins.then_inc(A.full, 1)

        def pe_project(pe, A, weights, src, rows):
            for c in range(NC):
                ps, w = A.put()
                if w > 0:
                    pe.wait_ge(A.free, w)
                pe.matmul(ps[0:rows, 0:CH], weights, src[:, cols(c)], start=True, stop=True).then_inc(A.full, 1)

        def act_empty(act, A, dst, rows, func=ACT.Identity, scale=1.0, bias=0.0, signal=None):
            for c in range(NC):
                ps, w = A.get()
                act.wait_ge(A.full, w)
                act.activation(dst[0:rows, cols(c)], ps[0:rows, 0:CH], func, scale=scale, bias=bias).then_inc(A.free, 1)
            if signal:
                act.drain().then_inc(S(signal), 1)

        def pe_tokens(pe, A, terms, n):
            for b in range(NB):
                ps, w = A.put()
                if w > 0:
                    pe.wait_ge(A.free, w)
                for j in range(TB):
                    for i, (src, rhs) in enumerate(terms):
                        ins = pe.matmul(ps[0:P0, j * n:(j + 1) * n], src[:, tcols(b * TB + j)], rhs,
                                        start=(i == 0), stop=(i == len(terms) - 1))
                ins.then_inc(A.full, 1)

        def tok(ps, n):
            return ps[0:P0, 0:TB * n].rearrange("p (t n) -> p t n", n=n)

        def twice(z):
            return z[:, :, :].rearrange("p t (two f) -> p t two f", two=2)

        def tiles(b):
            return slice(b * TB, (b + 1) * TB)

        def dve_softmax(dve, src, dst, n, f, tag):
            s = sm[:, 0:n]
            dve.tensor_reduce(s, src, AX.X, ALU.max)
            dve.drain()
            dve.tensor_tensor(dst, src, bc(s, f), ALU.subtract).then_inc(S(tag + "_sub"), 1)
            dve.wait_ge(S(tag + "_exp"), 1)
            dve.tensor_reduce(s, dst, AX.X, ALU.add)
            dve.drain()
            dve.reciprocal(st_rstd[:, 0:n], s)
            dve.drain()
            return dve.tensor_tensor(dst, dst, bc(st_rstd[:, 0:n], f), ALU.mult)

        def act_softmax(act, dst, tag):
            act_table(act, ACT.Exp)
            act.wait_ge(S(tag + "_sub"), 1)
            act.activation(dst, dst, ACT.Exp).then_inc(S(tag + "_exp"), 1)

        def softplus_act(act, t, a, l, tag):
            act.activation(a, t, ACT.Abs)
            act.drain()
            act.activation(a, a, ACT.Exp, scale=-1.0)
            act.drain()
            act.activation(l, a, ACT.Ln, bias=1.0).then_inc(S(tag), 1)

        def softplus_dve(dve, t, a, l, tmp, mask, tag):
            dve.wait_ge(S(tag), 1)
            dve.tensor_scalar(tmp, a, 1.0 / 3.0, -0.5, ALU.mult, ALU.add)
            dve.tensor_scalar(mask, a, 2.0 ** -6, None, ALU.is_lt)
            dve.drain()
            dve.tensor_tensor(tmp, tmp, a, ALU.mult)
            dve.drain()
            dve.scalar_tensor_tensor(out=tmp, in0=tmp, scalar=1.0, in1=a, op0=ALU.add, op1=ALU.mult)
            dve.drain()
            dve.copy_predicated(l, mask, tmp)
            dve.drain()
            return dve.scalar_tensor_tensor(out=l, in0=t, scalar=0.0, in1=l, op0=ALU.max, op1=ALU.add)

        mask8 = sb("mask8", [128, W], U8)


        PAIRS = [(TAPS[k], TAPS[k + 1] - TAPS[k]) for k in range(0, len(TAPS), 2)]

        def conv_sp(sp, b):
            src = x[bass.ds(b, 1), :, :] if not isinstance(b, int) else x[b:b + 1, :, :]
            for half in (slice(0, D), slice(D, 2 * D)):
                sp.dma_start(x2tok[:, :, half], src[:, 0:LB, :].rearrange("b (j p) f -> p (b j) f", p=P0)).then_inc(x_in, 16)
                sp.dma_start(xtail[:, half], src[:, LB:LX, :].rearrange("b p f -> p (b f)")).then_inc(x_in, 16)

        def conv_pe(pe, it):
            A = chan("conv_turned", singles(0, 4))
            pe.wait_ge(x_in, it * 64 + 64)
            pe_turn(pe, A, x2tok, 2 * D, None)
            ps, w = A.put()
            pe.transpose(ps[:, 0:TAIL], xtail[:, :], P("ident")[0:TAIL, 0:TAIL]).then_inc(A.full, 1)
            pe.wait_ge(S("conv_pairs"), 2)
            Y = chan("conv_out", singles(4, 8))
            ps, w = Y.put()
            for j in range(TB):
                for k, (o, _) in enumerate(PAIRS):
                    ins = pe.matmul(ps[0:P0, j * D:(j + 1) * D], xP[k][:, j * P0 + o:(j + 1) * P0 + o],
                                    P("tok_w", k * D, (k + 1) * D), start=(k == 0), stop=(k == len(PAIRS) - 1))
            ins.then_inc(Y.full, 1)

        def conv_pair(copy, k):
            d = PAIRS[k][1]
            copy(xP[k][0:D, :], xT[0:D, 0:XW])
            copy(xP[k][D:2 * D, :], xT[D:2 * D, d:d + XW])

        def conv_act(act):
            A = chan("conv_turned", None)
            for c in range(NC):
                ps, w = A.get()
                act.wait_ge(A.full, w)
                act.activation(xT[:, cols(c)], ps[:, 0:CH], ACT.Identity).then_inc(A.free, 1)
            ps, w = A.get()
            act.wait_ge(A.full, w)
            act.activation(xT[:, LB:LX], ps[:, 0:TAIL], ACT.Identity).then_inc(A.free, 1)
            act.drain().then_inc(S("conv_xT"), 1)
            act.wait_ge(S("conv_padded"), 1)
            conv_pair(lambda o, i: act.activation(o, i, ACT.Identity), 0)
            act.drain().then_inc(S("conv_pairs"), 1)

        def conv_dve(dve):
            dve.memset(xT[:, LX:], 0.0)
            dve.drain().then_inc(S("conv_padded"), 1)
            dve.wait_ge(S("conv_xT"), 1)
            for k in range(1, len(PAIRS)):
                conv_pair(dve.tensor_copy, k)
            dve.drain().then_inc(S("conv_pairs"), 1)
            Y = chan("conv_out", None)
            ps, w = Y.get()
            dve.wait_ge(Y.full, w)
            dve.tensor_tensor(h[:, :, :], tok(ps, D), bt(P("tok_b"), TB), ALU.add).then_inc(Y.free, 1)
            dve.drain()


        A0 = dict(xT=F[0], u=F[1], sz=F[2], dt=F[3], Bm=F[4], Cm=F[5], t=F[6], a=F[7], y=F[8])

        def scan0_pe(pe):
            A = chan("a0_proj", singles(0, 4))
            pe_turn(pe, A, xn, D, "a0_normed")
            pe.wait_ge(S("a0_xT"), 1)
            pe_project(pe, A, P("a0_xp", 0, 128), A0["xT"][0:D, :], 128)
            pe_project(pe, A, P("a0_xp", 128, 256), A0["xT"][0:D, :], 128)
            pe.wait_ge(S("a0_u"), 1)
            for n in ("a0_dt", "a0_B", "a0_C"):
                pe_project(pe, A, P(n), A0["u"], 128)
            pe.wait_ge(S("a0_split"), 1)
            pe.wait_ge(A.free, A.n_put)
            R = chan("a0_rep", pairs(0, 6))
            Y = chan("a0_sum", pairs(6, 8))
            n = 16 * NB
            for k in range(n + 3):
                if k < n:
                    b, g = divmod(k, 16)
                    q, r = slice(32 * (g // 4), 32 * (g // 4) + 32), g % 4
                    ps, w = R.put()
                    if w > 0:
                        pe.wait_ge(R.free, w)
                    for c in range(2):
                        for i in range(3):
                            ins = pe.matmul(ps[:, c, 0:CH], selrep[q, r * 128:(r + 1) * 128],
                                            Hb[i][q, cols(2 * b + c)], start=(i == 0), stop=(i == 2))
                    ins.then_inc(R.full, 1)
                if k >= 3:
                    i = k - 3
                    q, r = i % 16 // 4, i % 4
                    if i % 16 == 0:
                        y, w = Y.put()
                        if w > 0:
                            pe.wait_ge(Y.free, w)
                    pe.wait_ge(S("a0_read"), i + 1)
                    for c in range(2):
                        ins = pe.matmul(y[32 * q:32 * q + 32, c, 0:CH], P("sel_sum", 32 * r, 32 * r + 32),
                                        RC[i % 2][:, cols(c)], start=(r == 0), stop=(r == 3))
                    ins.then_inc(S("a0_summed"), 1)
                    if i % 16 == 15:
                        pe.drain().then_inc(Y.full, 1)
            pe.wait_ge(S("a0_y"), 1)
            Y2 = chan("a0_out", singles(0, 4))
            pe_tokens(pe, Y2, [(A0["y"], P("a0_out"))], D)

        def scan0_act(act):
            act_norm(act, T, "a0", ACT.Silu)
            A = chan("a0_proj", None)
            act_empty(act, A, A0["xT"], D, signal="a0_xT")
            act_empty(act, A, A0["u"], 128, func=ACT.Silu, signal="a0_u")
            act_empty(act, A, A0["sz"], 128, func=ACT.Silu)
            act_table(act, ACT.Exp)
            act_empty(act, A, A0["t"], 128, bias=P("a0_dtb"))
            act_empty(act, A, A0["Bm"], 128)
            act_empty(act, A, A0["Cm"], 128, signal="a0_BC")
            softplus_act(act, A0["t"], A0["a"], A0["dt"], "a0_ln")
            act_table(act, ACT.Exp)
            act.wait_ge(S("a0_dt"), 1)
            for k in range(16 * NB):
                b, g = divmod(k, 16)
                if k >= 2:
                    act.wait_ge(S("a0_scanned"), k - 1)
                act.activation(RA[k % 2], A0["dt"][:, b * LB:(b + 1) * LB], ACT.Exp,
                               scale=nA0[:, g:g + 1]).then_inc(S("a0_decay"), 1)

        def dve_split(dve, src, parts, tmp):
            dve.tensor_copy(parts[0], src)
            dve.drain()
            dve.tensor_tensor(tmp, src, parts[0], ALU.subtract)
            dve.drain()
            dve.tensor_copy(parts[1], tmp)
            dve.drain()
            dve.tensor_tensor(tmp, tmp, parts[1], ALU.subtract)
            dve.drain()
            return dve.tensor_copy(parts[2], tmp)

        def scan0_dve(dve):
            dve_norm(dve, h[:, :, :], xn[:, :, :], T, D, 1e-5, "a0").then_inc(S("a0_normed"), 1)
            dve.wait_ge(S("a0_u"), 1)
            dve_split(dve, A0["u"][:, :], [z[:, :] for z in Hb], F[9][:, :]).then_inc(S("a0_split"), 1)
            dve.wait_ge(S("a0_BC"), 1)
            softplus_dve(dve, A0["t"][:, :], A0["a"][:, :], A0["dt"][:, :], F[10][:, :], mask8[:, :],
                         "a0_ln").then_inc(S("a0_dt"), 1)
            dve.drain()
            dve.tensor_tensor(A0["Bm"][:, :], A0["Bm"][:, :], A0["dt"][:, :], ALU.mult)
            dve.drain()
            R = chan("a0_rep", None)
            n = 16
            for k in range(n + 1):
                if k < n:
                    ps, w = R.get()
                    dve.wait_ge(R.full, w)
                    if k >= 2:
                        dve.wait_ge(S("a0_scanned"), k - 1)
                    dve.tensor_tensor(RB[k % 2][:, :].rearrange("p (c n) -> p c n", c=2), ps[:, :, 0:CH],
                                      A0["Bm"][:, :].rearrange("p (c n) -> p c n", c=2), ALU.mult).then_inc(R.free, 1)
                if k >= 1:
                    i = k - 1
                    dve.wait_ge(S("a0_decay"), i + 1)
                    dve.wait_ge(R.free, i + 1)
                    if i >= 2:
                        dve.wait_ge(S("a0_read"), i - 1)
                    dve.tensor_tensor_scan(RS[i % 2][:, :], RA[i % 2][:, :], RB[i % 2][:, :], 0.0, ALU.mult,
                                           ALU.add).then_inc(S("a0_scanned"), 1)
            Y = chan("a0_sum", None)
            ps, w = Y.get()
            dve.wait_ge(Y.full, w)
            v = lambda z: z[:, :].rearrange("p (c n) -> p c n", c=2)
            dve.scalar_tensor_tensor(out=v(A0["y"]), in0=v(A0["u"]), scalar=P("a0_D"), in1=ps[:, :, 0:CH],
                                     op0=ALU.mult, op1=ALU.add).then_inc(Y.free, 1)
            dve.drain()
            ins = dve.tensor_tensor(A0["y"][:, :], A0["y"][:, :], A0["sz"][:, :], ALU.mult)
            ins.then_inc(S("a0_y"), 1)
            dve.drain()
            dve_residual(dve, "a0_out")

        def scan0_pool(pool):
            for k in range(16):
                pool.wait_ge(S("a0_scanned"), k + 1)
                if k >= 2:
                    pool.wait_ge(S("a0_summed"), k - 1)
                pool.tensor_tensor(RC[k % 2][:, :], RS[k % 2][:, :], A0["Cm"][:, :], ALU.mult).then_inc(S("a0_read"), 1)

        def dve_residual(dve, name):
            Y2 = chan(name, None)
            for b in range(NB):
                ps, w = Y2.get()
                dve.wait_ge(Y2.full, w)
                dve.tensor_tensor(h[:, tiles(b), :], h[:, tiles(b), :], tok(ps, D), ALU.add).then_inc(Y2.free, 1)
            dve.drain()


        def sx_pe(pe):
            A = chan("sx_turned", singles(4, 8))
            pe_turn(pe, A, X, D, "sx_normed")
            pe.wait_ge(S("sx_xT"), 1)
            Y = chan("sx_out", singles(0, 4))
            pe_tokens(pe, Y, [(F[0][0:D, :], P("f0_hl"))], D)

        def sx_act(act):
            act_norm(act, T, "sx")
            act_empty(act, chan("sx_turned", None), F[0], D, signal="sx_xT")

        def sx_dve(dve, it):
            dve_norm(dve, h[:, :, :], Xs, T, D, 1e-5, "sx").then_inc(S("sx_normed"), 1)
            dve.tensor_copy(h_all[:, bass.ds(it * T, T), :], h[:, :, :])
            Y = chan("sx_out", None)
            for b in range(NB):
                ps, w = Y.get()
                dve.wait_ge(Y.full, w)
                dve.tensor_tensor(fx[:, tiles(b), :], tok(ps, D), bt(P("f0_hlb_bc"), TB), ALU.add).then_inc(Y.free, 1)
            dve.drain()
            dve.tensor_copy(sx_all[:, bass.ds(it * T, T), :], fx[:, :, :])
            dve.drain()


        STACK_OF = [(0, 2, 3), (1,)]

        def pe_stack(pe, tag, nt, project):
            SP = [chan(f"{tag}_stack0", pairs(4, 8)), chan(f"{tag}_stack1", pairs(2, 4))]
            project(0)
            project(1)
            for s in range(nt):
                if s + 2 < nt:
                    project(s + 2)
                pe.wait_ge(S(f"{tag}_parts"), s + 1)
                for n in range(NH):
                    C = SP[n == STACK_OF[1][0]]
                    ps, w = C.put()
                    if w > 0:
                        pe.wait_ge(C.free, w)
                    for c in range(2):
                        for i in range(3):
                            ins = pe.matmul(ps[32 * i:32 * i + 32, c, 0:CH], identb[:, 32 * n:32 * n + 32],
                                            strips(s)[i][:, cols(c)], start=True, stop=True)
                    ins.then_inc(C.full, 1)

        def stack_copy(eng, copy, tag, s, i):
            C = chan(f"{tag}_stack{i}", None)
            for n in STACK_OF[i]:
                dst = K6[0:96, n, :] if s == 0 else Q6[0:96, (s - 1) * NH + n, :]
                ps, w = C.get()
                eng.wait_ge(C.full, w)
                copy(dst.rearrange("p (c n) -> p c n", c=2), ps[0:96, :, 0:CH]).then_inc(C.free, 1)

        def act_stack(act, tag, nt, fill):
            for s in range(nt + 1):
                if s < nt:
                    if s >= 2:
                        act.wait_ge(S(f"{tag}_parts"), s - 1)
                    fill(s)
                    if s >= 2:
                        for i in range(2):
                            act.wait_ge(chan(f"{tag}_stack{i}", None).full, len(STACK_OF[i]) * (s - 1))
                    act.activation(part_h[s % 2][:, :], part_x(tag, s), ACT.Identity).then_inc(S(f"{tag}_high"), 1)
                if s >= 1:
                    stack_copy(act, lambda o, i: act.activation(o, i, ACT.Identity), tag, s - 1, 0)
            act.drain().then_inc(S(f"{tag}_stacked"), 1)

        def dve_stack(dve, tag, nt):
            dve.memset(K6[96:99, :, :], 1.0)
            for s in range(nt + 1):
                if s < nt:
                    x, hi, lo = part_x(tag, s), part_h[s % 2], part_m[s % 2]
                    a, z, r = part_a[s % 2], part_z[s % 2], part_r[s % 2]
                    first, both = P("minus", 0, 1), P("minus", 2, 3)
                    second = P("minus", 1, 2)
                    dve.wait_ge(S(f"{tag}_high"), s + 1)
                    dve.scalar_tensor_tensor(out=r, in0=hi[:, :], scalar=first if s == 0 else both, in1=x,
                                             op0=ALU.mult, op1=ALU.add)
                    dve.scalar_tensor_tensor(out=a[:, :], in0=hi[:, :], scalar=second, in1=x, op0=ALU.mult, op1=ALU.add)
                    dve.drain()
                    dve.tensor_copy(lo[:, :], r)
                    dve.drain()
                    dve.scalar_tensor_tensor(out=z[:, :], in0=lo[:, :], scalar=first if s == 0 else second, in1=r,
                                             op0=ALU.mult, op1=ALU.add)
                    dve.drain().then_inc(S(f"{tag}_parts"), 1)
                if s >= 1:
                    stack_copy(dve, dve.tensor_copy, tag, s - 1, 1)
            dve.drain().then_inc(S(f"{tag}_stacked"), 1)

        def attend_pe(pe, tag, ne):
            for i in range(2):
                C = chan(f"{tag}_stack{i}", None)
                pe.wait_ge(C.free, C.n_put)
            pe.wait_ge(S(f"{tag}_stacked"), 2)
            SA = chan(f"{tag}_score", pairs(0, 8))
            for e in range(ne):
                for i in range(TB):
                    for kc in range(1 + (i >= CT)):
                        wd = min(CH, P0 * (i + 1) - kc * CH)
                        diag = i // CT == kc
                        for p in range(2):
                            ps, w = SA.put()
                            if w > 0:
                                pe.wait_ge(SA.free, w)
                            for m in range(2):
                                n = 2 * p + m
                                ins = pe.matmul(ps[0:P0, m, 0:wd], Q6[0:96, e * NH + n, tcols(i)],
                                                K6[0:96, n, kc * CH:kc * CH + wd], start=True, stop=True)
                                if diag:
                                    ins = pe.matmul(ps[0:P0, m, wd - P0:wd], identb[0:P0, 0:P0], maskqk[:, :],
                                                    start=False, stop=True, skip_group_check=True)
                            ins.then_inc(SA.full, 1)
            M = chan(f"{tag}_mrows", pairs(0, 2))
            ps, w = M.put()
            pe.wait_ge(S(f"{tag}_maxima"), 1)
            for i in range(TB):
                ins = pe.matmul(ps[0:3 * NH * ne, i // CT, (i % CT) * P0:(i % CT + 1) * P0], M3[:, i, 0:3 * NH * ne],
                                identb[0:P0, 0:P0], start=True, stop=True)
            ins.then_inc(M.full, 1)
            SB = chan(f"{tag}_scoreT", pairs(0, 6))
            OC = chan(f"{tag}_o", singles(6, 8))
            pe.wait_ge(S(f"{tag}_mplaced"), 48)
            groups = [(e, c, j) for e in range(ne) for c in range(2) for j in range(CT * c + CT)]
            obank = None
            for g in range(len(groups) + 1):
                if g < len(groups):
                    e, c, j = groups[g]
                    off = max(0, j - CT * c) * P0
                    wd = CH - off
                    for p in range(2):
                        ps, w = SB.put()
                        if w > 0:
                            pe.wait_ge(SB.free, w)
                        for m in range(2):
                            n = 2 * p + m
                            ins = pe.matmul(ps[0:P0, m, 0:wd], K6[0:99, n, tcols(j)],
                                            Q6[0:99, e * NH + n, c * CH + off:(c + 1) * CH], start=True, stop=True)
                            if j >= CT * c:
                                ins = pe.matmul(ps[0:P0, m, 0:P0], identb[0:P0, 0:P0], maskkq[:, :],
                                                start=False, stop=True, skip_group_check=True)
                        ins.then_inc(SB.full, 1)
                if g >= 1:
                    e, c, j = groups[g - 1]
                    off = max(0, j - CT * c) * P0
                    if j == 0:
                        obank, w = OC.put()
                        if w > 0:
                            pe.wait_ge(OC.free, w)
                    pe.wait_ge(SB.free, 2 * g)
                    for n in range(NH):
                        ins = pe.matmul(obank[32 * n:32 * n + 32, off:CH], vtok[:, j, 32 * n:32 * n + 32],
                                        PT[(2 * g - 2 + n // 2) % 4][:, n % 2, 0:CH - off], start=(j == 0),
                                        stop=(j == CT * c + CT - 1))
                    ins.then_inc(S(f"{tag}_probs_used"), 1)
                    if j == CT * c + CT - 1:
                        pe.drain().then_inc(OC.full, 1)

        def attend_sp(sp, tag, ne):
            sp.wait_ge(S(f"{tag}_mrow"), 1)
            for i in range(3):
                sp.dma_start(Q6[96 + i:97 + i, 0:NH * ne, :], MR[NH * ne * i:NH * ne * (i + 1), :]).then_inc(S(f"{tag}_mplaced"), 16)

        def attend_act(act, tag, ne):
            M = chan(f"{tag}_mrows", None)
            ps, w = M.get()
            act.wait_ge(M.full, w)
            act.activation(MR[0:3 * NH * ne, :].rearrange("p (c n) -> p c n", c=2), ps[0:3 * NH * ne, :, 0:CH],
                           ACT.Identity).then_inc(S(f"{tag}_mrow"), 1)
            SB = chan(f"{tag}_scoreT", None)
            ku = 0
            for e in range(ne):
                for c in range(2):
                    for j in range(CT * c + CT):
                        for p in range(2):
                            wd = CH - max(0, j - CT * c) * P0
                            ps, w = SB.get()
                            act.wait_ge(SB.full, w)
                            if ku >= 4:
                                act.wait_ge(S(f"{tag}_probs_used"), ku // 2 - 1)
                            act.activation(PT[ku % 4][:, :, 0:wd], ps[0:P0, :, 0:wd], ACT.Exp).then_inc(SB.free, 1)
                            ku += 1

        def attend_dve(dve, tag, oT, ne):
            SA = chan(f"{tag}_score", None)
            dve.memset(mx[:, :, :, 1, 0:CT], -3e38)
            for e in range(ne):
                for i in range(TB):
                    for kc in range(1 + (i >= CT)):
                        wd = min(CH, P0 * (i + 1) - kc * CH)
                        for p in range(2):
                            ps, w = SA.get()
                            dve.wait_ge(SA.full, w)
                            dve.tensor_reduce(mx[:, e, 2 * p:2 * p + 2, kc, i], ps[0:P0, :, 0:wd], AX.X,
                                              ALU.max).then_inc(SA.free, 1)
            dve.drain()
            n = NH * ne
            for e in range(ne):
                dve.tensor_tensor(m2[:, e, :, :], mx[:, e, :, 0, :], mx[:, e, :, 1, :], ALU.max)
            dve.drain()
            mv = m2[:, :, :, :].rearrange("p e n i -> p i (e n)")[:, :, 0:n]
            for i in range(3):
                dve.tensor_scalar(M3[:, :, i * n:(i + 1) * n], mv, -1.0, None, ALU.mult)
                if i < 2:
                    dve.drain()
                    dve.tensor_tensor(mv, mv, M3[:, :, i * n:(i + 1) * n], ALU.add)
                    dve.drain()
            dve.drain().then_inc(S(f"{tag}_maxima"), 1)
            OC = chan(f"{tag}_o", None)
            for e in range(ne):
                for c in range(2):
                    ps, w = OC.get()
                    dve.wait_ge(OC.full, w)
                    dve.tensor_copy(oT[e][:, cols(c)], ps[:, 0:CH]).then_inc(OC.free, 1)
            dve.drain().then_inc(S(f"{tag}_gathered"), 1)

        def ffn0_pe(pe):
            A = chan("f0_proj", singles(0, 2))
            pe_turn(pe, A, fx, D, "f0_sx")
            pe.wait_ge(S("f0_sxT"), 1)
            V = chan("f0_v", singles(2, 4))
            for c in range(NC):
                ps, w = V.put()
                if w > 0:
                    pe.wait_ge(V.free, w)
                for k in range(CT):
                    ins = pe.matmul(ps[0:P0, k * 128:(k + 1) * 128], F[1][0:D, tcols(c * CT + k)], P("f0_wv"),
                                    start=True, stop=True)
                ins.then_inc(V.full, 1)
            pe.wait_ge(V.free, V.n_put)
            pe_stack(pe, "f0", 1 + E0, lambda s: pe_project(
                pe, A, P("f0_wk") if s == 0 else P("f0_wq", (s - 1) * 128, s * 128), F[1][0:D, :], 128))
            pe.wait_ge(S("f0_vtok"), 1)
            attend_pe(pe, "f0", E0)
            pe.wait_ge(S("f0_gathered"), NB)
            G = chan("f0_oback", singles(0, 4))
            for e in range(E0):
                for c in range(NC):
                    ps, w = G.put()
                    if w > 0:
                        pe.wait_ge(G.free, w)
                    for k in range(CT):
                        ins = pe.transpose(ps[0:P0, k * 128:(k + 1) * 128], O0[e][:, tcols(c * CT + k)], P("ident"))
                    ins.then_inc(G.full, 1)
            pe.wait_ge(S("f0_masked"), 1)
            H = chan("f0_oturn", singles(4, 8))
            for hh in range(2):
                for c in range(NC):
                    ps, w = H.put()
                    if w > 0:
                        pe.wait_ge(H.free, w)
                    for k in range(CT):
                        ins = pe.transpose(ps[:, tcols(k)], ok0[:, c * CT + k, hh * 128:(hh + 1) * 128],
                                           P("ident")[0:P0, 0:P0])
                    ins.then_inc(H.full, 1)
            pe.wait_ge(S("f0_oturned"), 1)
            pe_tokens(pe, chan("f0_gates", singles(0, 4)),
                      [(F[3], P("f0_gate", 0, 16)), (F[4], P("f0_gate", 16, 32))], 16)
            Z = chan("f0_fc", singles(4, 8))
            pe_turn(pe, Z, fx, D, "f0_fx")
            pe.wait_ge(S("f0_fxT"), 1)
            pe_project(pe, Z, P("f0_fc1"), F[5][0:D, :], D)
            pe.wait_ge(S("f0_h1"), 1)
            pe_tokens(pe, chan("f0_fc2", singles(0, 4)), [(F[6][0:D, :], P("f0_fc2"))], D)
            pe_turn(pe, Z, xn, D, "f0_fout")
            pe.wait_ge(S("f0_foutT"), 1)
            pe_tokens(pe, chan("f0_fg", singles(0, 4)), [(F[7][0:D, :], P("f0_fg"))], 4)

        def ffn0_act(act):
            A = chan("f0_proj", None)
            act_empty(act, A, F[1], D, signal="f0_sxT")

            def fill(s):
                act_empty(act, A, part_x("f0", s), 128, scale=4.0 if s == 0 else 1.0)
                act.drain()

            act_stack(act, "f0", 1 + E0, fill)
            act_table(act, ACT.Exp)
            attend_act(act, "f0", E0)
            H = chan("f0_oturn", None)
            act_empty(act, H, F[3], 128)
            act_empty(act, H, F[4], 128, signal="f0_oturned")
            act_softmax(act, lg2[:, :, :], "f0_gs")
            act_norm(act, T * 4, "f0_ln")
            Z = chan("f0_fc", None)
            act_empty(act, Z, F[5], D, signal="f0_fxT")
            act_empty(act, Z, F[6], D, func=ACT.Relu, bias=P("f0_fc1b"), signal="f0_h1r")
            act_norm(act, T * 4, "f0_fn")
            act_empty(act, Z, F[7], D, signal="f0_foutT")
            act_softmax(act, lg2[:, :, 0:4], "f0_fgs")

        def ffn0_dve(dve, it):
            dve.tensor_copy(fx[:, :, :], sx_all[:, bass.ds(it * T, T), :])
            dve.drain().then_inc(S("f0_sx"), 1)
            dve.tensor_scalar(pad0[:, :, :], fx[:, :, :], 0.0, None, ALU.not_equal)
            V = chan("f0_v", None)
            for c in range(NC):
                ps, w = V.get()
                dve.wait_ge(V.full, w)
                dve.tensor_tensor(vtok[:, c * CT:(c + 1) * CT, :], ps[0:P0, 0:CT * 128].rearrange("p (t n) -> p t n", n=128),
                                  bt(P("ones_col"), CT), ALU.add).then_inc(V.free, 1)
            dve.drain().then_inc(S("f0_vtok"), 1)
            dve_stack(dve, "f0", 1 + E0)
            attend_dve(dve, "f0", O0, E0)
            G = chan("f0_oback", None)
            ov = ok0[:, :, :].rearrange("p t (n e d) -> p t n e d", n=NH, e=E0)
            for e in range(E0):
                for c in range(NC):
                    ps, w = G.get()
                    dve.wait_ge(G.full, w)
                    pv = ps[0:P0, 0:CT * 128].rearrange("p (t n d) -> p t n d", n=NH, d=32)
                    ts = slice(c * CT, (c + 1) * CT)
                    dve.reciprocal(rl[:, ts, :], pv[:, :, :, HD])
                    dve.drain()
                    dve.tensor_tensor(ov[:, ts, :, e, :], pv[:, :, :, 0:HD], bc(rl[:, ts, :], HD), ALU.mult).then_inc(G.free, 1)
                    dve.drain()
            o3 = ok0[:, :, :].rearrange("p t (n e d) -> p (t n) e d", n=NH, e=E0)
            p3 = pad0[:, :, :].rearrange("p t (n d) -> p (t n) d", n=NH)
            dve.tensor_tensor(o3, o3, p3.unsqueeze(2).broadcast_to([P0, T * NH, E0, HD]), ALU.mult).then_inc(S("f0_masked"), 1)
            Gt = chan("f0_gates", None)
            for b in range(NB):
                ps, w = Gt.get()
                dve.wait_ge(Gt.full, w)
                dve.tensor_tensor(lg[:, tiles(b), :], tok(ps, 16), bt(P("f0_gateb"), TB), ALU.add).then_inc(Gt.free, 1)
            dve.drain()
            l3 = lg[:, :, :].rearrange("p t (n e) -> p (t n) e", e=E0)
            g3 = lg2[:, :, :].rearrange("p t (n e) -> p (t n) e", e=E0)
            dve_softmax(dve, l3, g3, T * NH, E0, "f0_gs")
            dve.drain()
            q3 = gk0[:, :, :].rearrange("p t (n e d) -> p (t n) e d", n=NH, e=E0)
            dve.tensor_tensor(q3, o3, bc(g3, HD), ALU.mult)
            dve.drain()
            f3 = fx[:, :, :].rearrange("p t (n d) -> p (t n) d", n=NH)
            dve.tensor_reduce(f3, q3.rearrange("p t e d -> p t d e"), AX.X, ALU.add)
            dve.drain()
            for b in range(NB):
                for n in range(NH):
                    hs = slice(n * HD, (n + 1) * HD)
                    dve.tensor_tensor(fx[:, tiles(b), hs], fx[:, tiles(b), hs], sx_all[:, n * TB:(n + 1) * TB, hs], ALU.add)
            dve.drain()
            dve_norm(dve, f3, f3, T * NH, HD, 1e-8, "f0_ln")
            dve.drain()
            dve.tensor_tensor(fx[:, :, :], fx[:, :, :], bt(P("f0_lng"), T), ALU.mult)
            dve.drain()
            dve.tensor_tensor(fx[:, :, :], fx[:, :, :], bt(P("f0_lnb"), T), ALU.add)
            dve.drain().then_inc(S("f0_fx"), 1)
            dve.tensor_scalar(pad0[:, :, :], fx[:, :, :], 0.0, None, ALU.not_equal)
            dve.wait_ge(S("f0_fxT"), 1)
            dve.tensor_scalar(F[8][0:D, :], F[5][0:D, :], 0.0, None, ALU.not_equal)
            dve.wait_ge(S("f0_h1r"), 1)
            dve.drain()
            dve.tensor_tensor(F[6][0:D, :], F[6][0:D, :], F[8][0:D, :], ALU.mult).then_inc(S("f0_h1"), 1)
            Y = chan("f0_fc2", None)
            for b in range(NB):
                ps, w = Y.get()
                dve.wait_ge(Y.full, w)
                dve.tensor_tensor(xn[:, tiles(b), :], tok(ps, D), bt(P("f0_fc2b"), TB), ALU.add).then_inc(Y.free, 1)
            dve.drain()
            dve.tensor_tensor(xn[:, :, :], xn[:, :, :], pad0[:, :, :], ALU.mult)
            dve.drain()
            dve.tensor_tensor(xn[:, :, :], xn[:, :, :], fx[:, :, :], ALU.add)
            dve.drain()
            x3 = xn[:, :, :].rearrange("p t (n d) -> p (t n) d", n=NH)
            dve_norm(dve, x3, x3, T * NH, HD, 1e-8, "f0_fn")
            dve.drain()
            dve.tensor_tensor(xn[:, :, :], xn[:, :, :], bt(P("f0_fng"), T), ALU.mult)
            dve.drain()
            dve.tensor_tensor(xn[:, :, :], xn[:, :, :], bt(P("f0_fnb"), T), ALU.add)
            dve.drain().then_inc(S("f0_fout"), 1)
            Y = chan("f0_fg", None)
            for b in range(NB):
                ps, w = Y.get()
                dve.wait_ge(Y.full, w)
                dve.tensor_copy(lg[:, tiles(b), 0:4], tok(ps, 4)).then_inc(Y.free, 1)
            dve.drain()
            dve_softmax(dve, lg[:, :, 0:4], lg2[:, :, 0:4], T, 4, "f0_fgs")
            dve.drain()
            for n in range(NH):
                hs = slice(n * HD, (n + 1) * HD)
                dve.tensor_tensor(xn[:, :, hs], xn[:, :, hs], bc(lg2[:, :, n], HD), ALU.mult)
            dve.drain()
            dve.tensor_tensor(h[:, :, :], h[:, :, :], xn[:, :, :], ALU.add)
            dve.drain()


        def pe_back(pe, A, src, rows, n, ready):
            pe.wait_ge(S(ready), 1)
            for b in range(NB):
                ps, w = A.put()
                if w > 0:
                    pe.wait_ge(A.free, w)
                for j in range(TB):
                    ins = pe.transpose(ps[0:P0, j * n:(j + 1) * n], src[0:rows, tcols(b * TB + j)],
                                       P("ident")[0:rows, 0:rows])
                ins.then_inc(A.full, 1)

        def attn1_pe(pe):
            A = chan("a1_proj", singles(0, 4))
            pe_turn(pe, A, xn, D, "a1_normed")
            pe.wait_ge(S("a1_xT"), 1)
            pe_project(pe, A, P("a1_Wx", 0, 128), F[0][0:D, :], 128)
            pe_project(pe, A, P("a1_Wx", 128, 256), F[0][0:D, :], 128)
            V = chan("a1_xm_tok", singles(4, 8))
            for t in range(T):
                ps, w = V.put()
                if w > 0:
                    pe.wait_ge(V.free, w)
                pe.matmul(ps[0:P0, 0:256], F[0][0:D, tcols(t)], P("a1_Wx"), start=True, stop=True).then_inc(V.full, 1)
            pe.wait_ge(S("a1_xm"), 1)
            pe.wait_ge(V.free, V.n_put)
            Q = chan("a1_qk", singles(4, 8))
            for c in range(NC):
                ps, w = Q.put()
                if w > 0:
                    pe.wait_ge(Q.free, w)
                pe.matmul(ps[0:64, 0:CH], P("a1_qk", 0, 64), F[1][:, cols(c)], start=True, stop=False)
                pe.matmul(ps[0:64, 0:CH], P("a1_qk", 64, 128), F[2][:, cols(c)], start=False, stop=True).then_inc(Q.full, 1)
            G = chan("a1_back", singles(0, 2))
            pe_back(pe, G, F[4], 64, 64, "a1_kexp")
            pe.wait_ge(S("a1_ktok"), 1)
            K = chan("a1_kx", singles(2, 4))
            U = chan("a1_attn", singles(0, 2))
            for b in range(NB):
                ps, w = K.put()
                if w > 0:
                    pe.wait_ge(K.free, w)
                for j in range(TB):
                    t = b * TB + j
                    ins = pe.matmul(ps[0:32, 0:256], ktok[:, t, :], otok[:, t, :], start=(j == 0), stop=(j == TB - 1))
                ins.then_inc(K.full, 1)
                pe.wait_ge(S("a1_kxm"), b + 1)
                ps, w = K.put()
                if w > 0:
                    pe.wait_ge(K.free, w)
                for k in range(2):
                    ins = pe.transpose(ps[:, 32 * k:32 * k + 32], kxm[:, 128 * k:128 * k + 128], P("ident")[0:32, 0:32])
                ins.then_inc(K.full, 1)
                pe.wait_ge(S("a1_kvs"), b + 1)
                ps, w = K.put()
                if w > 0:
                    pe.wait_ge(K.free, w)
                ins = pe.matmul(ps[:, 0:64], P("a1_Wv"), kvs[:, :, :].rearrange("p t r -> p (t r)"), start=True, stop=True)
                ins.then_inc(K.full, 1)
                pe.wait_ge(S("a1_kvs2"), b + 1)
                ps, w = K.put()
                if w > 0:
                    pe.wait_ge(K.free, w)
                for k in range(2):
                    ins = pe.matmul(ps[0:32, 0:64], kvs2[:, k, :], P("a1_Wo", 64 * k, 64 * k + 64), start=(k == 0), stop=(k == 1))
                ins.then_inc(K.full, 1)
                if b == 0:
                    Z = chan("a1_q", singles(4, 8))
                    pe.wait_ge(S("a1_qsoft"), 1)
                    pe.wait_ge(Q.free, Q.n_put)
                    for c in range(NC):
                        zs, w = Z.put()
                        if w > 0:
                            pe.wait_ge(Z.free, w)
                        for k in range(CT):
                            ins = pe.transpose(zs[0:32, tcols(k)], qtok[:, c * CT + k, :], P("ident")[0:P0, 0:P0])
                        ins.then_inc(Z.full, 1)
                    pe.wait_ge(S("a1_qT"), 1)
                    pe.wait_ge(G.free, G.n_put)
                pe.wait_ge(S("a1_M"), b + 1)
                us, w = U.put()
                if w > 0:
                    pe.wait_ge(U.free, w)
                for j in range(TB):
                    ins = pe.matmul(us[0:P0, j * D:(j + 1) * D], F[5][0:32, tcols(b * TB + j)], Mh, start=True, stop=True)
                ins.then_inc(U.full, 1)
            M = chan("a1_mlp", singles(2, 6))
            pe.wait_ge(Z.free, Z.n_put)
            pe.wait_ge(K.free, K.n_put)
            pe_turn(pe, M, xn, D, "a1_n2")
            pe.wait_ge(S("a1_x2T"), 1)
            pe_project(pe, M, P("a1_W1", 0, 128), F[0][0:D, :], 128)
            pe_project(pe, M, P("a1_W1", 128, 256), F[0][0:D, :], 128)
            pe.wait_ge(S("a1_gelu"), 1)
            pe_tokens(pe, chan("a1_out", singles(6, 8)), [(F[1], P("a1_W2", 0, 64)), (F[2], P("a1_W2", 64, 128))], D)

        def attn1_act(act):
            act_norm(act, T, "a1_x")
            act_norm(act, T, "a1_n", ACT.Exp)
            A = chan("a1_proj", None)
            act_empty(act, A, F[0], D, scale=P("a1_g1"), bias=P("a1_b1"), signal="a1_xT")
            act_empty(act, A, F[1], 128, bias=P("a1_bx", 0, 1))
            act_empty(act, A, F[2], 128, bias=P("a1_bx", 1, 2), signal="a1_xm")
            act.wait_ge(S("a1_kmax"), 1)
            for b in range(NB):
                act.activation(F[4][32:64, b * LB:b * LB + L], F[3][32:64, b * LB:b * LB + L], ACT.Exp,
                               bias=ksm[32:64, b:b + 1], accum_out=ksm[32:64, 4 + b:5 + b])
            act.activation(F[4][0:32, :], F[3][0:32, :], ACT.Identity)
            act.drain().then_inc(S("a1_ke"), 1)
            act_softmax(act, qtok.rearrange("p t (h r) -> p (t h) r", r=4), "a1_qs")
            Z = chan("a1_q", None)
            act_empty(act, Z, F[5], 32, signal="a1_qT")
            act_norm(act, T, "a1_m", ACT.Gelu)
            M = chan("a1_mlp", None)
            act_empty(act, M, F[0], D, scale=P("a1_g2"), bias=P("a1_b2"), signal="a1_x2T")
            act_empty(act, M, F[1], 128, func=ACT.Gelu, bias=P("a1_W1b", 0, 1))
            act_empty(act, M, F[2], 128, func=ACT.Gelu, bias=P("a1_W1b", 1, 2), signal="a1_gelu")

        def attn1_dve(dve):
            dve_norm(dve, h[:, :, :], Xs, T, D, 1e-5, "a1_x")
            dve.drain()
            dve_norm(dve, Xs, xn[:, :, :], T, D, 1e-5, "a1_n").then_inc(S("a1_normed"), 1)
            V = chan("a1_xm_tok", None)
            for t in range(T):
                ps, w = V.get()
                dve.wait_ge(V.full, w)
                dve.tensor_tensor(otok[:, t, :], ps[0:P0, 0:256], P("a1_bx_bc"), ALU.add).then_inc(V.free, 1)
            Q = chan("a1_qk", None)
            for c in range(NC):
                ps, w = Q.get()
                dve.wait_ge(Q.full, w)
                dve.tensor_copy(F[3][0:64, cols(c)], ps[0:64, 0:CH]).then_inc(Q.free, 1)
            dve.drain()
            for b in range(NB):
                dve.tensor_reduce(ksm[32:64, 2 + b:3 + b], F[3][32:64, b * LB:b * LB + L], AX.X, ALU.max)
            dve.drain()
            dve.tensor_scalar(ksm[32:64, 0:NB], ksm[32:64, 2:2 + NB], -1.0, None, ALU.mult).then_inc(S("a1_kmax"), 1)
            dve.wait_ge(S("a1_ke"), 1)
            dve.reciprocal(ksm[32:64, 6:6 + NB], ksm[32:64, 4:4 + NB])
            dve.drain()
            for b in range(NB):
                dve.memset(F[4][32:64, b * LB + L:(b + 1) * LB], 0.0)
                ins = dve.tensor_scalar(F[4][32:64, b * LB:b * LB + L], F[4][32:64, b * LB:b * LB + L],
                                        ksm[32:64, 6 + b:7 + b], None, ALU.mult)
            dve.drain().then_inc(S("a1_kexp"), 1)
            G = chan("a1_back", None)
            for b in range(NB):
                ps, w = G.get()
                dve.wait_ge(G.full, w)
                pv = tok(ps, 64)
                dve.tensor_copy(qtok[:, tiles(b), :], pv[:, :, 0:32])
                dve.tensor_copy(ktok[:, tiles(b), :], pv[:, :, 32:64]).then_inc(G.free, 1)
            dve.drain().then_inc(S("a1_ktok"), 1)
            q3 = qtok.rearrange("p t (h r) -> p (t h) r", r=4)
            dve_softmax(dve, q3, q3, T * 8, 4, "a1_qs").then_inc(S("a1_qsoft"), 1)
            K = chan("a1_kx", None)
            U = chan("a1_attn", None)
            for b in range(NB):
                ps, w = K.get()
                dve.wait_ge(K.full, w)
                if b >= 1:
                    dve.drain()
                dve.tensor_tensor(kxm, ps[0:32, 0:256], P("a1_blk"), ALU.mult).then_inc(K.free, 1)
                dve.drain().then_inc(S("a1_kxm"), 1)
                ps, w = K.get()
                dve.wait_ge(K.full, w)
                dve.tensor_copy(kvs.rearrange("p t r -> p (t r)"), ps[:, 0:64]).then_inc(K.free, 1)
                dve.drain().then_inc(S("a1_kvs"), 1)
                ps, w = K.get()
                dve.wait_ge(K.full, w)
                dve.tensor_copy(kvs2.rearrange("p t r -> p (t r)"), ps[:, 0:64]).then_inc(K.free, 1)
                dve.drain().then_inc(S("a1_kvs2"), 1)
                ps, w = K.get()
                dve.wait_ge(K.full, w)
                dve.tensor_copy(Mh, ps[0:32, 0:64]).then_inc(K.free, 1)
                dve.drain().then_inc(S("a1_M"), 1)
                ps, w = U.get()
                dve.wait_ge(U.full, w)
                dve.tensor_tensor(fx[:, tiles(b), :], tok(ps, D), bt(P("a1_bo"), TB), ALU.add).then_inc(U.free, 1)
            dve.drain()
            dve.tensor_tensor(fx[:, :, :], fx[:, :, :], Xs, ALU.add)
            dve.drain()
            dve_norm(dve, fx[:, :, :], xn[:, :, :], T, D, 1e-5, "a1_m").then_inc(S("a1_n2"), 1)
            dve.tensor_tensor(h[:, :, :], h[:, :, :], fx[:, :, :], ALU.add)
            dve.drain()
            dve.tensor_tensor(h[:, :, :], h[:, :, :], bt(P("a1_W2b"), T), ALU.add)
            dve.drain()
            dve_residual(dve, "a1_out")


        def top2_dve(dve, v):
            rev = bt(P("rev"), T)
            cur = v
            for n in range(2):
                m, c = r8[n][:, :], r8[2][:, :]
                dve.tensor_reduce(m, cur, AX.X, ALU.max)
                dve.drain()
                dve.tensor_tensor(eqb[2][:, :, :], cur, bc(m, 8), ALU.is_equal)
                dve.drain()
                dve.tensor_tensor(eqb[2][:, :, :], eqb[2][:, :, :], rev, ALU.mult)
                dve.drain()
                dve.tensor_reduce(c, eqb[2][:, :, :], AX.X, ALU.max)
                dve.drain()
                dve.tensor_tensor(eqb[n][:, :, :], rev, bc(c, 8), ALU.is_equal)
                dve.drain()
                if n == 0:
                    dve.scalar_tensor_tensor(out=eqb[3][:, :, :], in0=eqb[0][:, :, :], scalar=MASKED, in1=v,
                                             op0=ALU.mult, op1=ALU.add)
                    dve.drain()
                    cur = eqb[3][:, :, :]

        def spread_weights_dve(dve, signal):
            dve.memset(W96, 0.0)
            dve.tensor_tensor(eqb[2][:, :, :], eqb[0][:, :, :], bc(r8[3][:, :], 8), ALU.mult)
            dve.tensor_tensor(eqb[3][:, :, :], eqb[1][:, :, :], bc(r8[4][:, :], 8), ALU.mult)
            dve.drain()
            for j in range(3):
                dve.tensor_tensor(W96[:, :, 32 * j:32 * j + 8], eqb[2][:, :, :], eqb[3][:, :, :], ALU.add)
            dve.drain().then_inc(S(signal), 1)

        def split_rows_dve(dve, src, tmp, ready, signal, n=1):
            dve.wait_ge(S(ready), n)
            r = slice(0, 96)
            dve.tensor_copy(Hb[0][r, :], src[r, :])
            dve.drain()
            dve.scalar_tensor_tensor(out=tmp[r, :], in0=Hb[0][r, :], scalar=P("split1"), in1=src[r, :], op0=ALU.mult, op1=ALU.add)
            dve.drain()
            dve.tensor_copy(Hb[1][r, :], tmp[r, :])
            dve.drain()
            dve.scalar_tensor_tensor(out=tmp[r, :], in0=Hb[1][r, :], scalar=P("split2"), in1=tmp[r, :], op0=ALU.mult, op1=ALU.add)
            dve.drain()
            dve.tensor_copy(Hb[2][r, :], tmp[r, :])
            dve.drain().then_inc(S(signal), 1)

        def split_doubled_dve(dve, signal):
            upper, lower = P("minus64", 0, 1), P("minus64", 1, 2)
            x, r = F[0], F[4]
            dve.tensor_copy(Hb[0][:, :], x[:, :])
            dve.drain()
            dve.scalar_tensor_tensor(out=r, in0=Hb[0][:, :], scalar=upper, in1=x[:, :], op0=ALU.mult, op1=ALU.add)
            dve.scalar_tensor_tensor(out=Xa, in0=Hb[0][:, :], scalar=lower, in1=x[:, :], op0=ALU.mult, op1=ALU.add)
            dve.drain()
            dve.tensor_copy(Hb[1][:, :], r[:, :])
            dve.drain()
            dve.scalar_tensor_tensor(out=Xb, in0=Hb[1][:, :], scalar=upper, in1=r[:, :], op0=ALU.mult, op1=ALU.add)
            dve.drain().then_inc(S(signal), 1)

        def pe_up(pe, out, o, c):
            pe.matmul(out, EW[:, 0, o:o + 128], Xa[:, cols(c)], start=True, stop=False)
            pe.matmul(out, EW[:, 1, o:o + 128], Xa[:, cols(c)], start=False, stop=False)
            return pe.matmul(out, EW[:, 2, o:o + 128], Xb[:, cols(c)], start=False, stop=True)

        def experts_pe(pe, tag, n, w1, w3, sel, w2, b2):
            CA = chan(f"{tag}_up", singles(0, 2))
            CB = chan(f"{tag}_side", singles(2, 6))
            CY = chan(f"{tag}_y", singles(6, 8))
            for k in range(n * NC + 2):
                if k < n * NC:
                    c, t = divmod(k, n)
                    ps, w = CA.put()
                    if w > 0:
                        pe.wait_ge(CA.free, w)
                    pe_up(pe, ps[:, 0:CH], w1 + t * 128, c).then_inc(CA.full, 1)
                    if w3 is not None:
                        ps, w = CB.put()
                        if w > 0:
                            pe.wait_ge(CB.free, w)
                        pe_up(pe, ps[:, 0:CH], w3 + t * 128, c).then_inc(CB.full, 1)
                    ps, w = CB.put()
                    if w > 0:
                        pe.wait_ge(CB.free, w)
                    pe.matmul(ps[:, 0:CH], sel[:, t * 128:(t + 1) * 128], Hb[2][0:96, cols(c)], start=True, stop=True).then_inc(CB.full, 1)
                if k >= 2:
                    i = k - 2
                    c, t = divmod(i, n)
                    if t == 0:
                        y, w = CY.put()
                        if w > 0:
                            pe.wait_ge(CY.free, w)
                    pe.wait_ge(S(f"{tag}_hidden"), i + 1)
                    for j in range(CT):
                        yj = y[0:P0, j * D:(j + 1) * D]
                        ins = pe.matmul(yj, HH[i % 3][:, tcols(j)], P(w2, t * D, t * D + D),
                                        start=(t == 0 and j == 0), stop=True, skip_group_check=True)
                        if b2 and t == n - 1:
                            pe.matmul(yj, F[1][0:8, tcols(c * CT + j)], P(b2), start=False, stop=True, skip_group_check=True)
                    ins.then_inc(S(f"{tag}_hidden_used"), 1)
                    if t == n - 1:
                        pe.drain().then_inc(CY.full, 1)

        def experts_act(act, tag, n, func, bias):
            CA = chan(f"{tag}_up", None)
            for k in range(n * NC):
                ps, w = CA.get()
                act.wait_ge(CA.full, w)
                if k >= 3:
                    act.wait_ge(S(f"{tag}_act_used"), k - 2)
                act.activation(SAr[k % 3], ps[:, 0:CH], func, bias=P(bias, k % n, k % n + 1) if bias else 0.0).then_inc(CA.free, 1)
                act.drain().then_inc(S(f"{tag}_act"), 1)

        def experts_dve(dve, tag, n, gated):
            CB = chan(f"{tag}_side", None)
            CY = chan(f"{tag}_y", None)
            for k in range(n * NC):
                dve.wait_ge(S(f"{tag}_act"), k + 1)
                src = SAr[k % 3]
                if gated:
                    ps, w = CB.get()
                    dve.wait_ge(CB.full, w)
                    dve.tensor_tensor(SAr[k % 3], SAr[k % 3], ps[:, 0:CH], ALU.mult).then_inc(CB.free, 1)
                    dve.drain()
                ps, w = CB.get()
                dve.wait_ge(CB.full, w)
                if k >= 3:
                    dve.wait_ge(S(f"{tag}_hidden_used"), k - 2)
                dve.tensor_tensor(HH[k % 3], SAr[k % 3], ps[:, 0:CH], ALU.mult).then_inc(CB.free, 1)
                dve.drain().then_inc(S(f"{tag}_hidden"), 1)
                dve.sem_inc(S(f"{tag}_act_used"), 1)
                if k % n == n - 1:
                    c = k // n
                    ps, w = CY.get()
                    dve.wait_ge(CY.full, w)
                    ts = slice(c * CT, (c + 1) * CT)
                    dve.tensor_tensor(h[:, ts, :], h[:, ts, :], ps[0:P0, 0:CT * D].rearrange("p (t n) -> p t n", n=D),
                                      ALU.add).then_inc(CY.free, 1)
            dve.drain()

        def ffn1_pe(pe):
            A = chan("f1_proj", singles(0, 2))
            R = chan("f1_rot", pairs(2, 6))
            V = chan("f1_v", singles(6, 8))
            pe.matmul(PS[0:64, 6, 0:128], P("f1_wq_r"), P("rot_q"), start=True, stop=True)
            pe.matmul(PS[0:64, 7, 0:128], P("f1_wk_r"), P("rot_k"), start=True, stop=True).then_inc(S("f1_wrot"), 1)
            pe_turn(pe, A, xn, D, "f1_normed")
            pe.wait_ge(S("f1_xT"), 1)
            pe.wait_ge(S("f1_wr"), 1)
            for plain, rot in ((P("f1_wk"), wrk), (P("f1_wq"), wrq)):
                for c in range(NC):
                    ps, w = R.put()
                    if w > 0:
                        pe.wait_ge(R.free, w)
                    pe.matmul(ps[:, 0, 0:CH], plain, F[0][0:D, cols(c)], start=True, stop=True)
                    pe.matmul(ps[:, 1, 0:CH], rot, F[0][0:D, cols(c)], start=True, stop=True).then_inc(R.full, 1)
            for c in range(NC):
                ps, w = V.put()
                if w > 0:
                    pe.wait_ge(V.free, w)
                for k in range(CT):
                    ins = pe.matmul(ps[0:P0, k * 128:(k + 1) * 128], F[0][0:D, tcols(c * CT + k)], P("f1_wv"), start=True, stop=True)
                ins.then_inc(V.full, 1)
            pe.wait_ge(V.free, V.n_put)
            pe.wait_ge(R.free, R.n_put)
            pe_stack(pe, "f1", 2, lambda s: None)
            pe.wait_ge(S("f1_vtok"), 1)
            attend_pe(pe, "f1", 1)
            pe.wait_ge(S("f1_gathered"), NB)
            G = chan("f1_oback", singles(0, 4))
            for c in range(NC):
                ps, w = G.put()
                if w > 0:
                    pe.wait_ge(G.free, w)
                for k in range(CT):
                    ins = pe.transpose(ps[0:P0, k * 128:(k + 1) * 128], O0[0][:, tcols(c * CT + k)], P("ident"))
                ins.then_inc(G.full, 1)
            H = chan("f1_turn", singles(4, 6))
            pe_turn(pe, H, fx, D, "f1_y")
            pe.wait_ge(S("f1_yT"), 1)
            pe.wait_ge(G.free, G.n_put)
            pe_tokens(pe, chan("f1_wo", singles(0, 2)), [(F[8][0:D, :], P("f1_wo"))], D)
            pe_turn(pe, H, x2tok, 128, "f1_n2")
            pe.wait_ge(S("f1_x2T"), 1)
            pe_tokens(pe, chan("f1_rt", singles(2, 4)), [(F[0][0:D, :], P("f1_rt"))], 8)
            pe_turn(pe, H, W96, 96, "f1_w96")
            pe.wait_ge(S("f1_xsplit"), 1)
            pe.wait_ge(S("f1_wsplit"), 1)
            pe.wait_ge(ups_split, 1)
            experts_pe(pe, "f1e", KT1, UP1, UP3, selmoe, "f1_w2", None)

        def ffn1_act(act):
            act_norm(act, T, "f1_x")
            act_norm(act, T, "f1_n")
            act.wait_ge(S("f1_wrot"), 1)
            act.activation(wrq, PS[0:64, 6, 0:128], ACT.Identity)
            act.activation(wrk, PS[0:64, 7, 0:128], ACT.Identity)
            act.drain().then_inc(S("f1_wr"), 1)
            A = chan("f1_proj", None)
            act_empty(act, A, F[0], D, scale=P("f1_ln1"), signal="f1_xT")

            def fill(s):
                act.wait_ge(S("f1_rotated"), s + 1)
                if s == 0:
                    act.activation(part_x("f1", 0), part_x("f1", 0), ACT.Identity, scale=0.25)
                    act.drain().then_inc(S("f1_scaled"), 1)

            act_stack(act, "f1", 2, fill)
            act_table(act, ACT.Exp)
            attend_act(act, "f1", 1)
            H = chan("f1_turn", None)
            act_empty(act, H, F[8], D, signal="f1_yT")
            act_norm(act, T, "f1_m")
            act_empty(act, H, F[0], 128, scale=P("f1_ln2"), signal="f1_x2T")
            act_softmax(act, lg2[:, :, 0:8], "f1_ps")
            act_table(act, ACT.Silu)
            act_empty(act, H, F[1], 96, signal="f1_w96T")
            experts_act(act, "f1e", KT1, ACT.Silu, None)

        def ffn1_dve(dve):
            dve_norm(dve, h[:, :, :], Xs, T, D, 1e-5, "f1_x")
            dve.drain()
            dve_norm(dve, Xs, xn[:, :, :], T, D, 1e-6, "f1_n", centre=False).then_inc(S("f1_normed"), 1)
            R = chan("f1_rot", None)
            for s in range(2):
                for c in range(NC):
                    ps, w = R.get()
                    dve.wait_ge(R.full, w)
                    cs = slice((c % 2) * CH, (c % 2 + 1) * CH)
                    dve.tensor_tensor(F[1][:, cols(c)], ps[:, 0, 0:CH], P("cos")[:, cs], ALU.mult)
                    dve.tensor_tensor(F[2][:, cols(c)], ps[:, 1, 0:CH], P("sin")[:, cs], ALU.mult).then_inc(R.free, 1)
                dve.drain()
                dve.tensor_tensor(part_x("f1", s), F[1][:, :], F[2][:, :], ALU.add).then_inc(S("f1_rotated"), 1)
                dve.drain()
            V = chan("f1_v", None)
            for c in range(NC):
                ps, w = V.get()
                dve.wait_ge(V.full, w)
                dve.tensor_tensor(vtok[:, c * CT:(c + 1) * CT, :], ps[0:P0, 0:CT * 128].rearrange("p (t n) -> p t n", n=128),
                                  bt(P("ones_col"), CT), ALU.add).then_inc(V.free, 1)
            dve.drain().then_inc(S("f1_vtok"), 1)
            dve.wait_ge(S("f1_scaled"), 1)
            dve_stack(dve, "f1", 2)
            attend_dve(dve, "f1", O0, 1)
            G = chan("f1_oback", None)
            for c in range(NC):
                ps, w = G.get()
                dve.wait_ge(G.full, w)
                pv = ps[0:P0, 0:CT * 128].rearrange("p (t n d) -> p t n d", n=NH, d=32)
                ts = slice(c * CT, (c + 1) * CT)
                dve.reciprocal(rl[:, ts, :], pv[:, :, :, HD])
                dve.drain()
                dve.tensor_tensor(fx[:, ts, :].rearrange("p t (n d) -> p t n d", n=NH), pv[:, :, :, 0:HD],
                                  bc(rl[:, ts, :], HD), ALU.mult).then_inc(G.free, 1)
            dve.drain().then_inc(S("f1_y"), 1)
            Y = chan("f1_wo", None)
            for b in range(NB):
                ps, w = Y.get()
                dve.wait_ge(Y.full, w)
                dve.tensor_tensor(X[:, tiles(b), 0:D], X[:, tiles(b), 0:D], tok(ps, D), ALU.add).then_inc(Y.free, 1)
            dve.drain()
            dve_norm(dve, Xs, xn[:, :, :], T, D, 1e-6, "f1_m", centre=False)
            dve.drain()
            dve.tensor_copy(twice(x2tok), xn[:, :, :].unsqueeze(2).broadcast_to([P0, T, 2, D])).then_inc(S("f1_n2"), 1)
            dve.tensor_tensor(h[:, :, :], h[:, :, :], Xs, ALU.add)
            Y = chan("f1_rt", None)
            for b in range(NB):
                ps, w = Y.get()
                dve.wait_ge(Y.full, w)
                dve.tensor_copy(lg[:, tiles(b), 0:8], tok(ps, 8)).then_inc(Y.free, 1)
            dve.drain()
            pr = lg2[:, :, 0:8]
            dve_softmax(dve, lg[:, :, 0:8], pr, T, 8, "f1_ps")
            dve.drain()
            top2_dve(dve, pr)
            dve.tensor_tensor(r8[2][:, :], r8[0][:, :], r8[1][:, :], ALU.add)
            dve.drain()
            dve.tensor_scalar(r8[2][:, :], r8[2][:, :], 1e-9, None, ALU.add)
            dve.drain()
            dve.reciprocal(r8[5][:, :], r8[2][:, :])
            dve.drain()
            dve.tensor_tensor(r8[3][:, :], r8[0][:, :], r8[5][:, :], ALU.mult)
            dve.tensor_tensor(r8[4][:, :], r8[1][:, :], r8[5][:, :], ALU.mult)
            dve.drain()
            spread_weights_dve(dve, "f1_w96")
            dve.wait_ge(S("f1_x2T"), 1)
            split_doubled_dve(dve, "f1_xsplit")
            split_rows_dve(dve, F[1], F[2], "f1_w96T", "f1_wsplit")
            experts_dve(dve, "f1e", KT1, True)


        QA, QB = (F[5].bitcast(BF16)[:, i * LB:(i + 1) * LB] for i in range(2))
        KA, KB = (F[6].bitcast(BF16)[:, i * LB:(i + 1) * LB] for i in range(2))
        KC = F[7].bitcast(BF16)[:, 0:LB]
        TERMS2 = [(QA, KA), (QA, KB), (QB, KC)]

        def attn2_pe(pe):
            A = chan("a2_proj", singles(0, 2))
            pe_turn(pe, A, X, D, "a2_normed")
            pe.wait_ge(S("a2_xT"), 1)
            pe_project(pe, A, P("a2_q"), F[0][0:D, :], 128)
            pe_project(pe, A, P("a2_k"), F[0][0:D, :], 128)
            pe.wait_ge(S("a2_parts"), 1)
            SA = chan("a2_score", pairs(2, 8))
            for t in range(T):
                ps, w = SA.put()
                if w > 0:
                    pe.wait_ge(SA.free, w)
                for m, ko in enumerate((0, L - CH)):
                    for k, (q, key) in enumerate(TERMS2):
                        ins = pe.matmul(ps[0:P0, m, 0:CH], q[:, tcols(t)], key[:, ko:ko + CH], start=(k == 0), stop=(k == 2))
                ins.then_inc(SA.full, 1)
            pe.wait_ge(S("a2_maxima"), 1)
            for c in range(NC):
                ps, w = A.put()
                if w > 0:
                    pe.wait_ge(A.free, w)
                for k in range(CT):
                    ins = pe.matmul(ps[0:3, tcols(k)], M3[:, c * CT + k, 0:3], identb[0:P0, 0:P0], start=True, stop=True)
                ins.then_inc(A.full, 1)
            pe.wait_ge(S("a2_mrow"), 1)
            pe.wait_ge(SA.free, SA.n_put)
            SB = chan("a2_scoreT", pairs(2, 8))
            OC = chan("a2_o", singles(0, 2))
            units = [(c, p) for c in range(NC) for p in range(3)]
            for u in range(len(units) + 2):
                if u < len(units):
                    c, p = units[u]
                    ps, w = SB.put()
                    if w > 0:
                        pe.wait_ge(SB.free, w)
                    for m in range(2):
                        j = 2 * p + m
                        for k, (q, key) in enumerate(TERMS2):
                            pe.matmul(ps[0:P0, m, 0:CH], key[:, tcols(j)], q[:, cols(c)], start=(k == 0), stop=False)
                        ins = pe.matmul(ps[0:P0, m, 0:CH], ones3[:, :], MR[0:3, cols(c)], start=False, stop=True)
                    ins.then_inc(SB.full, 1)
                if u >= 2:
                    i = u - 2
                    c, p = units[i]
                    if p == 0:
                        ob, w = OC.put()
                        if w > 0:
                            pe.wait_ge(OC.free, w)
                    pe.wait_ge(S("a2_probs"), i + 1)
                    for m in range(2):
                        j = 2 * p + m
                        kn = P0 if j < TB - 1 else L - (TB - 1) * P0
                        ins = pe.matmul(ob[0:65, 0:CH], X[0:kn, c // 2 * TB + j, :], PT[i % 3][0:kn, m, :],
                                        start=(j == 0), stop=(j == TB - 1))
                    ins.then_inc(S("a2_probs_used"), 1)
                    if p == 2:
                        pe.drain().then_inc(OC.full, 1)
            pe.wait_ge(S("a2_gathered"), 1)
            pe_back(pe, chan("a2_back", singles(0, 2)), F[3], 65, 65, "a2_gathered")

        def attn2_act(act):
            act_norm(act, T, "a2", ACT.Exp)
            A = chan("a2_proj", None)
            act_empty(act, A, F[0], D, signal="a2_xT")
            act_empty(act, A, F[1], 128)
            act_empty(act, A, F[2], 128, scale=0.125)
            act.drain()
            act.activation(Hb[0][:, :], F[1], ACT.Identity)
            act.activation(KA, F[2], ACT.Identity)
            act.activation(KC[0:D, :], F[2][0:D, :], ACT.Identity)
            act.drain().then_inc(S("a2_high"), 1)
            act_empty(act, A, MR, 3, signal="a2_mrow")
            SB = chan("a2_scoreT", None)
            for k in range(3 * NC):
                ps, w = SB.get()
                act.wait_ge(SB.full, w)
                if k >= 3:
                    act.wait_ge(S("a2_probs_used"), k - 2)
                act.activation(PT[k % 3], ps[0:P0, :, 0:CH], ACT.Exp).then_inc(SB.free, 1)
                act.drain().then_inc(S("a2_probs"), 1)

        def attn2_dve(dve):
            dve_norm(dve, h[:, :, :], Xs, T, D, 1e-5, "a2")
            dve.drain().then_inc(S("a2_normed"), 1)
            upper, lower = P("minus64", 0, 1), P("minus64", 1, 2)
            rq, rk = F[8], F[9]
            dve.wait_ge(S("a2_high"), 1)
            dve.scalar_tensor_tensor(out=rq, in0=Hb[0][:, :], scalar=upper, in1=F[1], op0=ALU.mult, op1=ALU.add)
            dve.scalar_tensor_tensor(out=QA, in0=Hb[0][:, :], scalar=lower, in1=F[1], op0=ALU.mult, op1=ALU.add)
            dve.tensor_tensor(rk, F[2], KA, ALU.subtract)
            dve.drain()
            dve.tensor_copy(Hb[1][:, :], rq)
            dve.tensor_copy(KB, rk)
            dve.drain()
            dve.scalar_tensor_tensor(out=QB, in0=Hb[1][:, :], scalar=upper, in1=rq, op0=ALU.mult, op1=ALU.add)
            dve.tensor_tensor(KC[D:2 * D, :], rk[D:2 * D, :], KB[D:2 * D, :], ALU.subtract)
            dve.drain().then_inc(S("a2_parts"), 1)
            SA = chan("a2_score", None)
            for t in range(T):
                ps, w = SA.get()
                dve.wait_ge(SA.full, w)
                dve.tensor_reduce(r8[0][:, t:t + 1], ps[0:P0, :, 0:CH], AX.XY, ALU.max).then_inc(SA.free, 1)
            dve.drain()
            for i in range(3):
                dve.tensor_scalar(M3[:, :, i], r8[0][:, :], -1.0, None, ALU.mult)
                if i < 2:
                    dve.drain()
                    dve.tensor_tensor(r8[0][:, :], r8[0][:, :], M3[:, :, i], ALU.add)
                    dve.drain()
            dve.drain().then_inc(S("a2_maxima"), 1)
            OC = chan("a2_o", None)
            for c in range(NC):
                ps, w = OC.get()
                dve.wait_ge(OC.full, w)
                dve.tensor_copy(F[3][0:65, cols(c)], ps[0:65, 0:CH]).then_inc(OC.free, 1)
            dve.drain().then_inc(S("a2_gathered"), 1)
            G = chan("a2_back", None)
            for b in range(NB):
                ps, w = G.get()
                dve.wait_ge(G.full, w)
                pv = tok(ps, 65)
                dve.reciprocal(r8[1][:, tiles(b)], pv[:, :, 64])
                dve.drain()
                dve.tensor_tensor(fx[:, tiles(b), :], pv[:, :, 0:64], bc(r8[1][:, tiles(b)], D), ALU.mult).then_inc(G.free, 1)
            dve.drain()
            dve.tensor_tensor(h[:, :, :], h[:, :, :], fx[:, :, :], ALU.add)
            dve.drain()


        def ffn2_pe(pe):
            A = chan("f2_turn", singles(0, 2))
            pe_turn(pe, A, X, D, "f2_normed")
            pe.wait_ge(S("f2_xT"), 1)
            V = chan("f2_logit", singles(2, 4))
            for t in range(T):
                ps, w = V.put()
                if w > 0:
                    pe.wait_ge(V.free, w)
                pe.matmul(ps[0:P0, 0:256], F[0][0:D, tcols(t)], P("f2_w1"), start=True, stop=True).then_inc(V.full, 1)
            pe_turn(pe, A, Ag[:, :, 0:128], 128, "f2_weights")
            pe_turn(pe, A, Ag[:, :, 128:256], 128, None)
            pe.wait_ge(S("f2_aT"), 1)
            pe.wait_ge(V.free, V.n_put)
            pe_tokens(pe, chan("f2_b2", singles(0, 2)), [(F[1], P("f2_b2", 0, 64)), (F[2], P("f2_b2", 64, 128))], D)
            pe.wait_ge(w2_in, 32)
            M = chan("f2_matrix", singles(2, 8))
            for t in range(T):
                for m in range(8):
                    ps, w = M.put()
                    if w > 0:
                        pe.wait_ge(M.free, w)
                    pe.matmul(ps[0:P0, :], F[1][:, tcols(t)], W2N[:, 0, 512 * m:512 * m + 512], start=True, stop=False)
                    pe.matmul(ps[0:P0, :], F[2][0:127, tcols(t)], W2N[0:127, 1, 512 * m:512 * m + 512],
                              start=False, stop=True).then_inc(M.full, 1)

        def ffn2_act(act):
            act_norm(act, T, "f2", ACT.Gelu)
            A = chan("f2_turn", None)
            act_empty(act, A, F[0], D, signal="f2_xT")
            act.wait_ge(S("f2_path"), 1)
            act.activation(Lg[:, :, :], Lg[:, :, :], ACT.Abs)
            act.drain()
            act.activation(Lg[:, :, :], Lg[:, :, :], ACT.Gelu).then_inc(S("f2_gelu"), 1)
            act_empty(act, A, F[1], 128)
            act_empty(act, A, F[2], 128, signal="f2_aT")

        def ffn2_dve(dve):
            dve_norm(dve, h[:, :, :], Xs, T, D, 1e-5, "f2").then_inc(S("f2_normed"), 1)
            dve.memset(Ag[:, :, 0:1], 1.0)
            dve.memset(Ag[:, :, 255:256], 0.0)
            V = chan("f2_logit", None)
            for t in range(T):
                ps, w = V.get()
                dve.wait_ge(V.full, w)
                dve.tensor_tensor(Lg[:, t, :], ps[0:P0, 0:256], P("f2_b1"), ALU.add).then_inc(V.free, 1)
            dve.drain()
            for lv in range(7):
                s, n = 2 ** lv - 1, 2 ** lv
                c0 = 2 * n - 1
                left, right = Ag[:, :, c0:c0 + 2 * n:2], Ag[:, :, c0 + 1:c0 + 2 * n:2]
                dve.scalar_tensor_tensor(out=right, in0=Lg[:, :, s:s + n], scalar=0.0, in1=Ag[:, :, s:s + n],
                                         op0=ALU.is_gt, op1=ALU.mult)
                dve.drain()
                dve.tensor_tensor(left, Ag[:, :, s:s + n], right, ALU.subtract)
                dve.drain()
            dve.sem_inc(S("f2_path"), 1)
            dve.wait_ge(S("f2_gelu"), 1)
            dve.tensor_tensor(Ag[:, :, :], Ag[:, :, :], Lg[:, :, :], ALU.mult).then_inc(S("f2_weights"), 1)
            dve_residual(dve, "f2_b2")
            M = chan("f2_matrix", None)
            for t in range(T):
                pv = prod[t % 2].rearrange("p (d o) -> p d o", o=D)
                if t >= 2:
                    dve.wait_ge(S("f2_summed"), t - 1)
                for m in range(8):
                    ps, w = M.get()
                    dve.wait_ge(M.full, w)
                    ins = dve.tensor_tensor(pv[:, 8 * m:8 * m + 8, :], ps[0:P0, :].rearrange("p (d o) -> p d o", o=D),
                                            bc(X[:, t, 8 * m:8 * m + 8], D), ALU.mult).then_inc(M.free, 1)
                dve.drain().then_inc(S("f2_prod"), 1)
            dve.tensor_reduce(xn[:, T - 1, :], prod[(T - 1) % 2].rearrange("p (d o) -> p o d", o=D), AX.X, ALU.add)
            dve.drain()
            dve.wait_ge(S("f2_summed"), T - 1)
            dve.tensor_tensor(h[:, :, :], h[:, :, :], xn[:, :, :], ALU.add)
            dve.drain()

        def ffn2_pool(pool):
            for t in range(T - 1):
                pool.wait_ge(S("f2_prod"), t + 1)
                n = 2048
                while n > D:
                    pool.tensor_tensor(prod[t % 2][:, 0:n], prod[t % 2][:, 0:n], prod[t % 2][:, n:2 * n], ALU.add)
                    pool.drain()
                    n //= 2
                pool.tensor_tensor(xn[:, t, :], prod[t % 2][:, 0:D], prod[t % 2][:, D:2 * D], ALU.add)\
                    .then_inc(S("f2_summed"), 1)

        A3 = dict(x=F[0], sz=F[1], t=F[2], u=F[3], dl=F[4], y=[F[5], F[8]], a=F[6], delta=F[7], tmp=F[8], bc=F[9], dx=F[10])

        CS = [F[6], F[9]]

        def scan3_pe(pe):
            A = chan("a3_proj", singles(0, 4))
            pe_turn(pe, A, xn, D, "a3_normed")
            pe.wait_ge(S("a3_xT"), 1)
            for di, dn in enumerate("fb"):
                w3 = f"a3{dn}_"
                pe_project(pe, A, P(w3 + "in", 0, 128), A3["x"][0:D, :], 128)
                pe_project(pe, A, P(w3 + "in", 128, 256), A3["x"][0:D, :], 128)
                pe.wait_ge(S("a3_u"), di + 1)
                pe_project(pe, A, P(w3 + "dl"), A3["u"], 4)
                pe_project(pe, A, P(w3 + "bc"), A3["u"], 96)
                pe.wait_ge(S("a3_dl"), di + 1)
                pe_project(pe, A, P(w3 + "dt"), A3["dl"][0:4, :], 128)
                pe.wait_ge(S("a3_split"), di + 1)
                pe.wait_ge(A.free, A.n_put)
                RD = chan(f"a3{dn}_drive", pairs(0, 4))
                RR = chan(f"a3{dn}_reads", pairs(4, 6))
                Y = chan(f"a3{dn}_sum", pairs(6, 8))
                n = DS
                for k in range(n + 3):
                    for i, o, C in ((k, 0, RD), (k - 1, 16, RR)):
                        if 0 <= i < n:
                            ps, w = C.put()
                            if w > 0:
                                pe.wait_ge(C.free, w)
                            for c in range(2):
                                ins = pe.matmul(ps[:, c, 0:CH], selbn[:, (i + o) * 128:(i + o + 1) * 128],
                                                Hb[2][0:96, cols(c)], start=True, stop=True)
                            ins.then_inc(C.full, 1)
                    if k >= 3:
                        i = k - 3
                        if i == 0:
                            y, w = Y.put()
                        pe.wait_ge(S(f"a3{dn}_read"), i + 1)
                        for c in range(2):
                            ins = pe.matmul(y[:, c, 0:CH], P("ident"), RC[i % 2][:, cols(c)], start=(i == 0), stop=(i == n - 1))
                        ins.then_inc(S(f"a3{dn}_summed"), 1)
                        if i == n - 1:
                            pe.drain().then_inc(Y.full, 1)
                if di == 0:
                    pe.wait_ge(S("a3_y"), 1)
            pe.wait_ge(S("a3_y"), 2)
            O = chan("a3_fold", singles(0, 4))
            for c in range(NC):
                ps, w = O.put()
                if w > 0:
                    pe.wait_ge(O.free, w)
                pe.matmul(ps[0:64, 0:CH], P("a3f_out"), A3["y"][0][:, cols(c)], start=True, stop=True)
                pe.matmul(ps[64:128, 0:CH], P("a3b_out"), A3["y"][1][:, cols(c)], start=True, stop=True).then_inc(O.full, 1)
            pe.wait_ge(S("a3_folded"), 1)
            pe_tokens(pe, chan("a3_out", singles(4, 6)), [(F[9], P("a3_fus"))], D)

        def scan3_act(act):
            act_norm(act, T, "a3_x")
            act_norm(act, T, "a3_n", ACT.Silu)
            A = chan("a3_proj", None)
            act_empty(act, A, A3["x"], D, scale=P("a3_g"), bias=P("a3_b"), signal="a3_xT")
            for di, dn in enumerate("fb"):
                w3 = f"a3{dn}_"
                if di == 1:
                    act.wait_ge(S("a3_y"), 1)
                act.wait_ge(S("a3_bordered"), 1)
                for c in range(NC):
                    ps, w = A.get()
                    act.wait_ge(A.full, w)
                    n = CH if c % 2 == 0 else CH - 1
                    o = 3 + (c % 2) * CH
                    act.activation(xsp[:, c // 2, o:o + n], ps[:, 0:n], ACT.Identity).then_inc(A.free, 1)
                act.drain().then_inc(S("a3_xs"), 1)
                act_empty(act, A, A3["sz"], 128, func=ACT.Silu)
                act.wait_ge(S("a3_conv"), di + 1)
                act.activation(A3["u"][:, :], A3["t"][:, :], ACT.Silu, bias=P(w3 + "cb")).then_inc(S("a3_u"), 1)
                act_table(act, ACT.Exp)
                act_empty(act, A, A3["dl"], 4, signal="a3_dl")
                act_empty(act, A, A3["bc"], 96, signal="a3_bc")
                act_empty(act, A, A3["t"], 128, bias=P(w3 + "dtb"))
                act.drain()
                softplus_act(act, A3["t"][:, :], A3["a"][:, :], A3["delta"][:, :], f"a3{dn}_ln")
                act_table(act, ACT.Exp)
                act.wait_ge(S("a3_delta"), di + 1)
                RR = chan(f"a3{dn}_reads", None)
                for k in range(DS + 1):
                    if k < DS:
                        if k >= 2:
                            act.wait_ge(S(f"a3{dn}_scanned"), k - 1)
                        act.activation(RA[k % 2][:, 0:L], A3["delta"][:, 0:L], ACT.Exp,
                                       scale=nA3[:, di, k:k + 1]).then_inc(S(f"a3{dn}_decay"), 1)
                    if k >= 1:
                        i = k - 1
                        ps, w = RR.get()
                        act.wait_ge(RR.full, w)
                        if i >= 2:
                            act.wait_ge(S(f"a3{dn}_read"), i - 1)
                        act.activation(CS[i % 2].rearrange("p (c n) -> p c n", c=2), ps[:, :, 0:CH],
                                       ACT.Identity).then_inc(RR.free, 1)
                if di == 0:
                    act_table(act, ACT.Silu)
            O = chan("a3_fold", None)
            act_empty(act, O, F[9], 128, signal="a3_folded")

        def scan3_pool(pool):
            for dn in "fb":
                for k in range(DS):
                    pool.wait_ge(S(f"a3{dn}_scanned"), k + 1)
                    pool.wait_ge(chan(f"a3{dn}_reads", None).free, k + 1)
                    if k >= 2:
                        pool.wait_ge(S(f"a3{dn}_summed"), k - 1)
                    pool.tensor_tensor(RC[k % 2], RS[k % 2], CS[k % 2], ALU.mult).then_inc(S(f"a3{dn}_read"), 1)

        def scan3_dve(dve):
            dve_norm(dve, h[:, :, :], Xs, T, D, 1e-5, "a3_x")
            dve.drain()
            dve_norm(dve, Xs, xn[:, :, :], T, D, 1e-5, "a3_n").then_inc(S("a3_normed"), 1)
            dve.memset(xsp[:, :, 0:3], 0.0)
            dve.memset(xsp[:, :, 3 + L:LB + 6], 0.0)
            for z in RS:
                dve.memset(z[:, L:LB], 0.0)
            dve.drain().then_inc(S("a3_bordered"), 1)
            for di, dn in enumerate("fb"):
                w3 = f"a3{dn}_"
                v2 = lambda z: z.rearrange("p (b n) -> p b n", b=NB)
                dve.wait_ge(S("a3_xs"), di + 1)
                for j in range(4):
                    o = j if di == 0 else 6 - j
                    src = xsp[:, :, o:o + LB]
                    if j == 0:
                        dve.tensor_scalar(v2(A3["t"][:, :]), src, P(w3 + "cw", 0, 1), None, ALU.mult)
                    else:
                        dve.scalar_tensor_tensor(out=v2(A3["t"][:, :]), in0=src, scalar=P(w3 + "cw", j, j + 1),
                                                 in1=v2(A3["t"][:, :]), op0=ALU.mult, op1=ALU.add)
                    dve.drain()
                dve.sem_inc(S("a3_conv"), 1)
                split_rows_dve(dve, A3["bc"], A3["tmp"], "a3_bc", "a3_split", di + 1)
                softplus_dve(dve, A3["t"][:, :], A3["a"][:, :], A3["delta"][:, :], A3["dx"][:, :], mask8[:, :],
                             f"a3{dn}_ln").then_inc(S("a3_delta"), 1)
                dve.drain()
                dve.tensor_tensor(A3["dx"][:, :], A3["delta"][:, :], A3["u"][:, :], ALU.mult)
                dve.drain()
                dve.drain()
                RD = chan(f"a3{dn}_drive", None)
                Y = chan(f"a3{dn}_sum", None)
                fl = (lambda z: z[:, 0:L]) if di == 0 else (lambda z: z[:, L - 1::-1])
                for k in range(DS + 1):
                    if k < DS:
                        ps, w = RD.get()
                        dve.wait_ge(RD.full, w)
                        if k >= 2:
                            dve.wait_ge(S(f"a3{dn}_scanned"), k - 1)
                        dve.tensor_tensor(RB[k % 2].rearrange("p (c n) -> p c n", c=2), ps[:, :, 0:CH],
                                          A3["dx"].rearrange("p (c n) -> p c n", c=2), ALU.mult).then_inc(RD.free, 1)
                    if k >= 1:
                        i = k - 1
                        dve.wait_ge(S(f"a3{dn}_decay"), i + 1)
                        dve.wait_ge(RD.free, i + 1)
                        if i >= 2:
                            dve.wait_ge(S(f"a3{dn}_read"), i - 1)
                        dve.tensor_tensor_scan(fl(RS[i % 2]), fl(RA[i % 2]), fl(RB[i % 2]), 0.0, ALU.mult,
                                               ALU.add).then_inc(S(f"a3{dn}_scanned"), 1)
                ps, w = Y.get()
                y = A3["y"][di]
                dve.wait_ge(Y.full, w)
                v = lambda z: z[:, :].rearrange("p (c n) -> p c n", c=2)
                dve.scalar_tensor_tensor(out=v(y), in0=v(A3["u"]), scalar=P(w3 + "Dp"), in1=ps[:, :, 0:CH],
                                         op0=ALU.mult, op1=ALU.add).then_inc(Y.free, 1)
                dve.drain()
                dve.tensor_tensor(y[:, :], y[:, :], A3["sz"][:, :], ALU.mult)
                dve.drain().then_inc(S("a3_y"), 1)
            dve.tensor_tensor(h[:, :, :], h[:, :, :], Xs, ALU.add)
            dve.drain()
            dve.tensor_tensor(h[:, :, :], h[:, :, :], bt(P("a3_fusb"), T), ALU.add)
            dve.drain()
            dve_residual(dve, "a3_out")


        def ffn3_pe(pe):
            A = chan("f3_turn", singles(0, 2))
            pe_turn(pe, A, x2tok, 128, "f3_normed")
            pe.wait_ge(S("f3_xT"), 1)
            pe_tokens(pe, chan("f3_rt", singles(2, 4)), [(F[0][0:D, :], P("f3_rt"))], 8)
            pe_turn(pe, A, W96, 96, "f3_w96")
            pe.wait_ge(S("f3_xsplit"), 1)
            pe.wait_ge(S("f3_wsplit"), 1)
            experts_pe(pe, "f3e", NE, UPX, None, selbn, "f3_w2", "f3_b2")

        def ffn3_act(act):
            act_norm(act, T, "f3_x")
            act_norm(act, T, "f3_n", ACT.Exp)
            A = chan("f3_turn", None)
            act_empty(act, A, F[0], 128, scale=P("f3_g"), bias=P("f3_b"), signal="f3_xT")
            act.wait_ge(S("f3_gap"), 1)
            act.activation(r8[2][:, :], r8[2][:, :], ACT.Exp).then_inc(S("f3_gapexp"), 1)
            act_table(act, ACT.Gelu)
            act_empty(act, A, F[1], 96, signal="f3_w96T")
            experts_act(act, "f3e", NE, ACT.Gelu, "f3_b1")

        def ffn3_dve(dve):
            dve_norm(dve, h[:, :, :], Xs, T, D, 1e-5, "f3_x")
            dve.drain()
            dve_norm(dve, Xs, xn[:, :, :], T, D, 1e-5, "f3_n")
            dve.drain()
            dve.tensor_copy(twice(x2tok), xn[:, :, :].unsqueeze(2).broadcast_to([P0, T, 2, D])).then_inc(S("f3_normed"), 1)
            dve.wait_ge(S("f3_xT"), 1)
            split_doubled_dve(dve, "f3_xsplit")
            Y = chan("f3_rt", None)
            for b in range(NB):
                ps, w = Y.get()
                dve.wait_ge(Y.full, w)
                dve.tensor_tensor(lg[:, tiles(b), 0:8], tok(ps, 8), bt(P("f3_rtb"), TB), ALU.add).then_inc(Y.free, 1)
            dve.drain()
            top2_dve(dve, lg[:, :, 0:8])
            dve.tensor_tensor(r8[2][:, :], r8[1][:, :], r8[0][:, :], ALU.subtract).then_inc(S("f3_gap"), 1)
            dve.wait_ge(S("f3_gapexp"), 1)
            dve.tensor_scalar(r8[5][:, :], r8[2][:, :], 1.0, None, ALU.add)
            dve.drain()
            dve.reciprocal(r8[3][:, :], r8[5][:, :])
            dve.drain()
            dve.tensor_tensor(r8[4][:, :], r8[2][:, :], r8[3][:, :], ALU.mult)
            dve.drain()
            spread_weights_dve(dve, "f3_w96")
            split_rows_dve(dve, F[1], F[2], "f3_w96T", "f3_wsplit")
            experts_dve(dve, "f3e", NE, False)

        block = ctx.enter_context(nc.Block())

        def part_over(e, at):
            e.drain().then_inc(arrive, 1)
            e.wait_ge(go, at)

        @block.tensor
        def _(pe):
            pe.wait_ge(first_in, 16)
            with pe.Fori(0, NIT) as it:
                conv_pe(pe, it)
                pe.wait_ge(weights_in, 16 * (WCH - 1))
                pe.wait_ge(consts_ready, 1)
                pe.wait_ge(selectors_ready, 1)
                scan0_pe(pe)
                sx_pe(pe)
                part_over(pe, it + 1)
            with pe.Fori(0, NIT) as it:
                ffn0_pe(pe)
                attn1_pe(pe)
                part_over(pe, it + (NIT + 1))
            with pe.Fori(0, NIT) as it:
                ffn1_pe(pe)
                attn2_pe(pe)
                ffn2_pe(pe)
                part_over(pe, it + (2 * NIT + 1))
            with pe.Fori(0, NIT) as it:
                scan3_pe(pe)
                ffn3_pe(pe)
                part_over(pe, it + (3 * NIT + 1))

        @block.scalar
        def _(act):
            act.wait_ge(first_in, 16)
            act.activation(nA0[:, :], P("a0_Alog"), ACT.Exp)
            act.activation(nA3[:, 0, :], P("a3f_Alog"), ACT.Exp)
            act.activation(nA3[:, 1, :], P("a3b_Alog"), ACT.Exp)
            act.drain().then_inc(S("A_exp"), 1)
            act.wait_ge(consts_ready, 1)
            with act.Fori(0, NIT) as it:
                conv_act(act)
                act.wait_ge(weights_in, 16 * (WCH - 1))
                scan0_act(act)
                sx_act(act)
                part_over(act, it + 1)
            with act.Fori(0, NIT) as it:
                ffn0_act(act)
                attn1_act(act)
                part_over(act, it + (NIT + 1))
            with act.Fori(0, NIT) as it:
                ffn1_act(act)
                attn2_act(act)
                ffn2_act(act)
                part_over(act, it + (2 * NIT + 1))
            with act.Fori(0, NIT) as it:
                scan3_act(act)
                ffn3_act(act)
                part_over(act, it + (3 * NIT + 1))

        @block.vector
        def _(dve):
            dve.memset(X[:, :, D:D + 1], 1.0)
            dve.memset(tbl[:, 0:1], 1.0)
            dve.memset(ones3[:, :], 1.0)
            dve.wait_ge(first_in, 16)
            dve.tensor_copy(identb[:, :], P("ident"))
            dve.tensor_copy(maskqk[:, :], P("mask_qk"))
            dve.tensor_copy(maskkq[:, :], P("mask_kq"))
            dve.wait_ge(S("A_exp"), 1)
            dve.tensor_scalar(nA0[:, :], nA0[:, :], -1.0, None, ALU.mult)
            dve.tensor_scalar(nA3[:, :, :], nA3[:, :, :], -1.0, None, ALU.mult)
            dve.drain().then_inc(consts_ready, 1)
            with dve.Fori(0, NIT) as it:
                conv_dve(dve)
                dve.wait_ge(weights_in, 16 * (WCH - 1))
                scan0_dve(dve)
                sx_dve(dve, it)
                part_over(dve, it + 1)
            with dve.Fori(0, NIT) as it:
                dve.tensor_copy(h[:, :, :], h_all[:, bass.ds(it * T, T), :])
                dve.drain()
                ffn0_dve(dve, it)
                attn1_dve(dve)
                dve.tensor_copy(h_all[:, bass.ds(it * T, T), :], h[:, :, :])
                part_over(dve, it + (NIT + 1))
            with dve.Fori(0, NIT) as it:
                dve.tensor_copy(h[:, :, :], h_all[:, bass.ds(it * T, T), :])
                dve.drain()
                ffn1_dve(dve)
                attn2_dve(dve)
                ffn2_dve(dve)
                dve.tensor_copy(h_all[:, bass.ds(it * T, T), :], h[:, :, :])
                part_over(dve, it + (2 * NIT + 1))
            with dve.Fori(0, NIT) as it:
                dve.tensor_copy(h[:, :, :], h_all[:, bass.ds(it * T, T), :])
                dve.drain()
                scan3_dve(dve)
                ffn3_dve(dve)
                dve.tensor_copy(h_all[:, bass.ds(it * T, T), :], h[:, :, :])
                dve.drain().then_inc(S("h_done"), 1)
                part_over(dve, it + (3 * NIT + 1))

        @block.gpsimd
        def _(pool):
            pool.wait_ge(selectors_in, 32)
            pool.tensor_copy(selrep[:, :], W2N[:, 0, 0:512])
            pool.tensor_copy(selbn[:, :], W2N[0:96, 1, :])
            pool.tensor_copy(selmoe[:, :], W2N[0:96, 0, 512:512 + KT1 * 128])
            pool.drain().then_inc(selectors_ready, 1)
            with pool.Fori(0, NIT) as it:
                scan0_pool(pool)
                part_over(pool, it + 1)
            w, r = W2N[:, 0, 0:ECOLS], W2N[:, 1, 0:ECOLS]
            lower = P("minus64", 1, 2)
            pool.wait_ge(weights_in, 16 * (WCH - 1))
            pool.wait_ge(ups_in, 16)
            pool.tensor_copy(EW[:, 0, :], w)
            pool.drain()
            pool.tensor_tensor(r, w, EW[:, 0, :], ALU.subtract)
            pool.drain()
            pool.tensor_copy(EW[:, 1, :], r)
            pool.drain()
            pool.tensor_scalar(r, EW[:, 0, :], lower, None, ALU.mult)
            pool.drain()
            pool.tensor_tensor(w, w, r, ALU.add)
            pool.drain()
            pool.tensor_copy(EW[:, 2, :], w)
            pool.drain()
            pool.tensor_scalar(r, EW[:, 2, :], lower, None, ALU.mult)
            pool.drain()
            pool.tensor_tensor(EW[:, 2, :], w, r, ALU.add)
            pool.drain().then_inc(ups_split, 1)
            with pool.Fori(0, NIT) as it:
                part_over(pool, it + (NIT + 1))
            with pool.Fori(0, NIT) as it:
                ffn2_pool(pool)
                part_over(pool, it + (2 * NIT + 1))
            with pool.Fori(0, NIT) as it:
                scan3_pool(pool)
                part_over(pool, it + (3 * NIT + 1))

        @block.sync
        def _(sp):
            conv_sp(sp, 0)
            first = OFF["a0_out"][1] + OFF["a0_out"][2]
            step = -(-(WCOLS - first) // (WCH - 1))
            sp.dma_start(WP[:, 0:first], pack[:, 0:first]).then_inc(first_in, 16)
            sp.dma_start(W2N[:, 0, 0:(4 + KT1) * 128], selectors[:, 4096:(36 + KT1) * 128]).then_inc(selectors_in, 16)
            sp.dma_start(W2N[:, 1, :], selectors[:, 0:4096]).then_inc(selectors_in, 16)
            for i in range(WCH - 1):
                a, b = first + i * step, min(WCOLS, first + (i + 1) * step)
                sp.dma_start(WP[:, a:b], pack[:, a:b]).then_inc(weights_in, 16)
            sp.wait_ge(selectors_ready, 1)
            sp.dma_start(W2N[:, 0, 0:ECOLS], ups[:, :]).then_inc(ups_in, 16)
            counted = pool_of_sems + [arrive]

            def iteration_end(engines):
                sp.wait_ge(arrive, engines)
                nums = sorted({s.num for s in counted})
                runs = []
                for n in nums:
                    if runs and runs[-1][1] == n:
                        runs[-1][1] = n + 1
                    else:
                        runs.append([n, n + 1])
                for a, b in runs:
                    sp.sem_clear(range(a, b))
                sp.drain().then_inc(go, 1)

            with sp.Fori(0, NIT - 1) as it:
                sp.wait_ge(S("conv_xT"), 1)
                conv_sp(sp, it + 1)
                iteration_end(4)
            iteration_end(4)
            with sp.Fori(0, NIT):
                attend_sp(sp, "f0", E0)
                iteration_end(4)
            sp.wait_ge(ups_split, 1)
            sp.dma_start(W2N[:, 0, :], w2s[0:128, :]).then_inc(w2_in, 16)
            sp.dma_start(W2N[0:127, 1, :], w2s[128:NODES, :]).then_inc(w2_in, 16)
            with sp.Fori(0, NIT):
                attend_sp(sp, "f1", 1)
                iteration_end(4)
            with sp.Fori(0, NIT) as it:
                sp.wait_ge(S("h_done"), 1)
                dst = out[bass.ds(it, 1), :, :]
                sp.dma_start(dst[:, 0:LB - P0, :].rearrange("b (j p) f -> p (b j) f", p=P0),
                             h_all[:, bass.ds(it * TB, TB - 1), :]).then_inc(out_done, 16)
                sp.dma_start(dst[:, LB - P0:L, :].rearrange("b p f -> p b f"),
                             h_all[0:L - (LB - P0), bass.ds(it * TB + TB - 1, 1), :]).then_inc(out_done, 16)
                iteration_end(4)
            sp.wait_ge(out_done, 2 * 16 * NIT)
            sp.wait_ge(w2_in, 32)


WCH = 4


def selector_bits():
    a = np.zeros((128, 36 + KT1, 128), np.float32)
    k = np.arange(128)
    for n in range(32):
        a[n:96:32, n, :] = 1
    for q in range(4):
        for r in range(4):
            a[32 * q + 8 * r + k // 16, 32 + r, k] = 1
    e = np.arange(KT1 * 128) // HID
    for j in range(3):
        a[32 * j:32 * j + 8, 36:, :] = (np.arange(8)[:, None] == e).reshape(8, KT1, 128)
    return a.reshape(128, -1)


def pack_weights(i):
    a = np.zeros((128, WCOLS), np.float32)

    def put(name, v):
        r, o, c = OFF[name]
        v = np.asarray(v)
        if v.ndim == 1:
            v = v[:, None]
        assert v.shape == (r, c), (name, v.shape, (r, c))
        a[0:r, o:o + c] = v

    def row(v, n=P0):
        return np.broadcast_to(np.asarray(v)[None, :], (n, len(v)))

    k = np.arange(128)
    put("ident", np.eye(128))
    m = np.where(np.arange(P0)[None, :] > np.arange(P0)[:, None], MASKED, 0.0)
    put("mask_qk", m)
    put("mask_kq", m.T)
    sums = np.zeros((128, 4, 32))
    for r in range(4):
        sums[k, r, 8 * r + k // 16] = 1
    put("sel_sum", sums.reshape(128, -1))
    put("split1", (np.arange(96) >= 32) * -1.0)
    put("split2", (np.arange(96) >= 64) * -1.0)
    put("tok_w", i["L0_tok_weight"].reshape(4, 128, 64).transpose(1, 0, 2).reshape(128, 256))
    put("tok_b", row(i["L0_tok_bias"][0]))
    put("a0_xp", i["L0_attn_x_proj"])
    for n, s in (("a0_dt", "dt_proj"), ("a0_B", "B_proj"), ("a0_C", "C_proj")):
        put(n, np.tile(i["L0_attn_" + s], (1, 8)))
    put("a0_dtb", np.tile(i["L0_attn_dt_proj_bias"], 8))
    put("a0_Alog", i["L0_attn_A_log"].reshape(16, 8, 16).transpose(1, 2, 0).reshape(128, 16))
    put("a0_D", i["L0_attn_D"])
    put("a0_out", i["L0_attn_out_proj"])

    hl = i["L0_ffn_hl_w"]
    put("f0_hl", hl.reshape(64, 64).T)
    put("f0_hlb_bc", row(i["L0_ffn_hl_b"].reshape(64)))
    wq = np.zeros((64, 4, 128), np.float32)
    wk = np.zeros((64, 128), np.float32)
    wv = np.zeros((64, 128), np.float32)
    gate = np.zeros((2, 128, 16), np.float32)
    fc1 = np.zeros((64, 64), np.float32)
    fc2 = np.zeros((64, 64), np.float32)
    for n in range(4):
        r = slice(16 * n, 16 * n + 16)
        s = slice(32 * n, 32 * n + 16)
        for d in (s, slice(32 * n + 16, 32 * n + 32)):
            for e in range(4):
                wq[r, e, d] = i["L0_ffn_wq"][n, e].T
            wk[r, d] = i["L0_ffn_wk"][n].T
        wv[r, s] = i["L0_ffn_wv"][n].T
        gate[n // 2, (n % 2) * 64:(n % 2) * 64 + 64, n * 4:n * 4 + 4] = i["L0_ffn_gate_w"][n].T
        fc1[r, r] = i["L0_ffn_fc1_w"].T
        fc2[r, r] = i["L0_ffn_fc2_w"].T
    put("f0_wq", wq.reshape(64, 512))
    put("f0_wk", wk)
    put("f0_wv", wv)
    one = (k % 32 == HD) * 1.0
    put("minus", -np.stack([k % 32 < 16, k % 32 >= 16, k >= 0], 1).astype(np.float32))
    put("ones_col", row(one))
    put("f0_gate", np.concatenate([gate[0], gate[1]], 1))
    put("f0_gateb", row(i["L0_ffn_gate_b"].reshape(16)))
    for n, s in (("f0_lng", "ln_g"), ("f0_lnb", "ln_b"), ("f0_fng", "fnorm_g"), ("f0_fnb", "fnorm_b"), ("f0_fc2b", "fc2_b")):
        put(n, row(np.tile(i["L0_ffn_" + s], 4)))
    put("f0_fc1", fc1)
    put("f0_fc1b", np.tile(i["L0_ffn_fc1_b"], 4))
    put("f0_fc2", fc2)
    put("f0_fg", i["L0_ffn_fgate_w"].T)

    put("a1_g1", i["L1_attn_ln1_g"])
    put("a1_b1", i["L1_attn_ln1_b"])
    put("a1_Wx", i["L1_attn_Wx"])
    put("a1_bx", i["L1_attn_bx"].reshape(2, 128).T)
    put("a1_bx_bc", row(i["L1_attn_bx"]))
    qk = np.zeros((2, 128, 64), np.float32)
    bv = np.zeros((128, 128), np.float32)
    for hd in range(8):
        r = slice(32 * (hd % 4), 32 * (hd % 4) + 32)
        qk[hd // 4, r, 4 * hd:4 * hd + 4] = i["L1_attn_Wq"]
        qk[hd // 4, r, 32 + 4 * hd:36 + 4 * hd] = i["L1_attn_Wk"]
        bv[r, r] = i["L1_attn_Wv"]
    put("a1_qk", np.concatenate([qk[0], qk[1]], 1))
    put("a1_blk", (np.arange(32)[:, None] // 4 == np.arange(256)[None, :] // 32) * 1.0)
    put("a1_Wv", bv)
    put("a1_Wo", i["L1_attn_Wo"].reshape(2, 128, 64).transpose(1, 0, 2).reshape(128, 128))
    put("a1_bo", row(i["L1_attn_bo"]))
    put("a1_g2", i["L1_attn_ln2_g"])
    put("a1_b2", i["L1_attn_ln2_b"])
    put("a1_W1", i["L1_attn_W1"])
    put("a1_W1b", i["L1_attn_b1"].reshape(2, 128).T)
    put("a1_W2", i["L1_attn_W2"].reshape(2, 128, 64).transpose(1, 0, 2).reshape(128, 128))
    put("a1_W2b", row(i["L1_attn_b2"]))

    put("f1_ln1", i["L1_ffn_ln1_w"])
    put("f1_ln2", np.tile(i["L1_ffn_ln2_w"], 2))
    q = np.zeros((64, 128), np.float32)
    kk = np.zeros((64, 128), np.float32)
    v = np.zeros((64, 128), np.float32)
    rq = np.zeros((64, 128), np.float32)
    rk = np.zeros((32, 128), np.float32)
    rot = np.zeros((16, 16), np.float32)
    for d in range(8):
        rot[d + 8, d] = -1
        rot[d, d + 8] = 1
    for n in range(4):
        s = slice(32 * n, 32 * n + 16)
        g = n // 2
        for d in (s, slice(32 * n + 16, 32 * n + 32)):
            q[:, d] = i["L1_ffn_wq"][16 * n:16 * n + 16].T
            kk[:, d] = i["L1_ffn_wk"][16 * g:16 * g + 16].T
            rq[16 * n:16 * n + 16, d] = rot
            rk[16 * g:16 * g + 16, d] = rot
        v[:, s] = i["L1_ffn_wv"][16 * g:16 * g + 16].T
    put("f1_wq", q)
    put("f1_wk", kk)
    put("f1_wv", v)
    put("f1_wq_r", i["L1_ffn_wq"])
    put("f1_wk_r", i["L1_ffn_wk"])
    put("rot_q", rq)
    put("rot_k", rk)
    inv = 1.0 / 10000.0 ** (np.arange(0, HD, 2, dtype=np.float32) / HD)
    fr = np.outer(np.arange(LB, dtype=np.float32), inv)
    emb = np.concatenate([fr, fr], -1)
    cs = np.zeros((2, 128, LB), np.float32)
    for n in range(8):
        cs[0, 16 * n:16 * n + 16] = np.cos(emb).T
        cs[1, 16 * n:16 * n + 16] = np.sin(emb).T
    put("cos", cs[0])
    put("sin", cs[1])
    put("f1_wo", i["L1_ffn_wo"].T)
    put("f1_rt", i["L1_ffn_router_w"].T)
    put("minus64", -np.stack([k < 64, k >= 64], 1).astype(np.float32))
    z = np.zeros((KT1 * 128, 64), np.float32)
    z[:NE * HID] = i["L1_ffn_w2"].transpose(0, 2, 1).reshape(NE * HID, 64)
    put("f1_w2", z.reshape(KT1, 128, 64).transpose(1, 0, 2).reshape(128, -1))
    put("rev", row(8.0 - np.arange(8)))

    put("a2_q", np.tile(i["L2_attn_Wq"].T, (1, 2)))
    put("a2_k", np.tile(i["L2_attn_Wk"].T, (1, 2)))
    z = np.zeros((64, 256), np.float32)
    z[:, :NODES] = i["L2_ffn_w1s"].T
    put("f2_w1", z)
    z = np.zeros(256, np.float32)
    z[:NODES] = i["L2_ffn_b1s"]
    put("f2_b1", row(z))
    z = np.zeros((256, 64), np.float32)
    z[:NODES] = i["L2_ffn_b2s"]
    put("f2_b2", z.reshape(2, 128, 64).transpose(1, 0, 2).reshape(128, 128))

    put("a3_g", i["L3_attn_norm_g"])
    put("a3_b", i["L3_attn_norm_b"])
    put("a3_fus", i["L3_attn_fusW"])
    put("a3_fusb", row(i["L3_attn_fusB"]))
    for d in "fb":
        w = lambda n: i[f"L3_attn_{n}_{d}"]
        put(f"a3{d}_in", w("inW"))
        put(f"a3{d}_cw", w("convW"))
        put(f"a3{d}_cb", w("convB"))
        put(f"a3{d}_dl", w("xW")[:, 0:4])
        put(f"a3{d}_bc", np.tile(w("xW")[:, 4:36], (1, 3)))
        put(f"a3{d}_dt", w("dtW"))
        put(f"a3{d}_dtb", w("dtB"))
        put(f"a3{d}_Alog", w("ALog"))
        put(f"a3{d}_Dp", w("Dp"))
        put(f"a3{d}_out", w("outW"))

    put("f3_g", np.tile(i["L3_ffn_gamma"], 2))
    put("f3_b", np.tile(i["L3_ffn_beta"], 2))
    put("f3_rt", i["L3_ffn_Wr"])
    put("f3_rtb", row(i["L3_ffn_br"]))
    put("f3_b1", i["L3_ffn_b1"].T)
    put("f3_w2", i["L3_ffn_W2"].transpose(1, 0, 2).reshape(128, -1))
    put("f3_b2", i["L3_ffn_b2"])
    return a


def pack_ups(i):
    a = np.zeros((64, ECOLS), np.float32)
    a[:, UP1:UP1 + NE * HID] = i["L1_ffn_w1"].reshape(NE * HID, 64).T
    a[:, UP3:UP3 + NE * HID] = i["L1_ffn_w3"].reshape(NE * HID, 64).T
    a[:, UPX:] = i["L3_ffn_W1"].transpose(1, 0, 2).reshape(64, -1)
    return np.concatenate([a, a], 0)


def kernel(**inputs):
    import concourse.bacc as _bacc
    from concourse.bass_utils import run_bass_kernel_spmd as _run

    i = {n: np.asarray(v) for n, v in inputs.items()}
    arrays = {
        "x_dram": np.ascontiguousarray(i["x"]),
        "pack_dram": pack_weights(i),
        "selectors_dram": selector_bits(),
        "w2s_dram": np.ascontiguousarray(i["L2_ffn_w2s"].reshape(NODES, 4096)),
        "ups_dram": pack_ups(i),
    }
    nc = _bacc.Bacc("TRN2", target_bir_lowering=False, num_devices=1)
    args = [nc.dram_tensor(n, a.shape, F32, kind="ExternalInput").ap() for n, a in arrays.items()]
    args.append(nc.dram_tensor("out_dram", (B, L, D), F32, kind="ExternalOutput").ap())
    audio_tower(nc, *args)
    r = _run(nc, [arrays], core_ids=[0])
    return r.results[0]["out_dram"]
```
